# Optimizing a Trainium2 kernel written in Bass

```python
import numpy as np
import jax
import jax.numpy as jnp

def _softmax(x, axis=-1):
    return jax.nn.softmax(x, axis=axis)

def _gelu(x):
    return jax.nn.gelu(x, approximate=True)

def _silu(x):
    return jax.nn.silu(x)

def _sigmoid(x):
    return jax.nn.sigmoid(x)

def _layernorm(x, axis=-1, eps=1e-05):
    m = jnp.mean(x, axis=axis, keepdims=True)
    v = jnp.var(x, axis=axis, keepdims=True)
    return (x - m) / jnp.sqrt(v + eps)

def _scatter_add(tgt, idx, src, axis=0):
    return tgt.at[idx].add(src)

def _segment_sum(src, seg, n):
    return jax.ops.segment_sum(src, seg, n)
kernel_name = 'mk_decoder_postln_d1_seqx_r2_d6e365'

def setup_inputs(seed: int=0):
    np.random.seed(seed)
    _w = jnp.asarray

    def _rec_inputs():
        import jax
        import jax.numpy as jnp
        _rk = jax.random.key(seed)
        x = -0.0003929 + 0.9999 * jax.random.normal(jax.random.fold_in(_rk, 1), (2, 2048, 512), jnp.float32)
        _lenS = 2048 - jax.random.randint(jax.random.fold_in(_rk, 7), (2,), 0, max(1, 2048 // 4) + 1, jnp.int32)
        _lenS2 = 77 - jax.random.randint(jax.random.fold_in(_rk, 8), (2,), 0, max(1, 77 // 4) + 1, jnp.int32)
        _ctx_1024P = jax.random.normal(jax.random.fold_in(_rk, 11), (2, 16, 512), jnp.float32)
        _ctx_1024c = jax.random.dirichlet(jax.random.fold_in(_rk, 511), 0.3 * jnp.ones((16,), jnp.float32), (2, 77))
        _ctx_1024t = jnp.einsum('bsk,bkd->bsd', _ctx_1024c, _ctx_1024P)
        _ctx_1024t = _ctx_1024t * jax.lax.rsqrt(jnp.mean(jnp.square(_ctx_1024t)) + 1e-12) * 0.953939
        ctx_1024 = 2.81802e-05 + 1.00001 * (_ctx_1024t + 0.3 * jax.random.normal(jax.random.fold_in(_rk, 611), (2, 77, 512), jnp.float32))
        return (x, ctx_1024)
    x, ctx_1024 = _rec_inputs()

    def _L0_attn_setup():
        import jax, jax.numpy as jnp
        import numpy as np
        MODEL_DIM = 512
        HEADS = 16
        HEAD_DIM = MODEL_DIM // HEADS
        B, T = (2, 1024)
        TB_LEN = 250
        key = jax.random.key(seed)
        ks = jax.random.split(key, 12)
        s = 0.02
        d = MODEL_DIM
        return {'x': jax.random.normal(ks[0], (B, T, d), dtype=jnp.float32), 'Wq': jax.random.normal(ks[1], (d, d), dtype=jnp.float32) * s, 'bq': jnp.zeros((d,), jnp.float32), 'Wk': jax.random.normal(ks[2], (d, d), dtype=jnp.float32) * s, 'bk': jnp.zeros((d,), jnp.float32), 'Wv': jax.random.normal(ks[3], (d, d), dtype=jnp.float32) * s, 'bv': jnp.zeros((d,), jnp.float32), 'Wo': jax.random.normal(ks[4], (d, d), dtype=jnp.float32) * s, 'bo': jnp.zeros((d,), jnp.float32), 'et_gate': jax.random.normal(ks[5], (1, 1, 1), dtype=jnp.float32), 'is_gate': jax.random.normal(ks[6], (1, 1, 1), dtype=jnp.float32), 'time_bias': jnp.linspace(-1.0, 1.0, TB_LEN, dtype=jnp.float32).reshape(1, 1, TB_LEN)}
    _L0_attn_all = _L0_attn_setup()
    _L0_attn_in = {k: v for k, v in _L0_attn_all.items() if k in ('Wq', 'bq', 'Wk', 'bk', 'Wv', 'bv', 'Wo', 'bo', 'et_gate', 'is_gate', 'time_bias')}
    del _L0_attn_all

    def _L0_xattn_setup():
        import jax, jax.numpy as jnp
        import numpy as np
        DIM = 512
        B, TQ, TK = (8, 1024, 1024)
        key = jax.random.key(seed)
        ks = jax.random.split(key, 8)
        s = 1.0 / np.sqrt(DIM)
        return {'texto': jax.random.normal(ks[0], (B, TQ, DIM), dtype=jnp.float32), 'imagen': jax.random.normal(ks[1], (B, TK, DIM), dtype=jnp.float32), 'Wq': jax.random.normal(ks[2], (DIM, DIM), dtype=jnp.float32) * s, 'bq': jnp.zeros((DIM,), dtype=jnp.float32), 'Wk': jax.random.normal(ks[3], (DIM, DIM), dtype=jnp.float32) * s, 'bk': jnp.zeros((DIM,), dtype=jnp.float32), 'Wv': jax.random.normal(ks[4], (DIM, DIM), dtype=jnp.float32) * s, 'bv': jnp.zeros((DIM,), dtype=jnp.float32)}
    _L0_xattn_all = _L0_xattn_setup()
    _L0_xattn_in = {k: v for k, v in _L0_xattn_all.items() if k in ('Wq', 'bq', 'Wk', 'bk', 'Wv', 'bv')}
    del _L0_xattn_all

    def _L0_ffn_setup():
        import jax, jax.numpy as jnp
        import numpy as np
        SL, BS, HS, FF, E, TOPK = (1024, 2, 512, 2048, 8, 2)
        key = jax.random.key(seed)
        ks = jax.random.split(key, 6)
        T = SL * BS
        x = jax.random.normal(ks[0], (SL, BS, HS), jnp.float32)
        scores = jax.random.uniform(ks[1], (T, E), jnp.float32)
        expert_weights = jax.random.uniform(ks[2], (T, TOPK), jnp.float32)
        expert_indices = jax.random.randint(ks[3], (T, TOPK), 0, E, jnp.int32)
        w1 = jax.random.normal(ks[4], (E, HS, FF), jnp.float32) * (1.0 / np.sqrt(HS))
        w2 = jax.random.normal(ks[5], (E, FF, HS), jnp.float32) * (1.0 / np.sqrt(FF))
        bias = jnp.zeros((HS,), jnp.float32)
        return dict(x=x, scores=scores, expert_weights=expert_weights, expert_indices=expert_indices, w1=w1, w2=w2, bias=bias)
    _L0_ffn_all = _L0_ffn_setup()
    _L0_ffn_in = {k: v for k, v in _L0_ffn_all.items() if k in ('scores', 'expert_weights', 'expert_indices', 'w1', 'w2', 'bias')}
    del _L0_ffn_all
    return {'x': x, 'ctx_1024': ctx_1024, 'L0_attn_Wq': _L0_attn_in['Wq'], 'L0_attn_bq': _L0_attn_in['bq'], 'L0_attn_Wk': _L0_attn_in['Wk'], 'L0_attn_bk': _L0_attn_in['bk'], 'L0_attn_Wv': _L0_attn_in['Wv'], 'L0_attn_bv': _L0_attn_in['bv'], 'L0_attn_Wo': _L0_attn_in['Wo'], 'L0_attn_bo': _L0_attn_in['bo'], 'L0_attn_et_gate': _L0_attn_in['et_gate'], 'L0_attn_is_gate': _L0_attn_in['is_gate'], 'L0_attn_time_bias': _L0_attn_in['time_bias'], 'L0_xattn_Wq': _L0_xattn_in['Wq'], 'L0_xattn_bq': _L0_xattn_in['bq'], 'L0_xattn_Wk': _L0_xattn_in['Wk'], 'L0_xattn_bk': _L0_xattn_in['bk'], 'L0_xattn_Wv': _L0_xattn_in['Wv'], 'L0_xattn_bv': _L0_xattn_in['bv'], 'L0_ffn_scores': _L0_ffn_in['scores'], 'L0_ffn_expert_weights': _L0_ffn_in['expert_weights'], 'L0_ffn_expert_indices': _L0_ffn_in['expert_indices'], 'L0_ffn_w1': _L0_ffn_in['w1'], 'L0_ffn_w2': _L0_ffn_in['w2'], 'L0_ffn_bias': _L0_ffn_in['bias']}

def reference(x, ctx_1024, L0_attn_Wq, L0_attn_bq, L0_attn_Wk, L0_attn_bk, L0_attn_Wv, L0_attn_bv, L0_attn_Wo, L0_attn_bo, L0_attn_et_gate, L0_attn_is_gate, L0_attn_time_bias, L0_xattn_Wq, L0_xattn_bq, L0_xattn_Wk, L0_xattn_bk, L0_xattn_Wv, L0_xattn_bv, L0_ffn_scores, L0_ffn_expert_weights, L0_ffn_expert_indices, L0_ffn_w1, L0_ffn_w2, L0_ffn_bias):
    import jax
    import jax.numpy as jnp

    def _L0_attn_ref(x, Wq, bq, Wk, bk, Wv, bv, Wo, bo, et_gate, is_gate, time_bias):
        import jax, jax.numpy as jnp
        import numpy as np
        MODEL_DIM = 512
        HEADS = 16
        HEAD_DIM = MODEL_DIM // HEADS
        B, T = (2, 1024)
        TB_LEN = 250
        Bb, Tt, D = x.shape
        H, hd = (HEADS, HEAD_DIM)
        Q = (x @ Wq.T + bq).reshape(Bb, Tt, H, hd).transpose(0, 2, 1, 3)
        K = (x @ Wk.T + bk).reshape(Bb, Tt, H, hd).transpose(0, 2, 1, 3)
        V = (x @ Wv.T + bv).reshape(Bb, Tt, H, hd).transpose(0, 2, 1, 3)
        scores = jnp.einsum('bhqd,bhkd->bhqk', Q, K) / jnp.sqrt(jnp.float32(hd))
        pos = jnp.arange(Tt)[None, :] - jnp.arange(Tt)[:, None]
        idx = jnp.clip(pos + TB_LEN // 2, 0, TB_LEN - 1)
        tp = time_bias[:, :, idx]
        tp = jnp.squeeze(tp, axis=1)[None, None]
        scores = scores + jax.nn.sigmoid(et_gate) * tp + is_gate
        attn = jax.nn.softmax(scores, axis=-1)
        context = jnp.matmul(attn, V)
        context = context.transpose(0, 2, 1, 3, 4).reshape(Bb, Tt, D)
        return context @ Wo.T + bo

    def _L0_xattn_ref(texto, imagen, Wq, bq, Wk, bk, Wv, bv):
        import jax, jax.numpy as jnp
        import numpy as np
        DIM = 512
        B, TQ, TK = (8, 1024, 1024)
        q = texto @ Wq + bq
        k = imagen @ Wk + bk
        v = imagen @ Wv + bv
        scale = 1.0 / jnp.sqrt(jnp.asarray(texto.shape[-1], dtype=q.dtype))
        scores = jnp.einsum('bqd,bkd->bqk', q, k) * scale
        attn = jax.nn.softmax(scores, axis=-1)
        return jnp.einsum('bqk,bkd->bqd', attn, v)

    def _L0_ffn_ref(x, scores, expert_weights, expert_indices, w1, w2, bias):
        import jax, jax.numpy as jnp
        import numpy as np
        SL, BS, HS, FF, E, TOPK = (1024, 2, 512, 2048, 8, 2)
        sl, bs, hs = x.shape
        n_exp = w1.shape[0]
        top_k = expert_indices.shape[-1]
        xf = x.reshape(-1, hs)
        flat_idx = expert_indices.reshape(-1)
        flat_w = expert_weights.reshape(-1)
        order = jnp.argsort(flat_idx)
        tok = order // top_k
        tokens_per_expert = jnp.bincount(flat_idx, length=n_exp).astype(jnp.int32)
        xs = xf[tok]
        h = jax.nn.gelu(jax.lax.ragged_dot(xs, w1, tokens_per_expert), approximate=False)
        ys = jax.lax.ragged_dot(h, w2, tokens_per_expert)
        ys = ys * flat_w[order][:, None]
        out = jnp.zeros_like(xf).at[tok].add(ys)
        return out.reshape(sl, bs, hs) + bias
    x = _layernorm(x + _L0_attn_ref(x, L0_attn_Wq, L0_attn_bq, L0_attn_Wk, L0_attn_bk, L0_attn_Wv, L0_attn_bv, L0_attn_Wo, L0_attn_bo, L0_attn_et_gate, L0_attn_is_gate, L0_attn_time_bias), axis=-1)
    x = _layernorm(x + _L0_xattn_ref(x, ctx_1024, L0_xattn_Wq, L0_xattn_bq, L0_xattn_Wk, L0_xattn_bk, L0_xattn_Wv, L0_xattn_bv), axis=-1)
    x = _layernorm(x + _L0_ffn_ref(x, L0_ffn_scores, L0_ffn_expert_weights, L0_ffn_expert_indices, L0_ffn_w1, L0_ffn_w2, L0_ffn_bias), axis=-1)
    return x

_drawn_inputs = setup_inputs


def setup_inputs(seed=0):
    import zlib

    import numpy as np

    out = dict(_drawn_inputs(seed))
    spreads = {'L0_attn_bq': (0.0, 0.8),
     'L0_attn_bk': (0.0, 2.0),
     'L0_attn_bv': (0.0, 0.358),
     'L0_attn_bo': (0.0, 0.1),
     'L0_xattn_bq': (0.0, 0.411),
     'L0_xattn_bk': (0.0, 2.0),
     'L0_xattn_bv': (0.0, 0.1),
     'L0_ffn_bias': (0.0, 0.1)}
    factors = {'L0_attn_Wq': 8.0, 'L0_attn_Wk': 8.0, 'L0_attn_Wv': 8.0, 'L0_attn_time_bias': 8.0}
    for name, (base, spread) in spreads.items():
        noise = np.random.default_rng([zlib.crc32(name.encode()), seed]).standard_normal(out[name].shape)
        drawn = base * np.exp(spread * noise) if base else spread * noise
        out[name] = jnp.asarray(drawn.astype(out[name].dtype))
    for name, factor in factors.items():
        out[name] = (out[name] * factor).astype(out[name].dtype)
    return out
```

```python
from contextlib import ExitStack

import concourse.bass as bass
from concourse import mybir

F32 = mybir.dt.float32
F32R = mybir.dt.float32r
I32 = mybir.dt.int32
ALU = mybir.AluOpType
ACT = mybir.ActivationFunctionType
AX = mybir.AxisListType

P = 128
B, T, D = 2, 2048, 512
H = 16
HD = D // H
NROW = B * T
KD = D // P
NB = T // P
NH = B * H
TB_LEN = 250
TB_MID = TB_LEN // 2
EPS = 1e-5
QSCALE = 1.0 / float(HD) ** 0.5
XSCALE = 1.0 / float(D) ** 0.5
LC = 77
NE, FF = 8, 2048
FC = FF // P
NTOK = 2048
TOPK = 2
NCOL = NTOK // P * TOPK
NTILE = (NTOK * TOPK) // P + NE - 1

NSTEP = NB - 2
ROW_STEP = 3 * HD
ROW_SHIFT = ROW_STEP + 2 * NSTEP
ROWS = ROW_SHIFT + 2
BAND = 3 * P


G = 4
GT = G * P
NG = NROW // GT


class Mem:
    pass


def bcast_rows(ap, n=P):
    return ap.partition_broadcast(n)


def stage_setup(nc, d, m):
    with ExitStack() as c:
        def sb(name, shape, dt=F32):
            return c.enter_context(nc.sbuf_tensor(name, shape, dt))

        def sem(name):
            return c.enter_context(nc.semaphore(name))

        weights = [("wq", d["L0_attn_Wq"]), ("wk", d["L0_attn_Wk"]), ("wv", d["L0_attn_Wv"]), ("wo", d["L0_attn_Wo"]),
                   ("xq", d["L0_xattn_Wq"])]
        raw = [m.v[:, i * KD:(i + 1) * KD, :] for i in range(2)]
        xqT, xk_w, xv_w = (m.v[:, i * KD:(i + 1) * KD, :] for i in (2, 3, 4))
        cx = sb("cx", [LC, B, D])
        cxT = sb("cxT", [P, B, KD, LC])
        kxT = sb("kxT", [P, B, KD, LC])
        xbk = sb("xbk", [P, KD])
        xbq = sb("xbq", [P, KD])
        xbv = sb("xbv", [P, D])
        tb0 = sb("tb0", [P, 1])
        tbl = sb("tbl", [P, 1])
        gates = sb("gates", [P, 2])
        eneg = sb("eneg", [P, 1])
        epl = sb("epl", [P, 1])
        sig = sb("sig", [P, 1])
        dstep = sb("dstep", [P, 1])
        dfar = sb("dfar", [P, 1])
        c0a = sb("c0a", [P, 1])
        trow = sb("trow", [1, TB_LEN])
        ext = sb("ext", [1, 512])
        hank = sb("hank", [P, BAND])
        anti = sb("anti", [P, P])
        ei = sb("ei", [P, NCOL], I32)
        ef = sb("ef", [P, NCOL])
        oh = sb("oh", [P, NE, NCOL])
        tri = sb("tri", [P, P])
        tot = sb("tot", [P, NE, NCOL])
        sc = [sb(f"sc{i}", [P, NE, NCOL]) for i in range(5)]
        w1 = sb("w_1", [P, NE, NCOL])
        w2 = sb("w_2", [P, NE, NCOL])
        w3 = sb("w_3", [P, NE, NCOL])
        w4 = sb("w_4", [P, NE, NCOL])
        posf = sb("posf", [P, NCOL])
        cntf = sb("cntf", [P, NE])
        cnti = sb("cnti", [P, NE], I32)
        cntj = sb("cntj", [P, NE], I32)
        pad = sb("pad", [P, NE])
        ps1 = sb("ps1", [P, NE])
        ps2 = sb("ps2", [P, NE])
        ps3 = sb("ps3", [P, NE])
        base = sb("base", [P, NE])
        tio = sb("tio", [1, NTILE])
        tacc = [sb(f"tacc{i}", [1, NTILE]) for i in range(2)]
        toki = sb("toki", [P, NCOL], I32)
        zi = sb("zi", [P, NTILE], I32)

        pt = [c.enter_context(nc.psum_tensor(f"pt{i}", [P, 512], F32)) for i in range(4)]
        pr = c.enter_context(nc.psum_tensor("pr", [P, 512], F32))
        pq = c.enter_context(nc.psum_tensor("pq", [P, 512], F32))

        raw_in = [sem(f"raw_in{i}") for i in range(2)]
        small_in = sem("small_in")
        xw_in = sem("xw_in")
        turned = sem("turned")
        hi_done = sem("hi_done")
        lo_done = sem("lo_done")
        const_done = sem("const_done")
        v = sem("v_chain")
        eneg_done = sem("eneg_done")
        ext_out = sem("ext_out")
        tab_in = sem("tab_in")
        perm_zero = sem("perm_zero")
        perm_out = sem("perm_out")
        perm_in = sem("perm_in")
        rank_done = sem("rank_done")
        xt = sem("xt")
        tab_turned = sem("tab_turned")
        xe = sem("xe")
        block = c.enter_context(nc.Block())

        V_EXT, V_OH, V_POS = 9, 15, 33
        wT = {"wq": m.wqT, "wk": m.wkT, "wv": m.wvT, "wo": m.woT}

        @block.sync
        def _(sp):
            for n in range(2):
                sp.dma_start(raw[n], weights[n][1].rearrange("(o p) i -> p o i", p=P)).then_inc(raw_in[n], 16)
            with nc.allow_non_contiguous_dma("small vectors"):
                sp.dma_start(m.bq[:], d["L0_attn_bq"].rearrange("(m p) -> p m", p=P)).then_inc(small_in, 16)
                sp.dma_start(m.bk[:], d["L0_attn_bk"].rearrange("(m p) -> p m", p=P)).then_inc(small_in, 16)
                sp.dma_start(xbk[:], d["L0_xattn_bk"].rearrange("(m p) -> p m", p=P)).then_inc(small_in, 16)
                sp.dma_start(xbq[:], d["L0_xattn_bq"].rearrange("(m p) -> p m", p=P)).then_inc(small_in, 16)
                tb = d["L0_attn_time_bias"][0, 0]
                sp.dma_start(tb0[:], bcast_rows(tb[0:1])).then_inc(small_in, 16)
                sp.dma_start(tbl[:], bcast_rows(tb[TB_LEN - 1:TB_LEN])).then_inc(small_in, 16)
                sp.dma_start(gates[:, 0:1], bcast_rows(d["L0_attn_et_gate"][0, 0])).then_inc(small_in, 16)
                sp.dma_start(gates[:, 1:2], bcast_rows(d["L0_attn_is_gate"][0, 0])).then_inc(small_in, 16)
                sp.dma_start(ei[:].rearrange("p (c j) -> p c j", j=TOPK),
                             d["L0_ffn_expert_indices"].rearrange("(c p) j -> p c j", p=P)).then_inc(small_in, 16)
                sp.dma_start(m.tokw[:].rearrange("p (c j) -> p c j", j=TOPK),
                             d["L0_ffn_expert_weights"].rearrange("(c p) j -> p c j", p=P)).then_inc(small_in, 16)
            sp.dma_start(trow[:], d["L0_attn_time_bias"][0]).then_inc(small_in, 16)
            sp.dma_start(m.bv[:], bcast_rows(d["L0_attn_bv"])).then_inc(small_in, 16)
            sp.dma_start(xbv[:], bcast_rows(d["L0_xattn_bv"])).then_inc(small_in, 16)
            sp.dma_start(cx[:], d["ctx_1024"].rearrange("b t c -> t b c")).then_inc(xw_in, 16)
            sp.dma_start(xk_w, d["L0_xattn_Wk"].rearrange("(k p) o -> p k o", p=P)).then_inc(xw_in, 16)
            sp.dma_start(xv_w, d["L0_xattn_Wv"].rearrange("(k p) o -> p k o", p=P)).then_inc(xw_in, 16)
            for n in range(2, len(weights)):
                sp.wait_ge(turned, KD * (n - 1))
                sp.dma_start(raw[n % 2], weights[n][1].rearrange("(o p) i -> p o i", p=P)).then_inc(raw_in[n % 2], 16)
            sp.wait_ge(v, V_EXT)
            sp.dma_start(m.ext_d, ext[:]).then_inc(ext_out, 16)
            sp.wait_ge(ext_out, 16)
            sp.dma_start(hank[:], bass.AP(m.ext_t, 0, [[1, P], [1, BAND]])).then_inc(tab_in, 16)
            sp.wait_ge(perm_out, 16 * NCOL)
            with nc.allow_non_contiguous_dma("token list"):
                sp.dma_start(m.perm[:], m.perm_d.rearrange("(t p) o -> p (t o)", p=P)).then_inc(perm_in, 16)
            sp.wait_ge(perm_in, 16)
            sp.wait_ge(tab_in, 16)

        @block.gpsimd
        def _(pool):
            pool.memset(m.ident[:], 0.0).then_inc(const_done, 1)
            pool.memset(tri[:], 1.0).then_inc(const_done, 1)
            pool.memset(anti[:], 0.0).then_inc(const_done, 1)
            pool.wait_ge(const_done, 3)
            pool.affine_select(out=anti[:], in_=anti[:], compare_op=ALU.not_equal, fill=1.0, base=1 - P,
                               pattern=[[1, P]], channel_multiplier=1).then_inc(const_done, 1)
            pool.affine_select(out=m.ident[:], in_=m.ident[:], compare_op=ALU.not_equal, fill=1.0, base=0,
                               pattern=[[-1, P]], channel_multiplier=1).then_inc(const_done, 1)
            pool.affine_select(out=tri[:], in_=tri[:], compare_op=ALU.is_gt, fill=0.0, base=0,
                               pattern=[[1, P]], channel_multiplier=-1).then_inc(const_done, 1)
            pool.iota(toki[:].rearrange("p (c j) -> p c j", j=TOPK), [[P, NCOL // TOPK], [0, TOPK]], base=0,
                      channel_multiplier=1).then_inc(const_done, 1)
            pool.iota(tio[:], [[P, NTILE]], base=0, channel_multiplier=0,
                      allow_small_or_imprecise_dtypes=True).then_inc(const_done, 1)
            pool.memset(zi[:], 0).then_inc(const_done, 1)
            pool.wait_ge(const_done, 9)
            pool.dma_start(m.perm_d.rearrange("(p t) o -> p (t o)", p=P), zi[:]).then_inc(perm_zero, 16)
            pool.wait_ge(perm_zero, 16)
            pool.wait_ge(v, V_POS)
            for col in range(NCOL):
                pool.indirect_dma_start(m.perm_d, bass.IndirectOffsetOnAxis(m.pos[:, col:col + 1], 0),
                                        toki[:, col:col + 1], None).then_inc(perm_out, 16)

        @block.scalar
        def _(act):
            act.wait_ge(small_in, 16 * 13)
            act.activation(eneg[:], gates[:, 0:1], ACT.Exp, scale=-1.0).then_inc(eneg_done, 1)
            n = 0
            for name, _ in weights[:4]:
                for k in range(KD):
                    act.wait_ge(turned, n + 1)
                    act.copy(wT[name][0][:, k, :], pt[n % 4][:]).then_inc(hi_done, 1)
                    n += 1
            for k in range(KD):
                act.wait_ge(turned, n + 1)
                act.copy(xqT[:, k, :], pt[n % 4][:]).then_inc(hi_done, 1)
                n += 1
            for b in range(B):
                act.wait_ge(xt, b + 1)
                act.copy(cxT[:, b], pt[b][:, 0:KD * LC].rearrange("p (k t) -> p k t", t=LC)).then_inc(xe, 1)
            for b in range(B):
                act.wait_ge(xt, 2 + b + 1)
                for k in range(KD):
                    act.activation(kxT[:, b, k, :], pt[2 + b][:, k * LC:(k + 1) * LC], ACT.Identity,
                                   bias=xbk[:, k:k + 1]).then_inc(xe, 1)
            for b in range(B):
                act.wait_ge(xt, 4 + b + 1)
                act.mul(m.g[:, b], pt[b][:, 0:KD * LC].rearrange("p (k t) -> p k t", t=LC), XSCALE).then_inc(xe, 1)
            act.wait_ge(xt, 7)
            act.mul(m.g0[:], pr[0:1, 0:B * LC].rearrange("p (b t) -> p b t", b=B), XSCALE).then_inc(xe, 1)

        @block.vector
        def _(dve):
            dve.memset(m.ones[:], 1.0).then_inc(v, 1)
            dve.memset(ext[:], 0.0).then_inc(v, 1)
            dve.memset(tacc[0][:], 0.0).then_inc(v, 1)
            dve.wait_ge(small_in, 16 * 13)
            dve.wait_ge(eneg_done, 1)
            dve.tensor_scalar(epl[:], eneg[:], 1.0, None, ALU.add).then_inc(v, 1)
            dve.wait_ge(v, 4)
            dve.reciprocal(sig[:], epl[:]).then_inc(v, 1)
            dve.wait_ge(v, 5)
            dve.tensor_scalar(trow[:], trow[:], tb0[0:1, :], sig[0:1, :], ALU.subtract, ALU.mult).then_inc(v, 1)
            dve.wait_ge(v, 6)
            first = 2 * P - 1 - TB_MID
            dve.tensor_copy(ext[:, first:first + TB_LEN], trow[:]).then_inc(v, 1)
            dve.wait_ge(v, 7)
            dve.tensor_scalar(ext[:, first + TB_LEN:512], ext[:, first + TB_LEN:512],
                              trow[:, TB_LEN - 1:TB_LEN], None, ALU.add).then_inc(v, 2)
            dve.tensor_tensor(dstep[:], tbl[:], tb0[:], ALU.subtract).then_inc(v, 1)
            dve.tensor_scalar(m.c0[:], tb0[:], sig[:, 0:1], gates[:, 1:2], ALU.mult, ALU.add)
            dve.wait_ge(v, 10)
            dve.tensor_tensor(dfar[:], dstep[:], sig[:], ALU.mult).then_inc(v, 1)
            dve.wait_ge(v, 11)
            dve.tensor_copy(m.dhi[:], dfar[:]).then_inc(v, 1)
            dve.wait_ge(v, 12)
            dve.tensor_tensor(m.dlo[:], dfar[:], m.dhi[:].bitcast(F32), ALU.subtract).then_inc(v, 1)
            dve.tensor_copy(ef[:], ei[:]).then_inc(v, 1)
            dve.wait_ge(v, 14)
            for e in range(NE):
                ins = dve.tensor_scalar(oh[:, e, :], ef[:], float(e), None, ALU.is_equal)
            ins.then_inc(v, 1)
            n = 0
            for name, _ in weights[:4]:
                for k in range(KD):
                    dve.wait_ge(hi_done, n + 1)
                    dve.tensor_tensor(wT[name][1][:, k, :], pt[n % 4][:], wT[name][0][:, k, :].bitcast(F32),
                                      ALU.subtract).then_inc(lo_done, 1)
                    n += 1
            dve.wait_ge(rank_done, 2)
            dve.tensor_copy(tot[:], pq[:, 0:NE * NCOL].rearrange("p (e c) -> p e c", e=NE)).then_inc(v, 1)
            dve.wait_ge(v, 16)
            src, step = tot, 1
            for i in range(5):
                dve.tensor_copy(sc[i][:, :, 0:step], src[:, :, 0:step])
                dve.tensor_tensor(sc[i][:, :, step:], src[:, :, step:], src[:, :, 0:NCOL - step], ALU.add)\
                    .then_inc(v, 1)
                dve.wait_ge(v, 17 + i)
                src, step = sc[i], 2 * step
            dve.tensor_scalar(cntf[:], src[:, :, NCOL - 1], float(P - 1), None, ALU.add).then_inc(v, 1)
            dve.wait_ge(v, 22)
            dve.tensor_copy(cnti[:], cntf[:]).then_inc(v, 1)
            dve.wait_ge(v, 23)
            dve.tensor_scalar(cntj[:], cnti[:], 7, 7, ALU.arith_shift_right, ALU.arith_shift_left).then_inc(v, 1)
            dve.wait_ge(v, 24)
            dve.tensor_scalar(pad[:], cntj[:], float(P), None, ALU.max).then_inc(v, 1)
            dve.wait_ge(v, 25)
            src, step = pad, 1
            for i, dst in enumerate((ps1, ps2, ps3)):
                dve.tensor_copy(dst[:, 0:step], src[:, 0:step])
                dve.tensor_tensor(dst[:, step:], src[:, step:], src[:, 0:NE - step], ALU.add).then_inc(v, 1)
                dve.wait_ge(v, 26 + i)
                src, step = dst, 2 * step
            dve.tensor_tensor(w1[:], sc[4][:], tot[:], ALU.subtract)
            dve.tensor_tensor(base[:], ps3[:], pad[:], ALU.subtract).then_inc(v, 1)
            dve.wait_ge(v, 29)
            dve.tensor_tensor(w2[:], w1[:], base[:].unsqueeze(2).broadcast_to([P, NE, NCOL]), ALU.add).then_inc(v, 1)
            dve.wait_ge(v, 30)
            dve.tensor_tensor(w3[:], pr[:, 0:NE * NCOL].rearrange("p (e c) -> p e c", e=NE), w2[:], ALU.add)\
                .then_inc(v, 1)
            dve.wait_ge(v, 31)
            dve.tensor_tensor(w4[:], w3[:], oh[:], ALU.mult).then_inc(v, 1)
            dve.wait_ge(v, 32)
            dve.tensor_reduce(posf[:], w4[:].rearrange("p e c -> p c e"), AX.X, ALU.add)
            dve.drain()
            dve.tensor_copy(m.pos[:], posf[:]).then_inc(v, 1)
            dve.wait_ge(const_done, 9)
            for e in range(1, NE):
                dve.scalar_tensor_tensor(out=tacc[e % 2][:], in0=tio[:], scalar=base[0:1, e:e + 1],
                                         in1=tacc[(e + 1) % 2][:], op0=ALU.is_ge, op1=ALU.add)
                dve.drain()
            dve.tensor_copy(m.texp[:], tacc[1][:])
            dve.tensor_scalar(m.efirst[:], base[0:1, :], 1.0 / P, None, ALU.mult).then_inc(v, 1)
            dve.wait_ge(v, 34)
            dve.tensor_scalar(m.tslot[:], m.texp[:], 1, None, ALU.bitwise_and).then_inc(v, 1)
            for b in range(B):
                dve.wait_ge(xt, 7 + b + 1)
                dve.tensor_tensor(m.vx[:, b, :], pt[2 + b][0:LC, :], xbv[0:LC, :], ALU.add).then_inc(v, 1)
            dve.tensor_copy(m.ident_r[:], m.ident[:])
            dve.tensor_scalar(m.bqs[:], m.bq[:], QSCALE, None, ALU.mult)
            dve.wait_ge(tab_turned, 1)
            dve.tensor_copy(m.t1[:], pq[:, 0:BAND]).then_inc(v, 1)
            dve.wait_ge(tab_turned, 2)
            dve.tensor_copy(m.t2hi[:], pt[0][:, 0:BAND]).then_inc(v, 1)
            dve.wait_ge(v, 39)
            dve.tensor_tensor(m.t2lo[:], pt[0][:, 0:BAND], m.t2hi[:].bitcast(F32), ALU.subtract)

        @block.tensor
        def _(pe):
            pe.wait_ge(const_done, 9)
            pe.wait_ge(v, 1)
            n = 0
            for w in range(5):
                pe.wait_ge(raw_in[w % 2], 16 * (w // 2 + 1))
                for k in range(KD):
                    if n >= 4:
                        pe.wait_ge(lo_done if n - 4 < 16 else hi_done, n - 3)
                    for o in range(KD):
                        ins = pe.transpose(pt[n % 4][:, o * P:(o + 1) * P], raw[w % 2][:, o, k * P:(k + 1) * P],
                                           m.ident[:])
                    ins.then_inc(turned, 1)
                    n += 1
            pe.wait_ge(v, V_OH)
            ohf = oh[:].rearrange("p e c -> p (e c)")
            pe.matmul(pr[:, 0:NE * NCOL], tri[:], ohf, start=True, stop=True).then_inc(rank_done, 1)
            pe.matmul(pq[:, 0:NE * NCOL], m.ones[:, 0:P], ohf, start=True, stop=True).then_inc(rank_done, 1)
            pe.wait_ge(xw_in, 48)
            pe.wait_ge(hi_done, 20)
            for b in range(B):
                for k in range(KD):
                    ins = pe.transpose(pt[b][:, k * LC:(k + 1) * LC], cx[:, b, k * P:(k + 1) * P],
                                       m.ident[0:LC, 0:LC])
                ins.then_inc(xt, 1)
            for b in range(B):
                pe.wait_ge(xe, b + 1)
                for o in range(KD):
                    for k in range(KD):
                        ins = pe.matmul(pt[2 + b][:, o * LC:(o + 1) * LC], xk_w[:, k, o * P:(o + 1) * P],
                                        cxT[:, b, k, :], start=(k == 0), stop=(k == KD - 1))
                ins.then_inc(xt, 1)
            for b in range(B):
                pe.wait_ge(xe, 2 + KD * (b + 1))
                for i in range(KD):
                    for o in range(KD):
                        ins = pe.matmul(pt[b][:, i * LC:(i + 1) * LC], xqT[:, o, i * P:(i + 1) * P],
                                        kxT[:, b, o, :], start=(o == 0), stop=(o == KD - 1))
                ins.then_inc(xt, 1)
            pe.wait_ge(v, V_POS)
            for b in range(B):
                for o in range(KD):
                    ins = pe.matmul(pr[0:1, b * LC:(b + 1) * LC], xbq[:, o:o + 1], kxT[:, b, o, :],
                                    start=(o == 0), stop=(o == KD - 1))
            ins.then_inc(xt, 1)
            for b in range(B):
                for k in range(KD):
                    ins = pe.matmul(pt[2 + b][0:LC, :], cxT[:, b, k, :], xv_w[:, k, :],
                                    start=(k == 0), stop=(k == KD - 1))
                ins.then_inc(xt, 1)
            pe.wait_ge(tab_in, 16)
            pe.matmul(pq[:, 0:BAND], anti[:], hank[:], start=True, stop=True).then_inc(tab_turned, 1)
            pe.wait_ge(v, 38)
            pe.wait_ge(xe, 2 + KD * B + 2)
            for a in range(BAND // P):
                ins = pe.transpose(pt[0][:, a * P:(a + 1) * P], m.t1[:, BAND - (a + 1) * P:BAND - a * P], m.ident[:])
            ins.then_inc(tab_turned, 1)


def stage_project(nc, d, m):
    xr = d["x"].rearrange("b (n t p) c -> (b n) p t c", t=G, p=P)
    with ExitStack() as c:
        def sb(name, shape, dt=F32):
            return c.enter_context(nc.sbuf_tensor(name, shape, dt))

        def sem(name):
            return c.enter_context(nc.semaphore(name))

        xg = [sb(f"xg{i}", [P, G, D]) for i in range(2)]
        xh = [sb(f"xh{i}", [P, KD, GT], F32R) for i in range(2)]
        xl = [sb(f"xl{i}", [P, KD, GT], F32R) for i in range(2)]
        qf = [sb(f"qf{i}", [P, GT]) for i in range(2)]
        qh = [sb(f"qh{i}", [P, GT], F32R) for i in range(2)]
        ql = [sb(f"ql{i}", [P, GT], F32R) for i in range(2)]
        pt = [c.enter_context(nc.psum_tensor(f"ptp{i}", [P, GT], F32)) for i in range(KD)]
        pm = [c.enter_context(nc.psum_tensor(f"pmp{i}", [P, GT], F32)) for i in range(4)]

        x_in = [sem(f"x_in{i}") for i in range(2)]
        x_turned = sem("x_turned")
        xh_done = sem("xh_done")
        xl_done = sem("xl_done")
        x_read = sem("x_read")
        mm_done = sem("mm_done")
        qf_done = sem("qf_done")
        qh_done = sem("qh_done")
        ql_done = sem("ql_done")
        v_done = sem("v_done")
        part_out = [sem(f"part_out{i}") for i in range(2)]
        block = c.enter_context(nc.Block())
        NQK = 2 * KD
        NMM = NQK + G
        LAST = NG - 2

        @block.sync
        def _(sp):
            for j in range(2):
                sp.sem_inc(part_out[j], 32)
                sp.dma_start(xg[j][:], xr[j]).then_inc(x_in[j], 16)

            def group(n, par, more):
                if more:
                    sp.wait_ge(x_turned, KD * (n + 1))
                    sp.dma_start(xg[par][:], xr[n + 2]).then_inc(x_in[par], 16)
                for j in range(NQK):
                    sp.wait_ge(ql_done, NQK * n + j + 1 + 2)
                    dst = (m.q_d, m.k_d)[j // KD]
                    rows = slice((j % KD) * P, (j % KD + 1) * P)
                    sp.dma_start(dst[0, n, rows, :], qh[j % 2][:].bitcast(F32)).then_inc(part_out[j % 2], 16)
                    sp.dma_start(dst[1, n, rows, :], ql[j % 2][:].bitcast(F32)).then_inc(part_out[j % 2], 16)

            with sp.Fori(0, LAST // 2) as i:
                for par in range(2):
                    group(2 * i + par, par, True)
            for n in range(LAST, NG):
                group(n, n % 2, False)
            for j in range(2):
                sp.wait_ge(part_out[j], 32 * (NQK // 2 * NG + 1))

        @block.scalar
        def _(act):
            def turn(n, par):
                act.wait_ge(x_read, n + 1)
                for k in range(KD):
                    act.wait_ge(x_turned, KD * n + k + 1)
                    act.copy(xh[par][:, k, :], pt[k][:]).then_inc(xh_done, 1)

            def scale(n):
                for j in range(NQK):
                    act.wait_ge(mm_done, (NMM - 1) * n + j + 1)
                    act.wait_ge(ql_done, NQK * n + j + 1)
                    bias = (m.bqs if j < KD else m.bk)[:, j % KD:j % KD + 1]
                    act.activation(qf[j % 2][:], pm[j % 4][:], ACT.Identity, bias=bias,
                                   scale=QSCALE if j < KD else 1.0).then_inc(qf_done, 1)

            turn(0, 0)
            with act.Fori(0, LAST // 2) as i:
                for par in range(2):
                    turn(2 * i + par + 1, 1 - par)
                    scale(2 * i + par)
            turn(NG - 1, 1)
            scale(NG - 2)
            scale(NG - 1)

        @block.vector
        def _(dve):
            dve.sem_inc(ql_done, 2)
            dve.sem_inc(v_done, G)

            def turn(n, par):
                for k in range(KD):
                    dve.wait_ge(xh_done, KD * n + k + 1)
                    dve.tensor_tensor(xl[par][:, k, :], pt[k][:], xh[par][:, k, :].bitcast(F32),
                                      ALU.subtract).then_inc(xl_done, 1)

            def parts(n):
                for j in range(NQK):
                    dve.wait_ge(qf_done, NQK * n + j + 1)
                    dve.wait_ge(part_out[j % 2], 32 * (NQK // 2 * n + j // 2 + 1))
                    dve.tensor_copy(qh[j % 2][:], qf[j % 2][:]).then_inc(qh_done, 1)
                    dve.wait_ge(qh_done, NQK * n + j + 1)
                    dve.tensor_tensor(ql[j % 2][:], qf[j % 2][:], qh[j % 2][:].bitcast(F32),
                                      ALU.subtract).then_inc(ql_done, 1)
                for j in range(G):
                    if j < G - 1:
                        dve.wait_ge(mm_done, (NMM - 1) * n + NQK + j + 1)
                    else:
                        dve.wait_ge(x_read, n + 1 + 2)
                    dve.tensor_tensor(m.v[:, G * n + j, :], pm[j % 4][:], m.bv[:], ALU.add).then_inc(v_done, 1)

            turn(0, 0)
            with dve.Fori(0, LAST // 2) as i:
                for par in range(2):
                    turn(2 * i + par + 1, 1 - par)
                    parts(2 * i + par)
            turn(NG - 1, 1)
            parts(NG - 2)
            parts(NG - 1)

        @block.tensor
        def _(pe):
            pe.sem_inc(x_read, 2)

            def turn(n, par, uses):
                pe.wait_ge(x_in[par], 16 * uses)
                for k in range(KD):
                    if not isinstance(n, int) or n > 0:
                        pe.wait_ge(xl_done, KD * (n - 1) + k + 1)
                    for t in range(G):
                        ins = pe.transpose(pt[k][:, t * P:(t + 1) * P], xg[par][:, t, k * P:(k + 1) * P], m.ident[:])
                    ins.then_inc(x_turned, 1)

            def products(n, par):
                pe.wait_ge(xl_done, KD * (n + 1))
                for j in range(NMM):
                    if j < 4:
                        pe.wait_ge(v_done, G * n + j + 1)
                    else:
                        pe.wait_ge(qf_done, NQK * n + j - 4 + 1)
                    if j < NQK:
                        w, o = (m.wqT, m.wkT)[j // KD], j % KD
                        terms = [(w[a][:, k, o * P:(o + 1) * P], (xh, xl)[b][par][:, k, :])
                                 for a, b in ((0, 0), (0, 1), (1, 0)) for k in range(KD)]
                    else:
                        t = j - NQK
                        terms = [((xh, xl)[b][par][:, k, t * P:(t + 1) * P], m.wvT[a][:, k, :])
                                 for a, b in ((0, 0), (1, 0), (0, 1)) for k in range(KD)]
                    for i, (lhs, rhs) in enumerate(terms):
                        ins = pe.matmul(pm[j % 4][:], lhs, rhs, start=(i == 0), stop=(i == len(terms) - 1))
                    ins.then_inc(mm_done if j < NMM - 1 else x_read, 1)

            turn(0, 0, 1)
            with pe.Fori(0, LAST // 2) as i:
                for par in range(2):
                    turn(2 * i + par + 1, 1 - par, i + 1 + par)
                    products(2 * i + par, par)
            turn(NG - 1, 1, NG // 2)
            products(NG - 2, 0)
            products(NG - 1, 1)


def band_cols(blk, lo, hi):
    a, b = max(lo, P * (blk - 1)), min(hi, P * (blk + 2))
    return (a, b, a - P * (blk - 1)) if a < b else None


def max_pieces(qb, kc):
    lo, hi = 512 * kc, 512 * (kc + 1)
    band = band_cols(qb, lo, hi)
    if band is None:
        return [(0, 512, None)]
    a, b, f = band
    out = [(0, a - lo, None)] if a > lo else []
    out.append((a - lo, b - lo, f))
    return out + ([(b - lo, 512, None)] if b < hi else [])


NPIECE = 8
MAX_UNITS = NB * 4
PER_STEP = 5


def stage_stack_rows(nc, d, m):
    with ExitStack() as c:
        def sb(name, shape, dt=F32):
            return c.enter_context(nc.sbuf_tensor(name, shape, dt))

        hot = sb("hot", [NSTEP, T])
        far = sb("far", [NSTEP, T])
        one = sb("one", [2, 512], F32R)
        hot_r = sb("hot_r", [NSTEP, T], F32R)
        far_r = [sb(f"far_r{i}", [NSTEP, T], F32R) for i in range(2)]
        shaped = c.enter_context(nc.semaphore("shaped"))
        rows_made = c.enter_context(nc.semaphore("rows_made"))
        rows_in = c.enter_context(nc.semaphore("rows_in"))
        block = c.enter_context(nc.Block())

        @block.gpsimd
        def _(pool):
            pool.memset(hot[:], 1.0).then_inc(shaped, 1)
            pool.memset(far[:], 1.0).then_inc(shaped, 1)
            pool.wait_ge(shaped, 2)
            pool.affine_select(out=hot[:], in_=hot[:], compare_op=ALU.is_ge, fill=0.0, base=0,
                               pattern=[[1, T]], channel_multiplier=-P).then_inc(shaped, 1)
            pool.affine_select(out=far[:], in_=far[:], compare_op=ALU.is_ge, fill=0.0, base=-2 * P,
                               pattern=[[1, T]], channel_multiplier=-P).then_inc(shaped, 1)
            pool.wait_ge(shaped, 4)
            pool.affine_select(out=hot[:], in_=hot[:], compare_op=ALU.is_gt, fill=0.0, base=P,
                               pattern=[[-1, T]], channel_multiplier=P).then_inc(shaped, 1)

        @block.vector
        def _(dve):
            dve.memset(one[:].bitcast(F32), 1.0)
            dve.wait_ge(shaped, 5)
            dve.tensor_copy(hot_r[:], hot[:])
            dve.tensor_scalar(far_r[0][:], far[:], m.dhi[0:NSTEP, :].bitcast(F32), None, ALU.mult)
            dve.tensor_scalar(far_r[1][:], far[:], m.dlo[0:NSTEP, :], None, ALU.mult).then_inc(rows_made, 1)

        @block.sync
        def _(sp):
            sp.wait_ge(rows_made, 1)
            for u in range(4):
                for i in range(2):
                    lo = ROW_STEP + i * NSTEP
                    sp.dma_start(m.qst[u][lo:lo + NSTEP, :].bitcast(F32), hot_r[:].bitcast(F32)).then_inc(rows_in, 16)
                    sp.dma_start(m.kst[u][lo:lo + NSTEP, :].bitcast(F32), far_r[i][:].bitcast(F32)).then_inc(rows_in, 16)
                for n in range(T // 512):
                    sp.dma_start(m.kst[u][ROW_SHIFT:ROWS, n * 512:(n + 1) * 512].bitcast(F32),
                                 one[:].bitcast(F32)).then_inc(rows_in, 16)
            sp.wait_ge(rows_in, 16 * 32)


def stage_attention(nc, d, m):
    with ExitStack() as c:
        def sb(name, shape, dt=F32):
            return c.enter_context(nc.sbuf_tensor(name, shape, dt))

        def sem(name):
            return c.enter_context(nc.semaphore(name))

        m.qst = [sb(f"qst{u}", [P, T], F32R) for u in range(4)]
        m.kst = [sb(f"kst{u}", [P, T], F32R) for u in range(4)]
        stage_stack_rows(nc, d, m)

        prob = [sb(f"prob{i}", [P, T]) for i in range(2)]
        vh = [sb(f"vh{i}", [P, NB, HD]) for i in range(2)]
        acc_s = sb("acc_s", [P, 512])
        sum_s = sb("sum_s", [P, 512])
        rec_s = sb("rec_s", [P, 512])
        cxo = [sb(f"cxo{i}", [P, 16, 32]) for i in range(2)]
        pieces = sb("pieces", [P, NB, NPIECE])
        junk = [sb(f"junk{i}", [P, BAND]) for i in range(2)]
        mq = sb("mq", [P, NB])
        mfull = sb("mfull", [P, NB])
        shift = sb("shift", [P, NB])
        sh_hi = sb("sh_hi", [NB, P], F32R)
        sh_lo = sb("sh_lo", [NB, P], F32R)

        st = [c.enter_context(nc.psum_tensor(f"st{i}", [P, 1024], F32)) for i in range(2)]
        mx = [c.enter_context(nc.psum_tensor(f"mx{i}", [P, 512], F32)) for i in range(2)]
        acc = c.enter_context(nc.psum_tensor("acc", [P, 512], F32))
        den = c.enter_context(nc.psum_tensor("den", [P, 512], F32))

        stack_in = [sem(f"stack_in{u}") for u in range(4)]
        shift_in = sem("shift_in")
        v_copied = sem("v_copied")
        s_done = [sem(f"s_done{i}") for i in range(2)]
        e_done = [sem(f"e_done{i}") for i in range(2)]
        pv_done = sem("pv_done")
        acc_taken = sem("acc_taken")
        mx_done = [sem(f"mx_done{i}") for i in range(2)]
        mx_taken = [sem(f"mx_taken{i}") for i in range(2)]
        m_chain = sem("m_chain")
        shift_done = sem("shift_done")
        turned = sem("sh_turned")
        sh_own = sem("sh_own")
        rec_done = sem("rec_done")
        norm_done = sem("norm_done")
        ctx_out = [sem(f"ctx_out{i}") for i in range(2)]
        block = c.enter_context(nc.Block())

        CTX_INC = 16 * 16
        LOOPS = NH // 4 - 1
        USES = (MAX_UNITS // 2 + 1, MAX_UNITS // 2)

        def four_heads(eng, body):
            with eng.Fori(0, LOOPS) as i:
                for u in range(4):
                    body(4 * i + u, i, u, False)
            for u in range(4):
                body(4 * LOOPS + u, LOOPS, u, u == 3)

        @block.sync
        def _(sp):
            def load_stacks(h, batch, u):
                for r, (q, k) in enumerate(((0, 0), (1, 0), (0, 1))):
                    for src, part, dst in ((m.q_d, q, m.qst), (m.k_d, k, m.kst)):
                        rows = src[part].rearrange("(b n) (h r) t -> b h r n t", b=B, r=HD)
                        sp.dma_start(dst[u][r * HD:(r + 1) * HD, :].bitcast(F32).rearrange("r (n t) -> r n t", t=GT),
                                     rows[batch, h]).then_inc(stack_in[u], 16)

            for u in range(4):
                load_stacks(u // B, u % B, u)
            for i in range(2):
                sp.sem_inc(ctx_out[i], 16)
            sp.wait_ge(mx_taken[0], USES[0] + 1)
            sp.dma_start(m.qst[0][ROW_SHIFT:ROW_SHIFT + 1, :].bitcast(F32), sh_hi[:].bitcast(F32)).then_inc(shift_in, 16)
            sp.dma_start(m.qst[0][ROW_SHIFT + 1:ROWS, :].bitcast(F32), sh_lo[:].bitcast(F32)).then_inc(shift_in, 16)

            def head(hh, i, u, last):
                if not last:
                    sp.wait_ge(mx_taken[0], USES[0] * (hh + 2) + 1)
                    nxt = m.qst[(u + 1) % 4]
                    sp.dma_start(nxt[ROW_SHIFT:ROW_SHIFT + 1, :].bitcast(F32), sh_hi[:].bitcast(F32)).then_inc(shift_in, 16)
                    sp.dma_start(nxt[ROW_SHIFT + 1:ROWS, :].bitcast(F32), sh_lo[:].bitcast(F32)).then_inc(shift_in, 16)
                if not isinstance(hh, int):
                    sp.wait_ge(s_done[1], NB * (hh + 1))
                    load_stacks(i * 2 + (u // B + 2), u % B, u)
                sp.wait_ge(norm_done, hh + 1 + 1)
                dst = m.ctx_d[hh].rearrange("(jm d) (jk g i) -> g d jk jm i", d=HD, jk=KD, g=4)
                src = cxo[u % 2]
                for g in range(4):
                    for jm in range(4):
                        sp.dma_start(dst[g, :, :, jm], src[g * HD:(g + 1) * HD, jm::4, :]).then_inc(ctx_out[u % 2], 16)

            four_heads(sp, head)
            for i in range(2):
                sp.wait_ge(ctx_out[i], CTX_INC * (NH // 2) + 16)

        @block.gpsimd
        def _(pool):
            pool.sem_inc(norm_done, 1)

            def copy_v(h, batch, par):
                src = m.v[:, batch * NB:(batch + 1) * NB, :].rearrange("p b (h e) -> p b h e", e=HD)
                pool.tensor_copy(vh[par][:], src[:, :, h, :]).then_inc(v_copied, 1)

            copy_v(0, 0, 0)

            def head(hh, i, u, last):
                if not last:
                    pool.wait_ge(acc_taken, hh + 1)
                    nu = u + 1
                    copy_v(i * 2 + nu // B, nu % B, nu % 2)
                pool.wait_ge(rec_done, hh + 1)
                pool.wait_ge(ctx_out[u % 2], CTX_INC * (i * 2 + u // 2) + 16)
                out = cxo[u % 2][:].rearrange("p j i -> p i j")
                pool.tensor_tensor(out, acc_s[:].rearrange("p (i j) -> p i j", j=16),
                                   rec_s[:].rearrange("p (i j) -> p i j", j=16), ALU.mult).then_inc(norm_done, 1)

            four_heads(pool, head)

        @block.scalar
        def _(act):
            for i in range(2):
                act.sem_inc(e_done[i], 1)

            def head(hh, i, u, last):
                for kb in range(NB):
                    act.wait_ge(pv_done, NB * hh + kb + 1)
                    for half in range(2):
                        act.wait_ge(s_done[half], NB * hh + kb + 1)
                        act.activation(prob[kb % 2][:, half * 1024:(half + 1) * 1024], st[half][:],
                                       ACT.Exp).then_inc(e_done[half], 1)

            four_heads(act, head)

        @block.vector
        def _(dve):
            for i in range(2):
                dve.sem_inc(mx_taken[i], 1)
            dve.memset(pieces[:], -3.0e38).then_inc(acc_taken, 1)
            dve.wait_ge(acc_taken, 1)

            def maxima(hh):
                slot = [0] * NB
                n_band = 0
                for unit in range(MAX_UNITS):
                    qb, kc, bank = unit // 4, unit % 4, unit % 2
                    scored = MAX_UNITS // 2 * hh + unit // 2 + 1
                    dve.wait_ge(mx_done[bank], scored)
                    cuts = sorted(max_pieces(qb, kc), key=lambda piece: piece[2] is not None)
                    for a, b, f in cuts:
                        out = pieces[:, qb, slot[qb]:slot[qb] + 1]
                        slot[qb] += 1
                        if f is None:
                            ins = dve.tensor_reduce(out, mx[bank][:, a:b], AX.X, ALU.max)
                        else:
                            ins = dve.tensor_tensor_reduce(junk[bank][:, 0:b - a], mx[bank][:, a:b],
                                                           m.t1[:, f:f + b - a], 1.0, -3.0e38, ALU.add, ALU.max, out)
                    ins.then_inc(mx_taken[bank], 1)
                assert max(slot) <= NPIECE
                for bank in range(2):
                    dve.wait_ge(mx_taken[bank], USES[bank] * hh + MAX_UNITS // 2 + 1)
                dve.tensor_reduce(mq[:], pieces[:], AX.X, ALU.max).then_inc(m_chain, 1)
                dve.wait_ge(m_chain, 2 * hh + 1)
                dve.tensor_scalar(mfull[:], mq[:], m.c0[:, 0:1], None, ALU.add).then_inc(m_chain, 1)
                dve.wait_ge(m_chain, 2 * hh + 2)
                dve.tensor_scalar(shift[:], mfull[:], -1.0, m.c0[:, 0:1], ALU.mult, ALU.add).then_inc(shift_done, 1)
                dve.wait_ge(turned, hh + 1)
                if not isinstance(hh, int) or hh > 0:
                    dve.wait_ge(shift_in, 32 * hh)
                dve.tensor_copy(sh_hi[:], mx[0][0:NB, 0:P]).then_inc(sh_own, 1)
                dve.wait_ge(sh_own, hh + 1)
                dve.tensor_tensor(sh_lo[:], mx[0][0:NB, 0:P], sh_hi[:].bitcast(F32), ALU.subtract).then_inc(mx_taken[0], 1)

            def take(hh):
                dve.wait_ge(pv_done, NB * (hh + 1) + 2)
                dve.wait_ge(norm_done, hh + 1)
                dve.tensor_copy(acc_s[:], acc[:])
                dve.tensor_copy(sum_s[:], den[:]).then_inc(acc_taken, 1)
                dve.wait_ge(acc_taken, hh + 2)
                dve.reciprocal(rec_s[:], sum_s[:]).then_inc(rec_done, 1)

            maxima(0)

            def head(hh, i, u, last):
                if not last:
                    maxima(hh + 1)
                take(hh)

            four_heads(dve, head)

        @block.tensor
        def _(pe):
            pe.sem_inc(pv_done, 2)

            def max_unit(hh, u, unit):
                qb, kc, bank = unit // 4, unit % 4, unit % 2
                pe.wait_ge(mx_taken[bank], USES[bank] * hh + unit // 2 + 1)
                pe.matmul(mx[bank][:], m.qst[u][0:ROW_SHIFT, qb * P:(qb + 1) * P],
                          m.kst[u][0:ROW_SHIFT, kc * 512:(kc + 1) * 512], start=True, stop=True)\
                    .then_inc(mx_done[bank], 1)

            def turn_shift(hh):
                pe.wait_ge(shift_done, hh + 1)
                pe.wait_ge(mx_taken[0], USES[0] * hh + MAX_UNITS // 2 + 1)
                pe.transpose(mx[0][0:NB, 0:P], shift[:], m.ident[:]).then_inc(turned, 1)

            def scores(hh, u, kb, half):
                pe.wait_ge(e_done[half], NB * hh + kb + 1)
                for n in range(2):
                    q0 = half * 1024 + n * 512
                    band = band_cols(kb, q0, q0 + 512)
                    ins = pe.matmul(st[half][:, n * 512:(n + 1) * 512], m.kst[u][0:ROWS, kb * P:(kb + 1) * P],
                                    m.qst[u][0:ROWS, q0:q0 + 512], start=True, stop=band is None)
                    if band:
                        a, b, f = band
                        o = a - half * 1024
                        for part in (m.t2hi, m.t2lo):
                            ins = pe.matmul(st[half][:, o:o + b - a], m.ident_r[:], part[:, f:f + b - a],
                                            start=False, stop=part is m.t2lo)
                ins.then_inc(s_done[half], 1)

            def values(hh, par, kb):
                for half in range(2):
                    pe.wait_ge(e_done[half], NB * hh + kb + 2)
                if kb == 0:
                    pe.wait_ge(acc_taken, hh + 1)
                for dst, lhs in ((acc, vh[par][:, kb, :]), (den, m.ones[:, 0:HD])):
                    for g in range(4):
                        ins = pe.matmul(dst[g * HD:(g + 1) * HD, :], lhs, prob[kb % 2][:, g * 512:(g + 1) * 512],
                                        start=(kb == 0), stop=(kb == NB - 1))
                ins.then_inc(pv_done, 1)

            pe.wait_ge(stack_in[0], 96)
            for unit in range(MAX_UNITS):
                max_unit(0, 0, unit)
            turn_shift(0)

            def head(hh, i, u, last):
                pe.wait_ge(shift_in, 32 * (hh + 1))
                nu = (u + 1) % 4
                if not last:
                    pe.wait_ge(stack_in[nu], 96 * (i + 1 + (u == 3)))
                units = list(range(MAX_UNITS)) if not last else []
                for kb in range(NB):
                    scores(hh, u, kb, 0)
                    for _ in range(PER_STEP // 2):
                        if units:
                            max_unit(hh + 1, nu, units.pop(0))
                    scores(hh, u, kb, 1)
                    for _ in range(PER_STEP - PER_STEP // 2):
                        if units:
                            max_unit(hh + 1, nu, units.pop(0))
                    if kb == 0:
                        pe.wait_ge(v_copied, hh + 1)
                    else:
                        values(hh, u % 2, kb - 1)
                    if kb == NB - 2 and not last:
                        turn_shift(hh + 1)
                values(hh, u % 2, NB - 1)

            four_heads(pe, head)


SLOTS = 4


def stage_rows(nc, d, m, out):
    with ExitStack() as c:
        def sb(name, shape, dt=F32):
            return c.enter_context(nc.sbuf_tensor(name, shape, dt))

        def sem(name):
            return c.enter_context(nc.semaphore(name))

        def slots(name, shape, dt=F32):
            return [sb(f"{name}{u}", shape, dt) for u in range(SLOTS)]

        bo, fb = sb("bo", [P, D]), sb("fb_r", [P, D])
        cin, xin = slots("cin", [P, KD, P]), slots("xin", [P, D])
        ch, cl = slots("ch", [P, KD, P], F32R), slots("cl", [P, KD, P], F32R)
        xb, res1 = slots("xb", [P, D]), slots("res1", [P, D])
        stats, mean = slots("stats", [P, 6]), slots("mean", [P, 2])
        veps, rstd = slots("veps", [P, 1]), slots("rstd", [P, 1])
        half, eps = sb("half", [P, 1]), sb("eps", [P, 1])
        x2, x2T = slots("x2", [P, D]), slots("x2T", [P, KD, P])
        nmax, esum, rsum = slots("nmax", [P, 1]), slots("esum", [P, 1]), slots("rsum", [P, 1])
        pe_, peT = slots("pex", [P, LC]), slots("pexT", [LC, P])
        res2, x3 = slots("res2", [P, D]), slots("x3", [P, D])
        res3, fin = slots("res3", [P, D]), slots("fin", [P, D])
        pa = [c.enter_context(nc.psum_tensor(f"pa{u}", [P, 512], F32)) for u in range(SLOTS)]
        pb = [c.enter_context(nc.psum_tensor(f"pb{u}", [P, 512], F32)) for u in range(SLOTS)]

        bias_in = sem("bias_in")
        tile_in = [sem(f"tile_in{u}") for u in range(SLOTS)]
        cut_hi = sem("cut_hi")
        cut = sem("cut")
        xb_done = sem("xb_done")
        proj_done = sem("proj_done")
        res_done = sem("res_done")
        stats_done = sem("stats_done")
        aggr_done = sem("aggr_done")
        rsum_done = sem("rsum_done")
        mid_done = sem("mid_done")
        veps_done = sem("veps_done")
        rstd_done = sem("rstd_done")
        x2_done = sem("x2_done")
        x2_turned = sem("x2_turned")
        x2T_done = sem("x2T_done")
        cs_done = sem("cs_done")
        nmax_done = sem("nmax_done")
        ex_done = sem("ex_done")
        ex_turned = sem("ex_turned")
        exT_done = sem("exT_done")
        cv_done = sem("cv_done")
        x3_done = sem("x3_done")
        stored = [sem(f"stored{u}") for u in range(SLOTS)]
        block = c.enter_context(nc.Block())
        TURNS = NB // SLOTS
        xrow = d["x"].rearrange("b (n p) c -> (b n) p c", p=P)
        x3row = m.x3_d.rearrange("(n p) c -> n p c", p=P)
        orow = out.rearrange("b (n p) c -> b n p c", p=P)

        def batches(eng, body):
            for b in range(B):
                with eng.Fori(0, TURNS) as i:
                    body(i + TURNS * b, i, b)

        def norms(t, b, k):
            done = SLOTS * (2 * t if b == 0 else 2 * TURNS + 3 * (t - TURNS))
            return done + SLOTS * k

        @block.sync
        def _(sp):
            sp.dma_start(bo[:], bcast_rows(d["L0_attn_bo"])).then_inc(bias_in, 16)
            sp.dma_start(fb[:], bcast_rows(d["L0_ffn_bias"])).then_inc(bias_in, 16)
            for u in range(SLOTS):
                sp.sem_inc(stored[u], 16)

            def load(row, t):
                for u in range(SLOTS):
                    sp.wait_ge(cut, SLOTS * t + u + 1)
                    sp.wait_ge(xb_done, SLOTS * t + u + 1)
                    sp.dma_start(cin[u][:].rearrange("p k r -> p (k r)"), m.ctx_d[row + u]).then_inc(tile_in[u], 16)
                    sp.dma_start(xin[u][:], xrow[row + u]).then_inc(tile_in[u], 16)

            def body(t, i, b):
                load(SLOTS * t, t)
                for u in range(SLOTS):
                    sp.wait_ge(x3_done, SLOTS * t + u + 1 + SLOTS)
                    if b == 0:
                        sp.dma_start(x3row[SLOTS * i + u], x3[u][:]).then_inc(stored[u], 16)
                    else:
                        sp.dma_start(orow[1, SLOTS * i + u], fin[u][:]).then_inc(stored[u], 16)

            batches(sp, body)
            for u in range(SLOTS):
                sp.wait_ge(stored[u], 16 * (B * TURNS + 1))

        @block.gpsimd
        def _(pool):
            pool.memset(eps[:], EPS)
            pool.memset(half[:], -0.5).then_inc(xb_done, SLOTS)
            pool.wait_ge(xb_done, SLOTS)
            pool.wait_ge(bias_in, 32)

            def body(t, i, b):
                for u in range(SLOTS):
                    pool.wait_ge(tile_in[u], 32 * (t + 1))
                    pool.wait_ge(x3_done, SLOTS * t + u + 1)
                    pool.tensor_tensor(xb[u][:], xin[u][:], bo[:], ALU.add).then_inc(xb_done, 1)
                for k in range(2 + b):
                    for u in range(SLOTS):
                        pool.wait_ge(aggr_done, norms(t, b, k) + u + 1)
                        pool.tensor_tensor(veps[u][:], mean[u][:, 1:2], eps[:], ALU.add).then_inc(veps_done, 1)
                    for u in range(SLOTS):
                        pool.wait_ge(veps_done, norms(t, b, k) + u + 1)
                        pool.tensor_tensor(rstd[u][:], veps[u][:], half[:], ALU.pow).then_inc(rstd_done, 1)

            batches(pool, body)

        @block.scalar
        def _(act):
            def body(t, i, b):
                for u in range(SLOTS):
                    act.wait_ge(x2_turned, SLOTS * t + u + 1)
                    act.copy(x2T[u][:], pb[u][:].rearrange("p (k r) -> p k r", k=KD)).then_inc(x2T_done, 1)
                for u in range(SLOTS):
                    act.wait_ge(nmax_done, SLOTS * t + u + 1)
                    act.activation(pe_[u][:], pa[u][:, 0:LC], ACT.Exp, bias=nmax[u][:, 0:1],
                                   accum_out=esum[u][:]).then_inc(ex_done, 1)
                for u in range(SLOTS):
                    act.wait_ge(ex_turned, SLOTS * t + u + 1)
                    act.copy(peT[u][:], pb[u][0:LC, 0:P]).then_inc(exT_done, 1)

            batches(act, body)

        @block.vector
        def _(dve):
            dve.sem_inc(cut, SLOTS)
            dve.sem_inc(x3_done, SLOTS)

            def normalise(t, b, k, src, dst, dst_done):
                n = norms(t, b, k)
                for u in range(SLOTS):
                    dve.wait_ge(res_done, n + u + 1)
                    dve.bn_stats(stats[u][:], src[u][:]).then_inc(stats_done, 1)
                for u in range(SLOTS):
                    dve.wait_ge(bias_in, 32)
                    dve.wait_ge(stats_done, n + u + 1)
                    dve.bn_aggr(mean[u][:], stats[u][:]).then_inc(aggr_done, 1)
                for u in range(SLOTS):
                    dve.wait_ge(rstd_done, n + u + 1)
                    dve.tensor_scalar(dst[u][:], src[u][:], mean[u][:, 0:1], rstd[u][:, 0:1],
                                      ALU.subtract, ALU.mult).then_inc(dst_done, 1)

            def body(t, i, b):
                for u in range(SLOTS):
                    dve.wait_ge(tile_in[u], 32 * (t + 1))
                    dve.tensor_copy(ch[u][:], cin[u][:]).then_inc(cut_hi, 1)
                    dve.wait_ge(cut_hi, SLOTS * t + u + 1)
                    dve.tensor_tensor(cl[u][:], cin[u][:], ch[u][:].bitcast(F32), ALU.subtract).then_inc(cut, 1)
                for u in range(SLOTS):
                    dve.wait_ge(proj_done, SLOTS * t + u + 1)
                    dve.wait_ge(xb_done, SLOTS * (t + 1) + u + 1)
                    dve.tensor_tensor(res1[u][:], pa[u][:], xb[u][:], ALU.add).then_inc(res_done, 1)
                normalise(t, b, 0, res1, x2, x2_done)
                for u in range(SLOTS):
                    dve.wait_ge(cs_done, SLOTS * t + u + 1)
                    dve.tensor_reduce(nmax[u][:], pa[u][:, 0:LC], AX.X, ALU.max, negate=True).then_inc(nmax_done, 1)
                for u in range(SLOTS):
                    dve.wait_ge(ex_done, SLOTS * t + u + 1)
                    dve.reciprocal(rsum[u][:], esum[u][:]).then_inc(rsum_done, 1)
                for u in range(SLOTS):
                    dve.wait_ge(cv_done, SLOTS * t + u + 1)
                    dve.wait_ge(rsum_done, SLOTS * t + u + 1)
                    dve.scalar_tensor_tensor(out=res2[u][:], in0=pa[u][:], scalar=rsum[u][:, 0:1], in1=x2[u][:],
                                             op0=ALU.mult, op1=ALU.add).then_inc(res_done, 1)
                for u in range(SLOTS):
                    dve.wait_ge(stored[u], 16 * (t + 1))
                if b == 0:
                    normalise(t, b, 1, res2, x3, x3_done)
                else:
                    normalise(t, b, 1, res2, x3, mid_done)
                    for u in range(SLOTS):
                        dve.wait_ge(mid_done, SLOTS * i + u + 1)
                        dve.tensor_tensor(res3[u][:], x3[u][:], fb[:], ALU.add).then_inc(res_done, 1)
                    normalise(t, b, 2, res3, fin, x3_done)

            dve.wait_ge(bias_in, 32)
            batches(dve, body)

        @block.tensor
        def _(pe):
            def body(t, i, b):
                for u in range(SLOTS):
                    pe.wait_ge(cut, SLOTS * (t + 1) + u + 1)
                    pe.wait_ge(x3_done, SLOTS * t + u + 1)
                    terms = [((ch, cl)[x][u][:, k, :], m.woT[w][:, k, :])
                             for x, w in ((0, 0), (1, 0), (0, 1)) for k in range(KD)]
                    for n, (lhs, rhs) in enumerate(terms):
                        ins = pe.matmul(pa[u][:], lhs, rhs, start=(n == 0), stop=(n == len(terms) - 1))
                    ins.then_inc(proj_done, 1)
                for u in range(SLOTS):
                    pe.wait_ge(x2_done, SLOTS * t + u + 1)
                    for k in range(KD):
                        ins = pe.transpose(pb[u][:, k * P:(k + 1) * P], x2[u][:, k * P:(k + 1) * P], m.ident[:])
                    ins.then_inc(x2_turned, 1)
                for u in range(SLOTS):
                    pe.wait_ge(x2T_done, SLOTS * t + u + 1)
                    pe.matmul(pa[u][:, 0:LC], m.ones[0:1, :], m.g0[:, b, :], start=True, stop=False)
                    for k in range(KD):
                        ins = pe.matmul(pa[u][:, 0:LC], x2T[u][:, k, :], m.g[:, b, k, :], start=False,
                                        stop=(k == KD - 1))
                    ins.then_inc(cs_done, 1)
                for u in range(SLOTS):
                    pe.wait_ge(ex_done, SLOTS * t + u + 1)
                    pe.transpose(pb[u][0:LC, 0:P], pe_[u][:], m.ident[:]).then_inc(ex_turned, 1)
                for u in range(SLOTS):
                    pe.wait_ge(exT_done, SLOTS * t + u + 1)
                    pe.matmul(pa[u][:], peT[u][:], m.vx[:, b, :], start=True, stop=True).then_inc(cv_done, 1)

            batches(pe, body)


def stage_experts(nc, d, m, out):
    with ExitStack() as c:
        def sb(name, shape, dt=F32):
            return c.enter_context(nc.sbuf_tensor(name, shape, dt))

        def sem(name):
            return c.enter_context(nc.semaphore(name))

        w1 = sb("ew1", [P, 2, KD, FF])
        w2 = sb("ew2", [P, 2, FC, D])
        pick = [sb(f"pick{i}", [P, 1], I32) for i in range(2)]
        xg = [sb(f"exg{i}", [P, D]) for i in range(2)]
        xgT = [sb(f"exgT{i}", [P, KD, P]) for i in range(2)]
        hid = sb("hid", [P, FF])
        hidT = sb("hidT", [P, FC, P])
        yt = [sb(f"yt{i}", [P, D]) for i in range(2)]
        ph = c.enter_context(nc.psum_tensor("ph", [P, FF], F32))
        pt = [c.enter_context(nc.psum_tensor(f"pte{i}", [P, 512], F32)) for i in range(2)]
        py = c.enter_context(nc.psum_tensor("py", [P, 512], F32))
        px = c.enter_context(nc.psum_tensor("px", [P, 512], F32))

        w_in = sem("w_in")
        picked = sem("picked")
        rows_in = [sem(f"rows_in{i}") for i in range(2)]
        x_turned = sem("ex_turned_x")
        xT_done = sem("exT_copied")
        h_done = [sem(f"h_done{j}") for j in range(4)]
        g_done = [sem(f"g_done{j}") for j in range(4)]
        ht_done = sem("ht_done")
        ht_copied = sem("ht_copied")
        y_done = sem("y_done")
        y_copied = sem("y_copied")
        y_out = [sem(f"y_out{i}") for i in range(2)]
        block = c.enter_context(nc.Block())
        PAIRS = NTILE // 2
        w1v = d["L0_ffn_w1"].rearrange("e (k p) f -> e p k f", p=P)
        w2v = d["L0_ffn_w2"].rearrange("e (k p) n -> e p k n", p=P)
        yrow = m.y_d.rearrange("(t p) c -> t p c", p=P)

        def tiles(eng, body):
            with eng.Fori(0, PAIRS) as i:
                for par in range(2):
                    body(2 * i + par, i, par)
            body(NTILE - 1, PAIRS, 0)

        @block.sync
        def _(sp):
            for e in range(NE):
                if e >= 2:
                    first = sp.value_load(m.efirst[0:1, e - 1:e], min_val=1, max_val=NTILE)
                    sp.wait_ge(y_done, first + 1)
                if e >= 1:
                    sp.wait_ge(w_in, 32 * e)
                sp.dma_start(w1[:, e % 2], w1v[e]).then_inc(w_in, 16)
                sp.dma_start(w2[:, e % 2], w2v[e]).then_inc(w_in, 16)

        @block.gpsimd
        def _(pool):
            def body(t, i, par):
                pool.wait_ge(x_turned, t + 1)
                pool.tensor_copy(pick[par][:], m.perm[:, bass.ds(t, 1)]).then_inc(picked, 1)
                pool.wait_ge(picked, 1)
                pool.wait_ge(picked, t + 1)
                pool.indirect_dma_start(xg[par][:], None, m.x3_d, bass.IndirectOffsetOnAxis(pick[par][:], 0))\
                    .then_inc(rows_in[par], 16)

            tiles(pool, body)

        @block.scalar
        def _(act):
            for j in range(4):
                act.sem_inc(g_done[j], 1)
            act.sem_inc(y_copied, 1)
            for i in range(2):
                act.sem_inc(y_out[i], 16)

            def copy_y(t, i, par):
                act.wait_ge(y_done, t + 2)
                act.wait_ge(y_out[par], 16 * (i + 1))
                act.copy(yt[par][:], py[:]).then_inc(y_copied, 1)
                act.wait_ge(y_copied, t + 2)
                act.dma_start(yrow[t], yt[par][:]).then_inc(y_out[par], 16)

            def body(t, i, par):
                for j in range(4):
                    act.wait_ge(h_done[j], t + 1)
                    act.wait_ge(ht_done, 4 * t + j + 1)
                    act.activation(hid[:, j * 512:(j + 1) * 512], ph[:, j * 512:(j + 1) * 512], ACT.Gelu)\
                        .then_inc(g_done[j], 1)
                copy_y(t, i, par)

            tiles(act, body)
            act.wait_ge(y_out[0], 16 * (PAIRS + 2))
            act.wait_ge(y_out[1], 16 * (PAIRS + 1))

        @block.vector
        def _(dve):
            dve.sem_inc(ht_copied, 2)

            def copy_x(t, par):
                dve.wait_ge(x_turned, t + 1 + 2)
                dve.tensor_copy(xgT[par][:], px[:].rearrange("p (k r) -> p k r", k=KD)).then_inc(xT_done, 1)

            copy_x(0, 0)

            def body(t, i, par):
                if not isinstance(t, int):
                    copy_x(t + 1, 1 - par)
                for j in range(4):
                    dve.wait_ge(ht_done, 4 * t + j + 1 + 4)
                    if j == 0:
                        dve.wait_ge(y_done, t + 1)
                    dve.tensor_copy(hidT[:, 4 * j:4 * j + 4, :], pt[j % 2][:].rearrange("p (k r) -> p k r", k=4))\
                        .then_inc(ht_copied, 1)

            tiles(dve, body)

        @block.tensor
        def _(pe):
            pe.sem_inc(x_turned, 2)
            pe.sem_inc(ht_done, 4)
            pe.sem_inc(y_done, 1)

            def turn_x(t, i, par):
                pe.wait_ge(rows_in[par], 16 * (i + 1))
                if not isinstance(t, int) or t > 0:
                    pe.wait_ge(xT_done, t)
                for k in range(KD):
                    ins = pe.transpose(px[:, k * P:(k + 1) * P], xg[par][:, k * P:(k + 1) * P], m.ident[:])
                ins.then_inc(x_turned, 1)

            def up(t, par):
                expert = pe.value_load(m.texp[0:1, bass.ds(t, 1)], min_val=0, max_val=NE - 1)
                slot = pe.value_load(m.tslot[0:1, bass.ds(t, 1)], min_val=0, max_val=1)
                pe.wait_ge(w_in, 32 * expert + 32)
                pe.wait_ge(xT_done, t + 1)
                for j in range(4):
                    pe.wait_ge(g_done[j], t + 1)
                    for k in range(KD):
                        ins = pe.matmul(ph[:, j * 512:(j + 1) * 512], xgT[par][:, k, :],
                                        w1[:, bass.ds(slot, 1), k, j * 512:(j + 1) * 512]
                                        .rearrange("p s f -> p (s f)"), start=(k == 0), stop=(k == KD - 1))
                    ins.then_inc(h_done[j], 1)
                return slot

            def down(t, slot):
                for j in range(4):
                    pe.wait_ge(g_done[j], t + 2)
                    pe.wait_ge(ht_copied, 4 * t + j + 1)
                    for k in range(4):
                        f = 4 * j + k
                        ins = pe.transpose(pt[j % 2][:, k * P:(k + 1) * P], hid[:, f * P:(f + 1) * P], m.ident[:])
                    ins.then_inc(ht_done, 1)
                for j in range(4):
                    pe.wait_ge(ht_copied, 4 * t + j + 1 + 2)
                    if j == 0:
                        pe.wait_ge(y_copied, t + 1)
                    for k in range(4):
                        f = 4 * j + k
                        ins = pe.matmul(py[:], hidT[:, f, :], w2[:, bass.ds(slot, 1), f, :]
                                        .rearrange("p s n -> p (s n)"), start=(f == 0), stop=(f == FC - 1))
                ins.then_inc(y_done, 1)

            turn_x(0, 0, 0)

            def body(t, i, par):
                slot = up(t, par)
                if not isinstance(t, int):
                    turn_x(t + 1, i + par, 1 - par)
                down(t, slot)

            tiles(pe, body)

    stage_combine(nc, d, m, out)


def stage_combine(nc, d, m, out):
    with ExitStack() as c:
        def sb(name, shape, dt=F32):
            return c.enter_context(nc.sbuf_tensor(name, shape, dt))

        def sem(name):
            return c.enter_context(nc.semaphore(name))

        N = NTOK // P
        fb = sb("fb_c", [P, D])
        half = sb("half_c", [P, 1])
        veps = [sb(f"cveps{i}", [P, 1]) for i in range(2)]
        x3 = sb("x3c", [P, N, D])
        yg = [[sb(f"yg{i}{j}", [P, D]) for j in range(TOPK)] for i in range(4)]
        s1 = [sb(f"s1_{i}", [P, D]) for i in range(2)]
        s2 = [sb(f"s2_{i}", [P, D]) for i in range(2)]
        xs = [sb(f"xs_{i}", [P, D]) for i in range(2)]
        stats = [sb(f"cst{i}", [P, 6]) for i in range(2)]
        mean = [sb(f"cmean{i}", [P, 2]) for i in range(2)]
        rstd = [sb(f"crstd{i}", [P, 1]) for i in range(2)]
        fin = [sb(f"cfin{i}", [P, D]) for i in range(2)]
        own_in = sem("own_in")
        y_in = [sem(f"y_in{i}") for i in range(4)]
        xs_done = sem("xs_done")
        sum_chain = sem("sum_chain")
        c_aggr = sem("c_aggr")
        c_veps = sem("c_veps")
        c_rstd = sem("c_rstd")
        fin_done = sem("fin_done")
        fin_out = [sem(f"fin_out{i}") for i in range(2)]
        block = c.enter_context(nc.Block())
        orow = out.rearrange("b (n p) c -> b n p c", p=P)

        @block.sync
        def _(sp):
            sp.dma_start(fb[:], bcast_rows(d["L0_ffn_bias"])).then_inc(own_in, 16)
            sp.dma_start(x3[:], m.x3_d.rearrange("(n p) c -> p n c", p=P)).then_inc(own_in, 16)
            for n in range(N):
                sp.wait_ge(fin_done, n + 1)
                sp.dma_start(orow[0, n], fin[n % 2][:]).then_inc(fin_out[n % 2], 16)
            for i in range(2):
                sp.wait_ge(fin_out[i], 16 * (N // 2))

        @block.gpsimd
        def _(pool):
            def gather(n):
                for j in range(TOPK):
                    pool.indirect_dma_start(yg[n % 4][j][:], None, m.y_d,
                                            bass.IndirectOffsetOnAxis(m.pos[:, TOPK * n + j:TOPK * n + j + 1], 0))\
                        .then_inc(y_in[n % 4], 16)

            pool.memset(half[:], -0.5).then_inc(c_veps, 1)
            for n in range(4):
                gather(n)
            for n in range(N):
                pool.wait_ge(c_aggr, n + 1)
                pool.tensor_scalar(veps[n % 2][:], mean[n % 2][:, 1:2], EPS, None, ALU.add).then_inc(c_veps, 1)
                pool.wait_ge(c_veps, n + 2)
                pool.tensor_tensor(rstd[n % 2][:], veps[n % 2][:], half[:], ALU.pow).then_inc(c_rstd, 1)
                if n + 4 < N:
                    gather(n + 4)

        @block.vector
        def _(dve):
            dve.wait_ge(own_in, 32)
            for n in range(N):
                i = n % 2
                dve.tensor_tensor(xs[i][:], x3[:, n, :], fb[:], ALU.add).then_inc(xs_done, 1)
                dve.wait_ge(y_in[n % 4], 32 * (n // 4 + 1))
                dve.wait_ge(xs_done, n + 1)
                dve.scalar_tensor_tensor(out=s1[i][:], in0=yg[n % 4][0][:], scalar=m.tokw[:, TOPK * n:TOPK * n + 1],
                                         in1=xs[i][:], op0=ALU.mult, op1=ALU.add).then_inc(sum_chain, 1)
                dve.wait_ge(sum_chain, 3 * n + 1)
                dve.scalar_tensor_tensor(out=s2[i][:], in0=yg[n % 4][1][:],
                                         scalar=m.tokw[:, TOPK * n + 1:TOPK * n + 2],
                                         in1=s1[i][:], op0=ALU.mult, op1=ALU.add).then_inc(sum_chain, 1)
                dve.wait_ge(sum_chain, 3 * n + 2)
                dve.bn_stats(stats[i][:], s2[i][:]).then_inc(sum_chain, 1)
                dve.wait_ge(sum_chain, 3 * n + 3)
                dve.bn_aggr(mean[i][:], stats[i][:]).then_inc(c_aggr, 1)
                dve.wait_ge(c_rstd, n + 1)
                if n >= 2:
                    dve.wait_ge(fin_out[i], 16 * (n // 2))
                dve.tensor_scalar(fin[i][:], s2[i][:], mean[i][:, 0:1], rstd[i][:, 0:1],
                                  ALU.subtract, ALU.mult).then_inc(fin_done, 1)



def build(nc, d, out):
    m = Mem()
    m.ext_t = nc.dram_tensor("ext_scr", [1, 512], F32)
    m.ext_d = m.ext_t.ap()
    m.perm_d = nc.dram_tensor("perm_scr", [NTILE * P, 1], I32).ap()
    m.q_d = nc.dram_tensor("q_scr", [2, NG, D, GT], F32).ap()
    m.k_d = nc.dram_tensor("k_scr", [2, NG, D, GT], F32).ap()
    m.ctx_d = nc.dram_tensor("ctx_scr", [NH, P, KD * P], F32).ap()
    m.x3_d = nc.dram_tensor("x3_scr", [NTOK, D], F32).ap()
    m.y_d = nc.dram_tensor("y_scr", [NTILE * P, D], F32).ap()
    with ExitStack() as c:
        def sb(name, shape, dt=F32):
            return c.enter_context(nc.sbuf_tensor(name, shape, dt))

        m.ident = sb("ident", [P, P])
        m.ident_r = sb("ident_r", [P, P], F32R)
        m.ones = sb("ones", [P, P])
        m.bq, m.bqs, m.bk = sb("bq", [P, KD]), sb("bqs", [P, KD]), sb("bk", [P, KD])
        m.bv = sb("bv", [P, D])
        m.c0 = sb("c0", [P, 1])
        m.dhi, m.dlo = sb("dhi", [P, 1], F32R), sb("dlo", [P, 1])
        m.t1 = sb("t1", [P, BAND])
        m.t2hi, m.t2lo = sb("t2hi", [P, BAND], F32R), sb("t2lo", [P, BAND], F32R)
        m.woT = [sb(f"woT{i}", [P, KD, D], F32R) for i in range(2)]
        m.g, m.g0, m.vx = sb("g", [P, B, KD, LC]), sb("g0", [1, B, LC]), sb("vx", [LC, B, D])
        m.pos, m.perm = sb("pos", [P, NCOL], I32), sb("perm", [P, NTILE], I32)
        m.tokw = sb("tokw", [P, NCOL])
        m.texp, m.tslot, m.efirst = sb("texp", [1, NTILE], I32), sb("tslot", [1, NTILE], I32), sb("efirst", [1, NE], I32)
        with nc.sbuf_tensor("v", [P, NROW // P, D], F32) as m.v:
            with ExitStack() as cw:
                def parts(name):
                    return [cw.enter_context(nc.sbuf_tensor(f"{name}{i}", [P, KD, D], F32R)) for i in range(2)]

                m.wqT, m.wkT, m.wvT = parts("wqT"), parts("wkT"), parts("wvT")
                stage_setup(nc, d, m)
                stage_project(nc, d, m)
            stage_attention(nc, d, m)
        stage_rows(nc, d, m, out)
        stage_experts(nc, d, m, out)


INPUTS = ["x", "ctx_1024", "L0_attn_Wq", "L0_attn_bq", "L0_attn_Wk", "L0_attn_bk", "L0_attn_Wv", "L0_attn_bv",
          "L0_attn_Wo", "L0_attn_bo", "L0_attn_et_gate", "L0_attn_is_gate", "L0_attn_time_bias", "L0_xattn_Wq",
          "L0_xattn_bq", "L0_xattn_Wk", "L0_xattn_bk", "L0_xattn_Wv", "L0_xattn_bv", "L0_ffn_expert_weights",
          "L0_ffn_expert_indices", "L0_ffn_w1", "L0_ffn_w2", "L0_ffn_bias"]


def kernel(**inputs):
    import numpy as _np
    import concourse.bacc as _bacc
    from concourse import mybir as _mybir
    from concourse.bass_utils import run_bass_kernel_spmd as _run

    nc = _bacc.Bacc("TRN2", target_bir_lowering=False, num_devices=1)
    arrays, d = {}, {}
    for name in INPUTS:
        a = _np.ascontiguousarray(inputs[name])
        arrays[f"in_{name}"] = a
        d[name] = nc.dram_tensor(f"in_{name}", a.shape, _mybir.dt.from_np(a.dtype), kind="ExternalInput").ap()
    out = nc.dram_tensor("out_rows", (B, T, D), F32, kind="ExternalOutput").ap()
    build(nc, d, out)
    r = _run(nc, [arrays], core_ids=[0])
    return r.results[0]["out_rows"]
```

```python
from contextlib import ExitStack

import concourse.bass as bass
from concourse import mybir

F32 = mybir.dt.float32
F32R = mybir.dt.float32r
I32 = mybir.dt.int32
ALU = mybir.AluOpType
ACT = mybir.ActivationFunctionType
AX = mybir.AxisListType

P = 128
B, T, D = 2, 2048, 512
H = 16
HD = D // H
NROW = B * T
KD = D // P
NB = T // P
NH = B * H
TB_LEN = 250
TB_MID = TB_LEN // 2
EPS = 1e-5
QSCALE = 1.0 / float(HD) ** 0.5
XSCALE = 1.0 / float(D) ** 0.5
LC = 77
NE, FF = 8, 2048
FC = FF // P
NTOK = 2048
TOPK = 2
NCOL = NTOK // P * TOPK
NTILE = (NTOK * TOPK) // P + NE - 1

NSTEP = NB - 2
ROW_STEP = 3 * HD
ROW_SHIFT = ROW_STEP + 2 * NSTEP
ROWS = ROW_SHIFT + 2
BAND = 3 * P


G = 4
GT = G * P
NG = NROW // GT


class Mem:
    pass


def bcast_rows(ap, n=P):
    return ap.partition_broadcast(n)


def stage_setup(nc, d, m):
    with ExitStack() as c:
        def sb(name, shape, dt=F32):
            return c.enter_context(nc.sbuf_tensor(name, shape, dt))

        def sem(name):
            return c.enter_context(nc.semaphore(name))

        weights = [("wq", d["L0_attn_Wq"]), ("wk", d["L0_attn_Wk"]), ("wv", d["L0_attn_Wv"]), ("wo", d["L0_attn_Wo"]),
                   ("xq", d["L0_xattn_Wq"])]
        raw = [m.v[:, i * KD:(i + 1) * KD, :] for i in range(2)]
        xqT, xk_w, xv_w = (m.v[:, i * KD:(i + 1) * KD, :] for i in (2, 3, 4))
        cx = sb("cx", [LC, B, D])
        cxT = sb("cxT", [P, B, KD, LC])
        kxT = sb("kxT", [P, B, KD, LC])
        xbk = sb("xbk", [P, KD])
        xbq = sb("xbq", [P, KD])
        xbv = sb("xbv", [P, D])
        tb0 = sb("tb0", [P, 1])
        tbl = sb("tbl", [P, 1])
        gates = sb("gates", [P, 2])
        eneg = sb("eneg", [P, 1])
        epl = sb("epl", [P, 1])
        sig = sb("sig", [P, 1])
        dstep = sb("dstep", [P, 1])
        dfar = sb("dfar", [P, 1])
        c0a = sb("c0a", [P, 1])
        trow = sb("trow", [1, TB_LEN])
        ext = sb("ext", [1, 512])
        hank = sb("hank", [P, BAND])
        anti = sb("anti", [P, P])
        ei = sb("ei", [P, NCOL], I32)
        ef = sb("ef", [P, NCOL])
        oh = sb("oh", [P, NE, NCOL])
        tri = sb("tri", [P, P])
        tot = sb("tot", [P, NE, NCOL])
        sc = [sb(f"sc{i}", [P, NE, NCOL]) for i in range(5)]
        w1 = sb("w_1", [P, NE, NCOL])
        w2 = sb("w_2", [P, NE, NCOL])
        w3 = sb("w_3", [P, NE, NCOL])
        w4 = sb("w_4", [P, NE, NCOL])
        posf = sb("posf", [P, NCOL])
        cntf = sb("cntf", [P, NE])
        cnti = sb("cnti", [P, NE], I32)
        cntj = sb("cntj", [P, NE], I32)
        pad = sb("pad", [P, NE])
        ps1 = sb("ps1", [P, NE])
        ps2 = sb("ps2", [P, NE])
        ps3 = sb("ps3", [P, NE])
        base = sb("base", [P, NE])
        tio = sb("tio", [1, NTILE])
        tacc = [sb(f"tacc{i}", [1, NTILE]) for i in range(2)]
        toki = sb("toki", [P, NCOL], I32)
        zi = sb("zi", [P, NTILE], I32)

        pt = [c.enter_context(nc.psum_tensor(f"pt{i}", [P, 512], F32)) for i in range(4)]
        pr = c.enter_context(nc.psum_tensor("pr", [P, 512], F32))
        pq = c.enter_context(nc.psum_tensor("pq", [P, 512], F32))

        raw_in = [sem(f"raw_in{i}") for i in range(2)]
        small_in = sem("small_in")
        xw_in = sem("xw_in")
        turned = sem("turned")
        hi_done = sem("hi_done")
        lo_done = sem("lo_done")
        const_done = sem("const_done")
        v = sem("v_chain")
        eneg_done = sem("eneg_done")
        ext_out = sem("ext_out")
        tab_in = sem("tab_in")
        perm_zero = sem("perm_zero")
        perm_out = sem("perm_out")
        perm_in = sem("perm_in")
        rank_done = sem("rank_done")
        xt = sem("xt")
        tab_turned = sem("tab_turned")
        xe = sem("xe")
        block = c.enter_context(nc.Block())

        V_EXT, V_OH, V_POS = 9, 15, 33
        wT = {"wq": m.wqT, "wk": m.wkT, "wv": m.wvT, "wo": m.woT}

        @block.sync
        def _(sp):
            for n in range(2):
                sp.dma_start(raw[n], weights[n][1].rearrange("(o p) i -> p o i", p=P)).then_inc(raw_in[n], 16)
            with nc.allow_non_contiguous_dma("small vectors"):
                sp.dma_start(m.bq[:], d["L0_attn_bq"].rearrange("(m p) -> p m", p=P)).then_inc(small_in, 16)
                sp.dma_start(m.bk[:], d["L0_attn_bk"].rearrange("(m p) -> p m", p=P)).then_inc(small_in, 16)
                sp.dma_start(xbk[:], d["L0_xattn_bk"].rearrange("(m p) -> p m", p=P)).then_inc(small_in, 16)
                sp.dma_start(xbq[:], d["L0_xattn_bq"].rearrange("(m p) -> p m", p=P)).then_inc(small_in, 16)
                tb = d["L0_attn_time_bias"][0, 0]
                sp.dma_start(tb0[:], bcast_rows(tb[0:1])).then_inc(small_in, 16)
                sp.dma_start(tbl[:], bcast_rows(tb[TB_LEN - 1:TB_LEN])).then_inc(small_in, 16)
                sp.dma_start(gates[:, 0:1], bcast_rows(d["L0_attn_et_gate"][0, 0])).then_inc(small_in, 16)
                sp.dma_start(gates[:, 1:2], bcast_rows(d["L0_attn_is_gate"][0, 0])).then_inc(small_in, 16)
                sp.dma_start(ei[:].rearrange("p (c j) -> p c j", j=TOPK),
                             d["L0_ffn_expert_indices"].rearrange("(c p) j -> p c j", p=P)).then_inc(small_in, 16)
                sp.dma_start(m.tokw[:].rearrange("p (c j) -> p c j", j=TOPK),
                             d["L0_ffn_expert_weights"].rearrange("(c p) j -> p c j", p=P)).then_inc(small_in, 16)
            sp.dma_start(trow[:], d["L0_attn_time_bias"][0]).then_inc(small_in, 16)
            sp.dma_start(m.bv[:], bcast_rows(d["L0_attn_bv"])).then_inc(small_in, 16)
            sp.dma_start(xbv[:], bcast_rows(d["L0_xattn_bv"])).then_inc(small_in, 16)
            sp.dma_start(cx[:], d["ctx_1024"].rearrange("b t c -> t b c")).then_inc(xw_in, 16)
            sp.dma_start(xk_w, d["L0_xattn_Wk"].rearrange("(k p) o -> p k o", p=P)).then_inc(xw_in, 16)
            sp.dma_start(xv_w, d["L0_xattn_Wv"].rearrange("(k p) o -> p k o", p=P)).then_inc(xw_in, 16)
            for n in range(2, len(weights)):
                sp.wait_ge(turned, KD * (n - 1))
                sp.dma_start(raw[n % 2], weights[n][1].rearrange("(o p) i -> p o i", p=P)).then_inc(raw_in[n % 2], 16)
            sp.wait_ge(v, V_EXT)
            sp.dma_start(m.ext_d, ext[:]).then_inc(ext_out, 16)
            sp.wait_ge(ext_out, 16)
            sp.dma_start(hank[:], bass.AP(m.ext_t, 0, [[1, P], [1, BAND]])).then_inc(tab_in, 16)
            sp.wait_ge(perm_out, 16 * NCOL)
            with nc.allow_non_contiguous_dma("token list"):
                sp.dma_start(m.perm[:], m.perm_d.rearrange("(t p) o -> p (t o)", p=P)).then_inc(perm_in, 16)
            sp.wait_ge(perm_in, 16)
            sp.wait_ge(tab_in, 16)

        @block.gpsimd
        def _(pool):
            pool.memset(m.ident[:], 0.0).then_inc(const_done, 1)
            pool.memset(tri[:], 1.0).then_inc(const_done, 1)
            pool.memset(anti[:], 0.0).then_inc(const_done, 1)
            pool.wait_ge(const_done, 3)
            pool.affine_select(out=anti[:], in_=anti[:], compare_op=ALU.not_equal, fill=1.0, base=1 - P,
                               pattern=[[1, P]], channel_multiplier=1).then_inc(const_done, 1)
            pool.affine_select(out=m.ident[:], in_=m.ident[:], compare_op=ALU.not_equal, fill=1.0, base=0,
                               pattern=[[-1, P]], channel_multiplier=1).then_inc(const_done, 1)
            pool.affine_select(out=tri[:], in_=tri[:], compare_op=ALU.is_gt, fill=0.0, base=0,
                               pattern=[[1, P]], channel_multiplier=-1).then_inc(const_done, 1)
            pool.iota(toki[:].rearrange("p (c j) -> p c j", j=TOPK), [[P, NCOL // TOPK], [0, TOPK]], base=0,
                      channel_multiplier=1).then_inc(const_done, 1)
            pool.iota(tio[:], [[P, NTILE]], base=0, channel_multiplier=0,
                      allow_small_or_imprecise_dtypes=True).then_inc(const_done, 1)
            pool.memset(zi[:], 0).then_inc(const_done, 1)
            pool.wait_ge(const_done, 9)
            pool.dma_start(m.perm_d.rearrange("(p t) o -> p (t o)", p=P), zi[:]).then_inc(perm_zero, 16)
            pool.wait_ge(perm_zero, 16)
            pool.wait_ge(v, V_POS)
            for col in range(NCOL):
                pool.indirect_dma_start(m.perm_d, bass.IndirectOffsetOnAxis(m.pos[:, col:col + 1], 0),
                                        toki[:, col:col + 1], None).then_inc(perm_out, 16)

        @block.scalar
        def _(act):
            act.wait_ge(small_in, 16 * 13)
            act.activation(eneg[:], gates[:, 0:1], ACT.Exp, scale=-1.0).then_inc(eneg_done, 1)
            n = 0
            for name, _ in weights[:4]:
                for k in range(KD):
                    act.wait_ge(turned, n + 1)
                    act.copy(wT[name][0][:, k, :], pt[n % 4][:]).then_inc(hi_done, 1)
                    n += 1
            for k in range(KD):
                act.wait_ge(turned, n + 1)
                act.copy(xqT[:, k, :], pt[n % 4][:]).then_inc(hi_done, 1)
                n += 1
            for b in range(B):
                act.wait_ge(xt, b + 1)
                act.copy(cxT[:, b], pt[b][:, 0:KD * LC].rearrange("p (k t) -> p k t", t=LC)).then_inc(xe, 1)
            for b in range(B):
                act.wait_ge(xt, 2 + b + 1)
                for k in range(KD):
                    act.activation(kxT[:, b, k, :], pt[2 + b][:, k * LC:(k + 1) * LC], ACT.Identity,
                                   bias=xbk[:, k:k + 1]).then_inc(xe, 1)
            for b in range(B):
                act.wait_ge(xt, 4 + b + 1)
                act.mul(m.g[:, b], pt[b][:, 0:KD * LC].rearrange("p (k t) -> p k t", t=LC), XSCALE).then_inc(xe, 1)
            act.wait_ge(xt, 7)
            act.mul(m.g0[:], pr[0:1, 0:B * LC].rearrange("p (b t) -> p b t", b=B), XSCALE).then_inc(xe, 1)

        @block.vector
        def _(dve):
            dve.memset(m.ones[:], 1.0).then_inc(v, 1)
            dve.memset(ext[:], 0.0).then_inc(v, 1)
            dve.memset(tacc[0][:], 0.0).then_inc(v, 1)
            dve.wait_ge(small_in, 16 * 13)
            dve.wait_ge(eneg_done, 1)
            dve.tensor_scalar(epl[:], eneg[:], 1.0, None, ALU.add).then_inc(v, 1)
            dve.wait_ge(v, 4)
            dve.reciprocal(sig[:], epl[:]).then_inc(v, 1)
            dve.wait_ge(v, 5)
            dve.tensor_scalar(trow[:], trow[:], tb0[0:1, :], sig[0:1, :], ALU.subtract, ALU.mult).then_inc(v, 1)
            dve.wait_ge(v, 6)
            first = 2 * P - 1 - TB_MID
            dve.tensor_copy(ext[:, first:first + TB_LEN], trow[:]).then_inc(v, 1)
            dve.wait_ge(v, 7)
            dve.tensor_scalar(ext[:, first + TB_LEN:512], ext[:, first + TB_LEN:512],
                              trow[:, TB_LEN - 1:TB_LEN], None, ALU.add).then_inc(v, 2)
            dve.tensor_tensor(dstep[:], tbl[:], tb0[:], ALU.subtract).then_inc(v, 1)
            dve.tensor_scalar(m.c0[:], tb0[:], sig[:, 0:1], gates[:, 1:2], ALU.mult, ALU.add)
            dve.wait_ge(v, 10)
            dve.tensor_tensor(dfar[:], dstep[:], sig[:], ALU.mult).then_inc(v, 1)
            dve.wait_ge(v, 11)
            dve.tensor_copy(m.dhi[:], dfar[:]).then_inc(v, 1)
            dve.wait_ge(v, 12)
            dve.tensor_tensor(m.dlo[:], dfar[:], m.dhi[:].bitcast(F32), ALU.subtract).then_inc(v, 1)
            dve.tensor_copy(ef[:], ei[:]).then_inc(v, 1)
            dve.wait_ge(v, 14)
            for e in range(NE):
                ins = dve.tensor_scalar(oh[:, e, :], ef[:], float(e), None, ALU.is_equal)
            ins.then_inc(v, 1)
            n = 0
            for name, _ in weights[:4]:
                for k in range(KD):
                    dve.wait_ge(hi_done, n + 1)
                    dve.tensor_tensor(wT[name][1][:, k, :], pt[n % 4][:], wT[name][0][:, k, :].bitcast(F32),
                                      ALU.subtract).then_inc(lo_done, 1)
                    n += 1
            dve.wait_ge(rank_done, 2)
            dve.tensor_copy(tot[:], pq[:, 0:NE * NCOL].rearrange("p (e c) -> p e c", e=NE)).then_inc(v, 1)
            dve.wait_ge(v, 16)
            src, step = tot, 1
            for i in range(5):
                dve.tensor_copy(sc[i][:, :, 0:step], src[:, :, 0:step])
                dve.tensor_tensor(sc[i][:, :, step:], src[:, :, step:], src[:, :, 0:NCOL - step], ALU.add)\
                    .then_inc(v, 1)
                dve.wait_ge(v, 17 + i)
                src, step = sc[i], 2 * step
            dve.tensor_scalar(cntf[:], src[:, :, NCOL - 1], float(P - 1), None, ALU.add).then_inc(v, 1)
            dve.wait_ge(v, 22)
            dve.tensor_copy(cnti[:], cntf[:]).then_inc(v, 1)
            dve.wait_ge(v, 23)
            dve.tensor_scalar(cntj[:], cnti[:], 7, 7, ALU.arith_shift_right, ALU.arith_shift_left).then_inc(v, 1)
            dve.wait_ge(v, 24)
            dve.tensor_scalar(pad[:], cntj[:], float(P), None, ALU.max).then_inc(v, 1)
            dve.wait_ge(v, 25)
            src, step = pad, 1
            for i, dst in enumerate((ps1, ps2, ps3)):
                dve.tensor_copy(dst[:, 0:step], src[:, 0:step])
                dve.tensor_tensor(dst[:, step:], src[:, step:], src[:, 0:NE - step], ALU.add).then_inc(v, 1)
                dve.wait_ge(v, 26 + i)
                src, step = dst, 2 * step
            dve.tensor_tensor(w1[:], sc[4][:], tot[:], ALU.subtract)
            dve.tensor_tensor(base[:], ps3[:], pad[:], ALU.subtract).then_inc(v, 1)
            dve.wait_ge(v, 29)
            dve.tensor_tensor(w2[:], w1[:], base[:].unsqueeze(2).broadcast_to([P, NE, NCOL]), ALU.add).then_inc(v, 1)
            dve.wait_ge(v, 30)
            dve.tensor_tensor(w3[:], pr[:, 0:NE * NCOL].rearrange("p (e c) -> p e c", e=NE), w2[:], ALU.add)\
                .then_inc(v, 1)
            dve.wait_ge(v, 31)
            dve.tensor_tensor(w4[:], w3[:], oh[:], ALU.mult).then_inc(v, 1)
            dve.wait_ge(v, 32)
            dve.tensor_reduce(posf[:], w4[:].rearrange("p e c -> p c e"), AX.X, ALU.add)
            dve.drain()
            dve.tensor_copy(m.pos[:], posf[:]).then_inc(v, 1)
            dve.wait_ge(const_done, 9)
            for e in range(1, NE):
                dve.scalar_tensor_tensor(out=tacc[e % 2][:], in0=tio[:], scalar=base[0:1, e:e + 1],
                                         in1=tacc[(e + 1) % 2][:], op0=ALU.is_ge, op1=ALU.add)
                dve.drain()
            dve.tensor_copy(m.texp[:], tacc[1][:])
            dve.tensor_scalar(m.efirst[:], base[0:1, :], 1.0 / P, None, ALU.mult).then_inc(v, 1)
            dve.wait_ge(v, 34)
            dve.tensor_scalar(m.tslot[:], m.texp[:], 1, None, ALU.bitwise_and).then_inc(v, 1)
            for b in range(B):
                dve.wait_ge(xt, 7 + b + 1)
                dve.tensor_tensor(m.vx[:, b, :], pt[2 + b][0:LC, :], xbv[0:LC, :], ALU.add).then_inc(v, 1)
            dve.tensor_copy(m.ident_r[:], m.ident[:])
            dve.tensor_scalar(m.bqs[:], m.bq[:], QSCALE, None, ALU.mult)
            dve.wait_ge(tab_turned, 1)
            dve.tensor_copy(m.t1[:], pq[:, 0:BAND]).then_inc(v, 1)
            dve.wait_ge(tab_turned, 2)
            dve.tensor_copy(m.t2hi[:], pt[0][:, 0:BAND]).then_inc(v, 1)
            dve.wait_ge(v, 39)
            dve.tensor_tensor(m.t2lo[:], pt[0][:, 0:BAND], m.t2hi[:].bitcast(F32), ALU.subtract)

        @block.tensor
        def _(pe):
            pe.wait_ge(const_done, 9)
            pe.wait_ge(v, 1)
            n = 0
            for w in range(5):
                pe.wait_ge(raw_in[w % 2], 16 * (w // 2 + 1))
                for k in range(KD):
                    if n >= 4:
                        pe.wait_ge(lo_done if n - 4 < 16 else hi_done, n - 3)
                    for o in range(KD):
                        ins = pe.transpose(pt[n % 4][:, o * P:(o + 1) * P], raw[w % 2][:, o, k * P:(k + 1) * P],
                                           m.ident[:])
                    ins.then_inc(turned, 1)
                    n += 1
            pe.wait_ge(v, V_OH)
            ohf = oh[:].rearrange("p e c -> p (e c)")
            pe.matmul(pr[:, 0:NE * NCOL], tri[:], ohf, start=True, stop=True).then_inc(rank_done, 1)
            pe.matmul(pq[:, 0:NE * NCOL], m.ones[:, 0:P], ohf, start=True, stop=True).then_inc(rank_done, 1)
            pe.wait_ge(xw_in, 48)
            pe.wait_ge(hi_done, 20)
            for b in range(B):
                for k in range(KD):
                    ins = pe.transpose(pt[b][:, k * LC:(k + 1) * LC], cx[:, b, k * P:(k + 1) * P],
                                       m.ident[0:LC, 0:LC])
                ins.then_inc(xt, 1)
            for b in range(B):
                pe.wait_ge(xe, b + 1)
                for o in range(KD):
                    for k in range(KD):
                        ins = pe.matmul(pt[2 + b][:, o * LC:(o + 1) * LC], xk_w[:, k, o * P:(o + 1) * P],
                                        cxT[:, b, k, :], start=(k == 0), stop=(k == KD - 1))
                ins.then_inc(xt, 1)
            for b in range(B):
                pe.wait_ge(xe, 2 + KD * (b + 1))
                for i in range(KD):
                    for o in range(KD):
                        ins = pe.matmul(pt[b][:, i * LC:(i + 1) * LC], xqT[:, o, i * P:(i + 1) * P],
                                        kxT[:, b, o, :], start=(o == 0), stop=(o == KD - 1))
                ins.then_inc(xt, 1)
            pe.wait_ge(v, V_POS)
            for b in range(B):
                for o in range(KD):
                    ins = pe.matmul(pr[0:1, b * LC:(b + 1) * LC], xbq[:, o:o + 1], kxT[:, b, o, :],
                                    start=(o == 0), stop=(o == KD - 1))
            ins.then_inc(xt, 1)
            for b in range(B):
                for k in range(KD):
                    ins = pe.matmul(pt[2 + b][0:LC, :], cxT[:, b, k, :], xv_w[:, k, :],
                                    start=(k == 0), stop=(k == KD - 1))
                ins.then_inc(xt, 1)
            pe.wait_ge(tab_in, 16)
            pe.matmul(pq[:, 0:BAND], anti[:], hank[:], start=True, stop=True).then_inc(tab_turned, 1)
            pe.wait_ge(v, 38)
            pe.wait_ge(xe, 2 + KD * B + 2)
            for a in range(BAND // P):
                ins = pe.transpose(pt[0][:, a * P:(a + 1) * P], m.t1[:, BAND - (a + 1) * P:BAND - a * P], m.ident[:])
            ins.then_inc(tab_turned, 1)


def stage_project(nc, d, m):
    xr = d["x"].rearrange("b (n t p) c -> (b n) p t c", t=G, p=P)
    with ExitStack() as c:
        def sb(name, shape, dt=F32):
            return c.enter_context(nc.sbuf_tensor(name, shape, dt))

        def sem(name):
            return c.enter_context(nc.semaphore(name))

        xg = [sb(f"xg{i}", [P, G, D]) for i in range(2)]
        xh = [sb(f"xh{i}", [P, KD, GT], F32R) for i in range(2)]
        xl = [sb(f"xl{i}", [P, KD, GT], F32R) for i in range(2)]
        qf = [sb(f"qf{i}", [P, GT]) for i in range(2)]
        qh = [sb(f"qh{i}", [P, GT], F32R) for i in range(2)]
        ql = [sb(f"ql{i}", [P, GT], F32R) for i in range(2)]
        pt = [c.enter_context(nc.psum_tensor(f"ptp{i}", [P, GT], F32)) for i in range(KD)]
        pm = [c.enter_context(nc.psum_tensor(f"pmp{i}", [P, GT], F32)) for i in range(4)]

        x_in = [sem(f"x_in{i}") for i in range(2)]
        x_turned = sem("x_turned")
        xh_done = sem("xh_done")
        xl_done = sem("xl_done")
        x_read = sem("x_read")
        mm_done = sem("mm_done")
        qf_done = sem("qf_done")
        qh_done = sem("qh_done")
        ql_done = sem("ql_done")
        v_done = sem("v_done")
        part_out = [sem(f"part_out{i}") for i in range(2)]
        block = c.enter_context(nc.Block())
        NQK = 2 * KD
        NMM = NQK + G
        LAST = NG - 2

        @block.sync
        def _(sp):
            for j in range(2):
                sp.sem_inc(part_out[j], 32)
                sp.dma_start(xg[j][:], xr[j]).then_inc(x_in[j], 16)

            def group(n, par, more):
                if more:
                    sp.wait_ge(x_turned, KD * (n + 1))
                    sp.dma_start(xg[par][:], xr[n + 2]).then_inc(x_in[par], 16)
                for j in range(NQK):
                    sp.wait_ge(ql_done, NQK * n + j + 1 + 2)
                    dst = (m.q_d, m.k_d)[j // KD]
                    rows = slice((j % KD) * P, (j % KD + 1) * P)
                    sp.dma_start(dst[0, n, rows, :], qh[j % 2][:].bitcast(F32)).then_inc(part_out[j % 2], 16)
                    sp.dma_start(dst[1, n, rows, :], ql[j % 2][:].bitcast(F32)).then_inc(part_out[j % 2], 16)

            with sp.Fori(0, LAST // 2) as i:
                for par in range(2):
                    group(2 * i + par, par, True)
            for n in range(LAST, NG):
                group(n, n % 2, False)
            for j in range(2):
                sp.wait_ge(part_out[j], 32 * (NQK // 2 * NG + 1))

        @block.scalar
        def _(act):
            def turn(n, par):
                act.wait_ge(x_read, n + 1)
                for k in range(KD):
                    act.wait_ge(x_turned, KD * n + k + 1)
                    act.copy(xh[par][:, k, :], pt[k][:]).then_inc(xh_done, 1)

            def scale(n):
                for j in range(NQK):
                    act.wait_ge(mm_done, (NMM - 1) * n + j + 1)
                    act.wait_ge(ql_done, NQK * n + j + 1)
                    bias = (m.bqs if j < KD else m.bk)[:, j % KD:j % KD + 1]
                    act.activation(qf[j % 2][:], pm[j % 4][:], ACT.Identity, bias=bias,
                                   scale=QSCALE if j < KD else 1.0).then_inc(qf_done, 1)

            turn(0, 0)
            with act.Fori(0, LAST // 2) as i:
                for par in range(2):
                    turn(2 * i + par + 1, 1 - par)
                    scale(2 * i + par)
            turn(NG - 1, 1)
            scale(NG - 2)
            scale(NG - 1)

        @block.vector
        def _(dve):
            dve.sem_inc(ql_done, 2)
            dve.sem_inc(v_done, G)

            def turn(n, par):
                for k in range(KD):
                    dve.wait_ge(xh_done, KD * n + k + 1)
                    dve.tensor_tensor(xl[par][:, k, :], pt[k][:], xh[par][:, k, :].bitcast(F32),
                                      ALU.subtract).then_inc(xl_done, 1)

            def parts(n):
                for j in range(NQK):
                    dve.wait_ge(qf_done, NQK * n + j + 1)
                    dve.wait_ge(part_out[j % 2], 32 * (NQK // 2 * n + j // 2 + 1))
                    dve.tensor_copy(qh[j % 2][:], qf[j % 2][:]).then_inc(qh_done, 1)
                    dve.wait_ge(qh_done, NQK * n + j + 1)
                    dve.tensor_tensor(ql[j % 2][:], qf[j % 2][:], qh[j % 2][:].bitcast(F32),
                                      ALU.subtract).then_inc(ql_done, 1)
                for j in range(G):
                    if j < G - 1:
                        dve.wait_ge(mm_done, (NMM - 1) * n + NQK + j + 1)
                    else:
                        dve.wait_ge(x_read, n + 1 + 2)
                    dve.tensor_tensor(m.v[:, G * n + j, :], pm[j % 4][:], m.bv[:], ALU.add).then_inc(v_done, 1)

            turn(0, 0)
            with dve.Fori(0, LAST // 2) as i:
                for par in range(2):
                    turn(2 * i + par + 1, 1 - par)
                    parts(2 * i + par)
            turn(NG - 1, 1)
            parts(NG - 2)
            parts(NG - 1)

        @block.tensor
        def _(pe):
            pe.sem_inc(x_read, 2)

            def turn(n, par, uses):
                pe.wait_ge(x_in[par], 16 * uses)
                for k in range(KD):
                    if not isinstance(n, int) or n > 0:
                        pe.wait_ge(xl_done, KD * (n - 1) + k + 1)
                    for t in range(G):
                        ins = pe.transpose(pt[k][:, t * P:(t + 1) * P], xg[par][:, t, k * P:(k + 1) * P], m.ident[:])
                    ins.then_inc(x_turned, 1)

            def products(n, par):
                pe.wait_ge(xl_done, KD * (n + 1))
                for j in range(NMM):
                    if j < 4:
                        pe.wait_ge(v_done, G * n + j + 1)
                    else:
                        pe.wait_ge(qf_done, NQK * n + j - 4 + 1)
                    if j < NQK:
                        w, o = (m.wqT, m.wkT)[j // KD], j % KD
                        terms = [(w[a][:, k, o * P:(o + 1) * P], (xh, xl)[b][par][:, k, :])
                                 for a, b in ((0, 0), (0, 1), (1, 0)) for k in range(KD)]
                    else:
                        t = j - NQK
                        terms = [((xh, xl)[b][par][:, k, t * P:(t + 1) * P], m.wvT[a][:, k, :])
                                 for a, b in ((0, 0), (1, 0), (0, 1)) for k in range(KD)]
                    for i, (lhs, rhs) in enumerate(terms):
                        ins = pe.matmul(pm[j % 4][:], lhs, rhs, start=(i == 0), stop=(i == len(terms) - 1))
                    ins.then_inc(mm_done if j < NMM - 1 else x_read, 1)

            turn(0, 0, 1)
            with pe.Fori(0, LAST // 2) as i:
                for par in range(2):
                    turn(2 * i + par + 1, 1 - par, i + 1 + par)
                    products(2 * i + par, par)
            turn(NG - 1, 1, NG // 2)
            products(NG - 2, 0)
            products(NG - 1, 1)


def band_cols(blk, lo, hi):
    a, b = max(lo, P * (blk - 1)), min(hi, P * (blk + 2))
    return (a, b, a - P * (blk - 1)) if a < b else None


def max_pieces(qb, kc):
    lo, hi = 512 * kc, 512 * (kc + 1)
    band = band_cols(qb, lo, hi)
    if band is None:
        return [(0, 512, None)]
    a, b, f = band
    out = [(0, a - lo, None)] if a > lo else []
    out.append((a - lo, b - lo, f))
    return out + ([(b - lo, 512, None)] if b < hi else [])


NPIECE = 8
MAX_UNITS = NB * 4
PAIRS = NB // 2 - 1
DENS = PAIRS + 2


def stage_stack_rows(nc, d, m):
    with ExitStack() as c:
        def sb(name, shape, dt=F32):
            return c.enter_context(nc.sbuf_tensor(name, shape, dt))

        hot = sb("hot", [NSTEP, T])
        far = sb("far", [NSTEP, T])
        one = sb("one", [2, 512], F32R)
        hot_r = sb("hot_r", [NSTEP, T], F32R)
        far_r = [sb(f"far_r{i}", [NSTEP, T], F32R) for i in range(2)]
        shaped = c.enter_context(nc.semaphore("shaped"))
        rows_made = c.enter_context(nc.semaphore("rows_made"))
        rows_in = c.enter_context(nc.semaphore("rows_in"))
        block = c.enter_context(nc.Block())

        @block.gpsimd
        def _(pool):
            pool.memset(hot[:], 1.0).then_inc(shaped, 1)
            pool.memset(far[:], 1.0).then_inc(shaped, 1)
            pool.wait_ge(shaped, 2)
            pool.affine_select(out=hot[:], in_=hot[:], compare_op=ALU.is_ge, fill=0.0, base=0,
                               pattern=[[1, T]], channel_multiplier=-P).then_inc(shaped, 1)
            pool.affine_select(out=far[:], in_=far[:], compare_op=ALU.is_ge, fill=0.0, base=-2 * P,
                               pattern=[[1, T]], channel_multiplier=-P).then_inc(shaped, 1)
            pool.wait_ge(shaped, 4)
            pool.affine_select(out=hot[:], in_=hot[:], compare_op=ALU.is_gt, fill=0.0, base=P,
                               pattern=[[-1, T]], channel_multiplier=P).then_inc(shaped, 1)

        @block.vector
        def _(dve):
            dve.memset(one[:].bitcast(F32), 1.0)
            dve.wait_ge(shaped, 5)
            dve.tensor_copy(hot_r[:], hot[:])
            dve.tensor_scalar(far_r[0][:], far[:], m.dhi[0:NSTEP, :].bitcast(F32), None, ALU.mult)
            dve.tensor_scalar(far_r[1][:], far[:], m.dlo[0:NSTEP, :], None, ALU.mult).then_inc(rows_made, 1)

        @block.sync
        def _(sp):
            sp.wait_ge(rows_made, 1)
            for u in range(4):
                for i in range(2):
                    lo = ROW_STEP + i * NSTEP
                    sp.dma_start(m.qst[u][lo:lo + NSTEP, :].bitcast(F32), hot_r[:].bitcast(F32)).then_inc(rows_in, 16)
                    sp.dma_start(m.kst[u][lo:lo + NSTEP, :].bitcast(F32), far_r[i][:].bitcast(F32)).then_inc(rows_in, 16)
                for n in range(T // 512):
                    sp.dma_start(m.kst[u][ROW_SHIFT:ROWS, n * 512:(n + 1) * 512].bitcast(F32),
                                 one[:].bitcast(F32)).then_inc(rows_in, 16)
            sp.wait_ge(rows_in, 16 * 32)


def stage_attention(nc, d, m):
    with ExitStack() as c:
        def sb(name, shape, dt=F32):
            return c.enter_context(nc.sbuf_tensor(name, shape, dt))

        def sem(name):
            return c.enter_context(nc.semaphore(name))

        m.qst = [sb(f"qst{u}", [P, T], F32R) for u in range(4)]
        m.kst = [sb(f"kst{u}", [P, T], F32R) for u in range(4)]
        stage_stack_rows(nc, d, m)

        prob = [sb(f"prob{i}", [P, T]) for i in range(4)]
        vh = [sb(f"vh{i}", [P, NB, HD]) for i in range(2)]
        acc_s = sb("acc_s", [P, 512])
        sum_s = sb("sum_s", [P, 512])
        cxo = [sb(f"cxo{i}", [P, 16, 32]) for i in range(2)]
        pieces = sb("pieces", [P, NB, NPIECE])
        junk = [sb(f"junk{i}", [P, BAND]) for i in range(2)]
        mq = sb("mq", [P, NB])
        mfull = sb("mfull", [P, NB])
        shift = sb("shift", [P, NB])
        sh_hi = sb("sh_hi", [NB, P], F32R)
        sh_lo = sb("sh_lo", [NB, P], F32R)

        st = [c.enter_context(nc.psum_tensor(f"st{i}", [P, 1024], F32)) for i in range(2)]
        mx = [c.enter_context(nc.psum_tensor(f"mx{i}", [P, 512], F32)) for i in range(2)]
        acc = c.enter_context(nc.psum_tensor("acc", [P, 512], F32))
        den = c.enter_context(nc.psum_tensor("den", [P, 512], F32))

        stack_in = [sem(f"stack_in{u}") for u in range(4)]
        shift_in = sem("shift_in")
        v_copied = sem("v_copied")
        s_done = [sem(f"s_done{i}") for i in range(2)]
        e_done = [sem(f"e_done{i}") for i in range(2)]
        pv_done = sem("pv_done")
        paired = sem("paired")
        den_done = sem("den_done")
        acc_taken = sem("acc_taken")
        mx_done = [sem(f"mx_done{i}") for i in range(2)]
        mx_taken = [sem(f"mx_taken{i}") for i in range(2)]
        m_chain = sem("m_chain")
        shift_done = sem("shift_done")
        turned = sem("sh_turned")
        sh_own = sem("sh_own")
        rec_done = sem("rec_done")
        norm_done = sem("norm_done")
        ctx_out = [sem(f"ctx_out{i}") for i in range(2)]
        block = c.enter_context(nc.Block())

        CTX_INC = 16 * 16
        LOOPS = NH // 4 - 1
        USES = (MAX_UNITS // 2 + 1, MAX_UNITS // 2)

        def four_heads(eng, body):
            with eng.Fori(0, LOOPS) as i:
                for u in range(4):
                    body(4 * i + u, i, u, False)
            for u in range(4):
                body(4 * LOOPS + u, LOOPS, u, u == 3)

        @block.sync
        def _(sp):
            def load_stacks(h, batch, u):
                for r, (q, k) in enumerate(((0, 0), (1, 0), (0, 1))):
                    for src, part, dst in ((m.q_d, q, m.qst), (m.k_d, k, m.kst)):
                        rows = src[part].rearrange("(b n) (h r) t -> b h r n t", b=B, r=HD)
                        sp.dma_start(dst[u][r * HD:(r + 1) * HD, :].bitcast(F32).rearrange("r (n t) -> r n t", t=GT),
                                     rows[batch, h]).then_inc(stack_in[u], 16)

            for u in range(4):
                load_stacks(u // B, u % B, u)
            for i in range(2):
                sp.sem_inc(ctx_out[i], CTX_INC + 16)
            sp.wait_ge(mx_taken[0], USES[0] + 1)
            sp.dma_start(m.qst[0][ROW_SHIFT:ROW_SHIFT + 1, :].bitcast(F32), sh_hi[:].bitcast(F32)).then_inc(shift_in, 16)
            sp.dma_start(m.qst[0][ROW_SHIFT + 1:ROWS, :].bitcast(F32), sh_lo[:].bitcast(F32)).then_inc(shift_in, 16)

            def head(hh, i, u, last):
                if not last:
                    sp.wait_ge(mx_taken[0], USES[0] * (hh + 2) + 1)
                    nxt = m.qst[(u + 1) % 4]
                    sp.dma_start(nxt[ROW_SHIFT:ROW_SHIFT + 1, :].bitcast(F32), sh_hi[:].bitcast(F32)).then_inc(shift_in, 16)
                    sp.dma_start(nxt[ROW_SHIFT + 1:ROWS, :].bitcast(F32), sh_lo[:].bitcast(F32)).then_inc(shift_in, 16)
                if not isinstance(hh, int):
                    sp.wait_ge(s_done[1], NB * (hh + 1))
                    load_stacks(i * 2 + (u // B + 2), u % B, u)
                sp.wait_ge(norm_done, hh + 1 + 1)
                dst = m.ctx_d[hh].rearrange("(jm d) (jk g i) -> g d jk jm i", d=HD, jk=KD, g=4)
                src = cxo[u % 2]
                for g in range(4):
                    for jm in range(4):
                        sp.dma_start(dst[g, :, :, jm], src[g * HD:(g + 1) * HD, jm::4, :]).then_inc(ctx_out[u % 2], 16)

            four_heads(sp, head)
            for i in range(2):
                sp.wait_ge(ctx_out[i], CTX_INC * (NH // 2 + 1) + 16)

        @block.gpsimd
        def _(pool):
            def copy_v(h, batch, par):
                src = m.v[:, batch * NB:(batch + 1) * NB, :].rearrange("p b (h e) -> p b h e", e=HD)
                pool.tensor_copy(vh[par][:], src[:, :, h, :]).then_inc(v_copied, 1)

            copy_v(0, 0, 0)

            def normalise(hh, i, u):
                pool.wait_ge(acc_taken, hh + 1)
                pool.wait_ge(rec_done, hh + 1)
                pool.wait_ge(ctx_out[(u + 1) % 2], CTX_INC * (i * 2 + (u - 1) // 2 + 1) + 16)
                out = cxo[(u + 1) % 2][:].rearrange("p j i -> p i j")
                pool.tensor_tensor(out, acc_s[:].rearrange("p (i j) -> p i j", j=16),
                                   sum_s[:].rearrange("p (i j) -> p i j", j=16), ALU.mult).then_inc(norm_done, 1)

            def head(hh, i, u, last):
                for pair in range(PAIRS):
                    even, odd = prob[2 * pair % 4], prob[(2 * pair + 1) % 4]
                    for half in range(2):
                        pool.wait_ge(e_done[half], NB * hh + 2 * pair + 3)
                    pool.wait_ge(pv_done, NB * hh + 2 * pair + 1)
                    pool.tensor_tensor(even[:], even[:], odd[:], ALU.add).then_inc(paired, 1)
                    if pair == 0:
                        normalise(hh, i, u)
                    if pair == 1 and not last:
                        nu = u + 1
                        copy_v(i * 2 + nu // B, nu % B, nu % 2)

            four_heads(pool, head)
            normalise(NH, LOOPS, 4)

        @block.scalar
        def _(act):
            for i in range(2):
                act.sem_inc(e_done[i], 1)

            def head(hh, i, u, last):
                for kb in range(NB):
                    if kb < 4:
                        act.wait_ge(den_done, DENS * hh + (PAIRS, PAIRS, PAIRS + 1, DENS)[kb])
                    else:
                        act.wait_ge(den_done, DENS * (hh + 1) + kb // 2 - 1)
                    for half in range(2):
                        act.wait_ge(s_done[half], NB * hh + kb + 1)
                        act.activation(prob[kb % 4][:, half * 1024:(half + 1) * 1024], st[half][:],
                                       ACT.Exp).then_inc(e_done[half], 1)

            four_heads(act, head)

        @block.vector
        def _(dve):
            for i in range(2):
                dve.sem_inc(mx_taken[i], 1)
            dve.memset(sum_s[:], 1.0)
            dve.memset(acc_s[:], 0.0)
            dve.memset(pieces[:], -3.0e38).then_inc(acc_taken, 1)
            dve.wait_ge(acc_taken, 1)

            def invert(piece):
                part = sum_s[:, piece * P:(piece + 1) * P]
                ins = dve.reciprocal(part, part)
                if piece == 3:
                    ins.then_inc(rec_done, 1)

            def maxima(hh, beside=()):
                slot = [0] * NB
                n_band = 0
                for unit in range(MAX_UNITS):
                    qb, kc, bank = unit // 4, unit % 4, unit % 2
                    scored = MAX_UNITS // 2 * hh + unit // 2 + 1
                    dve.wait_ge(mx_done[bank], scored)
                    cuts = sorted(max_pieces(qb, kc), key=lambda piece: piece[2] is not None)
                    for a, b, f in cuts:
                        out = pieces[:, qb, slot[qb]:slot[qb] + 1]
                        slot[qb] += 1
                        if f is None:
                            ins = dve.tensor_reduce(out, mx[bank][:, a:b], AX.X, ALU.max)
                        else:
                            ins = dve.tensor_tensor_reduce(junk[bank][:, 0:b - a], mx[bank][:, a:b],
                                                           m.t1[:, f:f + b - a], 1.0, -3.0e38, ALU.add, ALU.max, out)
                    ins.then_inc(mx_taken[bank], 1)
                    if unit in beside:
                        invert(beside.index(unit))
                assert max(slot) <= NPIECE
                for bank in range(2):
                    dve.wait_ge(mx_taken[bank], USES[bank] * hh + MAX_UNITS // 2 + 1)
                dve.tensor_reduce(mq[:], pieces[:], AX.X, ALU.max).then_inc(m_chain, 1)
                dve.wait_ge(m_chain, 2 * hh + 1)
                dve.tensor_scalar(mfull[:], mq[:], m.c0[:, 0:1], None, ALU.add).then_inc(m_chain, 1)
                dve.wait_ge(m_chain, 2 * hh + 2)
                dve.tensor_scalar(shift[:], mfull[:], -1.0, m.c0[:, 0:1], ALU.mult, ALU.add).then_inc(shift_done, 1)
                dve.wait_ge(turned, hh + 1)
                if not isinstance(hh, int) or hh > 0:
                    dve.wait_ge(shift_in, 32 * hh)
                dve.tensor_copy(sh_hi[:], mx[0][0:NB, 0:P]).then_inc(sh_own, 1)
                dve.wait_ge(sh_own, hh + 1)
                dve.tensor_tensor(sh_lo[:], mx[0][0:NB, 0:P], sh_hi[:].bitcast(F32), ALU.subtract).then_inc(mx_taken[0], 1)

            def take(hh):
                dve.wait_ge(den_done, DENS * (hh + 2))
                dve.wait_ge(norm_done, hh + 1)
                dve.tensor_copy(acc_s[:], acc[:])
                dve.tensor_copy(sum_s[:], den[:]).then_inc(acc_taken, 1)

            maxima(0)

            def head(hh, i, u, last):
                dve.wait_ge(acc_taken, hh + 1)
                if not last:
                    maxima(hh + 1, (1, 4, 7, 10))
                else:
                    for piece in range(4):
                        invert(piece)
                take(hh)

            four_heads(dve, head)
            dve.wait_ge(acc_taken, NH + 1)
            for piece in range(4):
                invert(piece)

        @block.tensor
        def _(pe):
            pe.sem_inc(den_done, DENS)

            def max_unit(hh, u, unit):
                qb, kc, bank = unit // 4, unit % 4, unit % 2
                pe.wait_ge(mx_taken[bank], USES[bank] * hh + unit // 2 + 1)
                pe.matmul(mx[bank][:], m.qst[u][0:ROW_SHIFT, qb * P:(qb + 1) * P],
                          m.kst[u][0:ROW_SHIFT, kc * 512:(kc + 1) * 512], start=True, stop=True)\
                    .then_inc(mx_done[bank], 1)

            def turn_shift(hh):
                pe.wait_ge(shift_done, hh + 1)
                pe.wait_ge(mx_taken[0], USES[0] * hh + MAX_UNITS // 2 + 1)
                pe.transpose(mx[0][0:NB, 0:P], shift[:], m.ident[:]).then_inc(turned, 1)

            def scores(hh, u, kb, half):
                pe.wait_ge(e_done[half], NB * hh + kb + 1)
                for n in range(2):
                    q0 = half * 1024 + n * 512
                    band = band_cols(kb, q0, q0 + 512)
                    ins = pe.matmul(st[half][:, n * 512:(n + 1) * 512], m.kst[u][0:ROWS, kb * P:(kb + 1) * P],
                                    m.qst[u][0:ROWS, q0:q0 + 512], start=True, stop=band is None)
                    if band:
                        a, b, f = band
                        o = a - half * 1024
                        for part in (m.t2hi, m.t2lo):
                            ins = pe.matmul(st[half][:, o:o + b - a], m.ident_r[:], part[:, f:f + b - a],
                                            start=False, stop=part is m.t2lo)
                ins.then_inc(s_done[half], 1)

            def values(hh, par, kb):
                for half in range(2):
                    pe.wait_ge(e_done[half], NB * hh + kb + 2)
                if kb == 0:
                    pe.wait_ge(acc_taken, hh + 1)
                for g in range(4):
                    ins = pe.matmul(acc[g * HD:(g + 1) * HD, :], vh[par][:, kb, :], prob[kb % 4][:, g * 512:(g + 1) * 512],
                                    start=(kb == 0), stop=(kb == NB - 1))
                ins.then_inc(pv_done, 1)

            def row_sums(hh, n):
                if n < PAIRS:
                    pe.wait_ge(paired, PAIRS * hh + n + 1)
                kb = 2 * n if n < PAIRS else PAIRS + n
                for g in range(4):
                    ins = pe.matmul(den[g * HD:(g + 1) * HD, :], m.ones[:, 0:HD], prob[kb % 4][:, g * 512:(g + 1) * 512],
                                    start=(n == 0), stop=(n == DENS - 1))
                ins.then_inc(den_done, 1)

            pe.wait_ge(stack_in[0], 96)
            for unit in range(MAX_UNITS):
                max_unit(0, 0, unit)
            turn_shift(0)

            def head(hh, i, u, last):
                pe.wait_ge(shift_in, 32 * (hh + 1))
                nu = (u + 1) % 4
                if not last:
                    pe.wait_ge(stack_in[nu], 96 * (i + 1 + (u == 3)))
                units = list(range(MAX_UNITS)) if not last else []

                def spread(n):
                    for _ in range(n):
                        if units:
                            max_unit(hh + 1, nu, units.pop(0))

                for kb in range(NB):
                    scores(hh, u, kb, 0)
                    spread(1)
                    scores(hh, u, kb, 1)
                    spread(1)
                    if kb == 0:
                        pe.wait_ge(v_copied, hh + 1)
                        spread(2)
                        continue
                    if kb == NB - 1 and not last:
                        assert not units
                        turn_shift(hh + 1)
                    values(hh, u % 2, kb - 1)
                    spread(2)
                    if kb % 2 == 1 and kb > 1:
                        row_sums(hh, (kb - 3) // 2)
                        spread(1)
                row_sums(hh, PAIRS)
                values(hh, u % 2, NB - 1)
                row_sums(hh, PAIRS + 1)

            four_heads(pe, head)


class Norm:
    def __init__(self, sem, name):
        self.res = sem(name + "_res")
        self.stats = sem(name + "_stats")
        self.aggr = sem(name + "_aggr")
        self.veps = sem(name + "_veps")
        self.rstd = sem(name + "_rstd")
        self.done = sem(name + "_done")


SLOTS = 4
TURNS = NB // SLOTS


def stage_rows(nc, d, m, out):
    with ExitStack() as c:
        def sb(name, shape, dt=F32):
            return c.enter_context(nc.sbuf_tensor(name, shape, dt))

        def sem(name):
            return c.enter_context(nc.semaphore(name))

        def slots(name, shape, dt=F32):
            return [sb(f"{name}{u}", shape, dt) for u in range(SLOTS)]

        bo, fb = sb("bo", [P, D]), sb("fb_r", [P, D])
        half, eps = sb("half", [P, 1]), sb("eps", [P, 1])
        cin, xin = slots("cin", [P, KD, P]), slots("xin", [P, D])
        ch, cl = slots("ch", [P, KD, P], F32R), slots("cl", [P, KD, P], F32R)
        res1, x2, x2T = slots("res1", [P, D]), slots("x2", [P, D]), slots("x2T", [P, KD, P])
        row3 = slots("row3", [P, D])
        stats = [slots(f"stats{k}", [P, 6]) for k in range(3)]
        mean = [slots(f"mean{k}", [P, 2]) for k in range(3)]
        veps = [slots(f"veps{k}", [P, 1]) for k in range(3)]
        rstd = [slots(f"rstd{k}", [P, 1]) for k in range(3)]
        nmax, esum, rsum = slots("nmax", [P, 1]), slots("esum", [P, 1]), slots("rsum", [P, 1])
        ex, exT = slots("pex", [P, LC]), slots("pexT", [LC, P])
        pa = [c.enter_context(nc.psum_tensor(f"pa{u}", [P, 512], F32)) for u in range(SLOTS)]
        pb = [c.enter_context(nc.psum_tensor(f"pb{u}", [P, 512], F32)) for u in range(SLOTS)]

        bias_in = sem("bias_in")
        tile_in = [sem(f"tile_in{u}") for u in range(SLOTS)]
        const_made = sem("const_made")
        cut_hi = sem("cut_hi")
        cut = sem("cut")
        xb_done = sem("xb_done")
        proj_done = sem("proj_done")
        x2_turned = sem("x2_turned")
        x2T_done = sem("x2T_done")
        cs_done = sem("cs_done")
        nmax_done = sem("nmax_done")
        ex_done = sem("ex_done")
        rsum_done = sem("rsum_done")
        ex_turned = sem("ex_turned")
        exT_done = sem("exT_done")
        cv_done = sem("cv_done")
        stored = [sem(f"stored{u}") for u in range(SLOTS)]
        n1, n2, n3 = Norm(sem, "norm1"), Norm(sem, "norm2"), Norm(sem, "norm3")
        block = c.enter_context(nc.Block())
        xrow = d["x"].rearrange("b (n p) c -> (b n) p c", p=P)
        x3row = m.x3_d.rearrange("(n p) c -> n p c", p=P)
        orow = out.rearrange("b (n p) c -> b n p c", p=P)

        def turns(eng, front, both, back):
            front(0)
            with eng.Fori(0, TURNS) as i:
                both(i, 0)
            with eng.Fori(0, TURNS - 1) as i:
                both(i + TURNS, 1)
            back(B * TURNS - 1, 1)

        @block.sync
        def _(sp):
            sp.dma_start(bo[:], bcast_rows(d["L0_attn_bo"])).then_inc(bias_in, 16)
            sp.dma_start(fb[:], bcast_rows(d["L0_ffn_bias"])).then_inc(bias_in, 16)
            for u in range(SLOTS):
                sp.sem_inc(stored[u], 16)

            def load(t):
                for u in range(SLOTS):
                    sp.wait_ge(cut, SLOTS * t + u + 1)
                    sp.wait_ge(n1.res, SLOTS * t + u + 1)
                    sp.dma_start(cin[u][:].rearrange("p k r -> p (k r)"), m.ctx_d[SLOTS * t + u]).then_inc(tile_in[u], 16)
                    sp.dma_start(xin[u][:], xrow[SLOTS * t + u]).then_inc(tile_in[u], 16)

            def store(t, b):
                for u in range(SLOTS):
                    if b == 0:
                        sp.wait_ge(n2.done, SLOTS * t + u + 1)
                        sp.dma_start(x3row[SLOTS * t + u], row3[u][:]).then_inc(stored[u], 16)
                    else:
                        sp.wait_ge(n3.done, SLOTS * (t - TURNS) + u + 1)
                        sp.dma_start(orow[1, SLOTS * (t - TURNS) + u], row3[u][:]).then_inc(stored[u], 16)

            load(0)
            load(1)
            with sp.Fori(0, TURNS) as i:
                load(i + 2)
                store(i, 0)
            with sp.Fori(0, TURNS - 2) as i:
                load(i + TURNS + 2)
                store(i + TURNS, 1)
            for t in range(B * TURNS - 2, B * TURNS):
                store(t, 1)
            for u in range(SLOTS):
                sp.wait_ge(stored[u], 16 * (B * TURNS + 1))

        @block.gpsimd
        def _(pool):
            pool.memset(eps[:], EPS)
            pool.memset(half[:], -0.5).then_inc(const_made, 1)
            pool.wait_ge(const_made, 1)
            pool.wait_ge(bias_in, 32)

            def add_bias(t):
                for u in range(SLOTS):
                    pool.wait_ge(tile_in[u], 32 * (t + 1))
                    pool.tensor_tensor(xin[u][:], xin[u][:], bo[:], ALU.add).then_inc(xb_done, 1)

            def rstds(norm, k, t):
                for u in range(SLOTS):
                    pool.wait_ge(norm.aggr, SLOTS * t + u + 1)
                    pool.tensor_tensor(veps[k][u][:], mean[k][u][:, 1:2], eps[:], ALU.add).then_inc(norm.veps, 1)
                for u in range(SLOTS):
                    pool.wait_ge(norm.veps, SLOTS * t + u + 1)
                    pool.tensor_tensor(rstd[k][u][:], veps[k][u][:], half[:], ALU.pow).then_inc(norm.rstd, 1)

            def front(t):
                add_bias(t)
                rstds(n1, 0, t)

            def both(t, b):
                add_bias(t + 1)
                rstds(n1, 0, t + 1)
                rstds(n2, 1, t)
                if b == 1:
                    rstds(n3, 2, t - TURNS)

            def back(t, b):
                rstds(n2, 1, t)
                rstds(n3, 2, t - TURNS)

            turns(pool, front, both, back)

        @block.scalar
        def _(act):
            def front(t):
                for u in range(SLOTS):
                    act.wait_ge(tile_in[u], 32 * (t + 1))
                    if not isinstance(t, int) or t > 0:
                        act.wait_ge(proj_done, SLOTS * (t - 1) + u + 1)
                    act.copy(ch[u][:], cin[u][:]).then_inc(cut_hi, 1)

            def copy_x2(t):
                for u in range(SLOTS):
                    act.wait_ge(x2_turned, SLOTS * t + u + 1)
                    act.copy(x2T[u][:], pb[u][:].rearrange("p (k r) -> p k r", k=KD)).then_inc(x2T_done, 1)

            def softmax(t):
                for u in range(SLOTS):
                    act.wait_ge(nmax_done, SLOTS * t + u + 1)
                    act.activation(ex[u][:], pb[u][:, 0:LC], ACT.Exp, bias=nmax[u][:, 0:1],
                                   accum_out=esum[u][:]).then_inc(ex_done, 1)
                for u in range(SLOTS):
                    act.wait_ge(ex_turned, SLOTS * t + u + 1)
                    act.copy(exT[u][:], pb[u][0:LC, P:2 * P]).then_inc(exT_done, 1)

            def both(t, b):
                front(t + 1)
                copy_x2(t)
                softmax(t)

            def back(t, b):
                copy_x2(t)
                softmax(t)

            turns(act, front, both, back)

        @block.vector
        def _(dve):
            dve.sem_inc(cut, SLOTS)
            dve.sem_inc(n1.res, SLOTS)
            dve.sem_inc(n2.res, SLOTS)

            def statistics(norm, k, src, t, credit):
                for u in range(SLOTS):
                    dve.wait_ge(norm.res, SLOTS * t + u + 1 + credit)
                    dve.bn_stats(stats[k][u][:], src[u][:]).then_inc(norm.stats, 1)
                for u in range(SLOTS):
                    counted = SLOTS * t + u + 1
                    dve.wait_ge(bias_in, 32)
                    dve.wait_ge(norm.stats, counted)
                    dve.bn_aggr(mean[k][u][:], stats[k][u][:]).then_inc(norm.aggr, 1)

            def apply(norm, k, src, dst, t):
                for u in range(SLOTS):
                    dve.wait_ge(norm.rstd, SLOTS * t + u + 1)
                    if dst is x2:
                        dve.wait_ge(n2.res, SLOTS * t + u + 1)
                    dve.tensor_scalar(dst[u][:], src[u][:], mean[k][u][:, 0:1], rstd[k][u][:, 0:1],
                                      ALU.subtract, ALU.mult).then_inc(norm.done, 1)

            def low_parts(t):
                for u in range(SLOTS):
                    dve.wait_ge(cut_hi, SLOTS * t + u + 1)
                    dve.tensor_tensor(cl[u][:], cin[u][:], ch[u][:].bitcast(F32), ALU.subtract).then_inc(cut, 1)

            def sum1(t):
                for u in range(SLOTS):
                    dve.wait_ge(proj_done, SLOTS * t + u + 1)
                    dve.wait_ge(xb_done, SLOTS * t + u + 1)
                    dve.tensor_tensor(res1[u][:], pa[u][:], xin[u][:], ALU.add).then_inc(n1.res, 1)

            def maxima(t):
                for u in range(SLOTS):
                    dve.wait_ge(cs_done, SLOTS * t + u + 1)
                    dve.tensor_reduce(nmax[u][:], pb[u][:, 0:LC], AX.X, ALU.max, negate=True).then_inc(nmax_done, 1)

            def inverses(t):
                for u in range(SLOTS):
                    dve.wait_ge(ex_done, SLOTS * t + u + 1)
                    dve.reciprocal(rsum[u][:], esum[u][:]).then_inc(rsum_done, 1)

            def sum2(t):
                for u in range(SLOTS):
                    dve.wait_ge(cv_done, SLOTS * t + u + 1)
                    dve.wait_ge(rsum_done, SLOTS * t + u + 1)
                    dve.wait_ge(stored[u], 16 * (t + 1))
                    dve.scalar_tensor_tensor(out=row3[u][:], in0=pb[u][:], scalar=rsum[u][:, 0:1], in1=x2[u][:],
                                             op0=ALU.mult, op1=ALU.add).then_inc(n2.res, 1)

            def last_norm(t):
                for u in range(SLOTS):
                    dve.wait_ge(n2.done, SLOTS * (t + TURNS) + u + 1)
                    dve.tensor_tensor(row3[u][:], row3[u][:], fb[:], ALU.add).then_inc(n3.res, 1)
                statistics(n3, 2, row3, t, 0)
                apply(n3, 2, row3, row3, t)

            def front(t):
                low_parts(t)
                sum1(t)
                statistics(n1, 0, res1, t, SLOTS)
                apply(n1, 0, res1, x2, t)

            def both(t, b):
                low_parts(t + 1)
                maxima(t)
                inverses(t)
                sum1(t + 1)
                statistics(n1, 0, res1, t + 1, SLOTS)
                sum2(t)
                apply(n1, 0, res1, x2, t + 1)
                statistics(n2, 1, row3, t, SLOTS)
                apply(n2, 1, row3, row3, t)
                if b == 1:
                    last_norm(t - TURNS)

            def back(t, b):
                maxima(t)
                inverses(t)
                sum2(t)
                statistics(n2, 1, row3, t, SLOTS)
                apply(n2, 1, row3, row3, t)
                last_norm(t - TURNS)

            dve.wait_ge(bias_in, 32)
            turns(dve, front, both, back)

        @block.tensor
        def _(pe):
            def project(t, tiles):
                for u in tiles:
                    pe.wait_ge(cut, SLOTS * (t + 1) + u + 1)
                    pe.wait_ge(n1.res, SLOTS * t + u + 1)
                    terms = [((ch, cl)[x][u][:, k, :], m.woT[w][:, k, :])
                             for x, w in ((0, 0), (1, 0), (0, 1)) for k in range(KD)]
                    for n, (lhs, rhs) in enumerate(terms):
                        ins = pe.matmul(pa[u][:], lhs, rhs, start=(n == 0), stop=(n == len(terms) - 1))
                    ins.then_inc(proj_done, 1)

            def turn_x2(t):
                for u in range(SLOTS):
                    pe.wait_ge(n1.done, SLOTS * t + u + 1)
                    pe.wait_ge(n2.res, SLOTS * t + u + 1)
                    for k in range(KD):
                        ins = pe.transpose(pb[u][:, k * P:(k + 1) * P], x2[u][:, k * P:(k + 1) * P], m.ident[:])
                    ins.then_inc(x2_turned, 1)

            def cross_scores(t, b):
                for u in range(SLOTS):
                    pe.wait_ge(x2T_done, SLOTS * t + u + 1)
                    pe.matmul(pb[u][:, 0:LC], m.ones[0:1, :], m.g0[:, b, :], start=True, stop=False)
                    for k in range(KD):
                        ins = pe.matmul(pb[u][:, 0:LC], x2T[u][:, k, :], m.g[:, b, k, :], start=False,
                                        stop=(k == KD - 1))
                    ins.then_inc(cs_done, 1)

            def turn_exp(t):
                for u in range(SLOTS):
                    pe.wait_ge(ex_done, SLOTS * t + u + 1)
                    pe.transpose(pb[u][0:LC, P:2 * P], ex[u][:], m.ident[:]).then_inc(ex_turned, 1)

            def cross_values(t, b):
                for u in range(SLOTS):
                    pe.wait_ge(exT_done, SLOTS * t + u + 1)
                    pe.matmul(pb[u][:], exT[u][:], m.vx[:, b, :], start=True, stop=True).then_inc(cv_done, 1)

            def front(t):
                project(t, range(SLOTS))

            def both(t, b):
                turn_x2(t)
                project(t + 1, range(1))
                cross_scores(t, b)
                project(t + 1, range(1, SLOTS - 1))
                turn_exp(t)
                project(t + 1, range(SLOTS - 1, SLOTS))
                cross_values(t, b)

            def back(t, b):
                turn_x2(t)
                cross_scores(t, b)
                turn_exp(t)
                cross_values(t, b)

            turns(pe, front, both, back)


def stage_experts(nc, d, m, out):
    with ExitStack() as c:
        def sb(name, shape, dt=F32):
            return c.enter_context(nc.sbuf_tensor(name, shape, dt))

        def sem(name):
            return c.enter_context(nc.semaphore(name))

        w1 = sb("ew1", [P, 2, KD, FF])
        w2 = sb("ew2", [P, 2, FC, D])
        pick = [sb(f"pick{i}", [P, 1], I32) for i in range(2)]
        xg = [sb(f"exg{i}", [P, D]) for i in range(2)]
        xgT = [sb(f"exgT{i}", [P, KD, P]) for i in range(2)]
        hid = sb("hid", [P, FF])
        hidT = sb("hidT", [P, FC, P])
        yt = [sb(f"yt{i}", [P, D]) for i in range(2)]
        ph = c.enter_context(nc.psum_tensor("ph", [P, FF], F32))
        pt = [c.enter_context(nc.psum_tensor(f"pte{i}", [P, 512], F32)) for i in range(2)]
        py = c.enter_context(nc.psum_tensor("py", [P, 512], F32))
        px = c.enter_context(nc.psum_tensor("px", [P, 512], F32))

        w_in = sem("w_in")
        picked = sem("picked")
        rows_in = [sem(f"rows_in{i}") for i in range(2)]
        x_turned = sem("ex_turned_x")
        xT_done = sem("exT_copied")
        h_done = [sem(f"h_done{j}") for j in range(4)]
        g_done = [sem(f"g_done{j}") for j in range(4)]
        ht_done = sem("ht_done")
        ht_copied = sem("ht_copied")
        y_done = sem("y_done")
        y_copied = sem("y_copied")
        y_out = [sem(f"y_out{i}") for i in range(2)]
        block = c.enter_context(nc.Block())
        PAIRS = NTILE // 2
        w1v = d["L0_ffn_w1"].rearrange("e (k p) f -> e p k f", p=P)
        w2v = d["L0_ffn_w2"].rearrange("e (k p) n -> e p k n", p=P)
        yrow = m.y_d.rearrange("(t p) c -> t p c", p=P)

        def tiles(eng, body):
            with eng.Fori(0, PAIRS) as i:
                for par in range(2):
                    body(2 * i + par, i, par)
            body(NTILE - 1, PAIRS, 0)

        @block.sync
        def _(sp):
            for e in range(NE):
                if e >= 2:
                    first = sp.value_load(m.efirst[0:1, e - 1:e], min_val=1, max_val=NTILE)
                    sp.wait_ge(y_done, first + 1)
                if e >= 1:
                    sp.wait_ge(w_in, 32 * e)
                sp.dma_start(w1[:, e % 2], w1v[e]).then_inc(w_in, 16)
                sp.dma_start(w2[:, e % 2], w2v[e]).then_inc(w_in, 16)

        @block.gpsimd
        def _(pool):
            def body(t, i, par):
                pool.wait_ge(x_turned, t + 1)
                pool.tensor_copy(pick[par][:], m.perm[:, bass.ds(t, 1)]).then_inc(picked, 1)
                pool.wait_ge(picked, 1)
                pool.wait_ge(picked, t + 1)
                pool.indirect_dma_start(xg[par][:], None, m.x3_d, bass.IndirectOffsetOnAxis(pick[par][:], 0))\
                    .then_inc(rows_in[par], 16)

            tiles(pool, body)

        @block.scalar
        def _(act):
            for j in range(4):
                act.sem_inc(g_done[j], 1)
            act.sem_inc(y_copied, 1)
            for i in range(2):
                act.sem_inc(y_out[i], 16)

            def copy_y(t, i, par):
                act.wait_ge(y_done, t + 2)
                act.wait_ge(y_out[par], 16 * (i + 1))
                act.copy(yt[par][:], py[:]).then_inc(y_copied, 1)
                act.wait_ge(y_copied, t + 2)
                act.dma_start(yrow[t], yt[par][:]).then_inc(y_out[par], 16)

            def body(t, i, par):
                for j in range(4):
                    act.wait_ge(h_done[j], t + 1)
                    act.wait_ge(ht_done, 4 * t + j + 1)
                    act.activation(hid[:, j * 512:(j + 1) * 512], ph[:, j * 512:(j + 1) * 512], ACT.Gelu)\
                        .then_inc(g_done[j], 1)
                copy_y(t, i, par)

            tiles(act, body)
            act.wait_ge(y_out[0], 16 * (PAIRS + 2))
            act.wait_ge(y_out[1], 16 * (PAIRS + 1))

        @block.vector
        def _(dve):
            dve.sem_inc(ht_copied, 2)

            def copy_x(t, par):
                dve.wait_ge(x_turned, t + 1 + 2)
                dve.tensor_copy(xgT[par][:], px[:].rearrange("p (k r) -> p k r", k=KD)).then_inc(xT_done, 1)

            copy_x(0, 0)

            def body(t, i, par):
                if not isinstance(t, int):
                    copy_x(t + 1, 1 - par)
                for j in range(4):
                    dve.wait_ge(ht_done, 4 * t + j + 1 + 4)
                    if j == 0:
                        dve.wait_ge(y_done, t + 1)
                    dve.tensor_copy(hidT[:, 4 * j:4 * j + 4, :], pt[j % 2][:].rearrange("p (k r) -> p k r", k=4))\
                        .then_inc(ht_copied, 1)

            tiles(dve, body)

        @block.tensor
        def _(pe):
            pe.sem_inc(x_turned, 2)
            pe.sem_inc(ht_done, 4)
            pe.sem_inc(y_done, 1)

            def turn_x(t, i, par):
                pe.wait_ge(rows_in[par], 16 * (i + 1))
                if not isinstance(t, int) or t > 0:
                    pe.wait_ge(xT_done, t)
                for k in range(KD):
                    ins = pe.transpose(px[:, k * P:(k + 1) * P], xg[par][:, k * P:(k + 1) * P], m.ident[:])
                ins.then_inc(x_turned, 1)

            def up(t, par):
                expert = pe.value_load(m.texp[0:1, bass.ds(t, 1)], min_val=0, max_val=NE - 1)
                slot = pe.value_load(m.tslot[0:1, bass.ds(t, 1)], min_val=0, max_val=1)
                pe.wait_ge(w_in, 32 * expert + 32)
                pe.wait_ge(xT_done, t + 1)
                for j in range(4):
                    pe.wait_ge(g_done[j], t + 1)
                    for k in range(KD):
                        ins = pe.matmul(ph[:, j * 512:(j + 1) * 512], xgT[par][:, k, :],
                                        w1[:, bass.ds(slot, 1), k, j * 512:(j + 1) * 512]
                                        .rearrange("p s f -> p (s f)"), start=(k == 0), stop=(k == KD - 1))
                    ins.then_inc(h_done[j], 1)
                return slot

            def down(t, slot):
                for j in range(4):
                    pe.wait_ge(g_done[j], t + 2)
                    pe.wait_ge(ht_copied, 4 * t + j + 1)
                    for k in range(4):
                        f = 4 * j + k
                        ins = pe.transpose(pt[j % 2][:, k * P:(k + 1) * P], hid[:, f * P:(f + 1) * P], m.ident[:])
                    ins.then_inc(ht_done, 1)
                for j in range(4):
                    pe.wait_ge(ht_copied, 4 * t + j + 1 + 2)
                    if j == 0:
                        pe.wait_ge(y_copied, t + 1)
                    for k in range(4):
                        f = 4 * j + k
                        ins = pe.matmul(py[:], hidT[:, f, :], w2[:, bass.ds(slot, 1), f, :]
                                        .rearrange("p s n -> p (s n)"), start=(f == 0), stop=(f == FC - 1))
                ins.then_inc(y_done, 1)

            turn_x(0, 0, 0)

            def body(t, i, par):
                slot = up(t, par)
                if not isinstance(t, int):
                    turn_x(t + 1, i + par, 1 - par)
                down(t, slot)

            tiles(pe, body)

    stage_combine(nc, d, m, out)


def stage_combine(nc, d, m, out):
    with ExitStack() as c:
        def sb(name, shape, dt=F32):
            return c.enter_context(nc.sbuf_tensor(name, shape, dt))

        def sem(name):
            return c.enter_context(nc.semaphore(name))

        N = NTOK // P
        fb = sb("fb_c", [P, D])
        half = sb("half_c", [P, 1])
        veps = [sb(f"cveps{i}", [P, 1]) for i in range(2)]
        x3 = sb("x3c", [P, N, D])
        yg = [[sb(f"yg{i}{j}", [P, D]) for j in range(TOPK)] for i in range(4)]
        s1 = [sb(f"s1_{i}", [P, D]) for i in range(2)]
        s2 = [sb(f"s2_{i}", [P, D]) for i in range(2)]
        xs = [sb(f"xs_{i}", [P, D]) for i in range(2)]
        stats = [sb(f"cst{i}", [P, 6]) for i in range(2)]
        mean = [sb(f"cmean{i}", [P, 2]) for i in range(2)]
        rstd = [sb(f"crstd{i}", [P, 1]) for i in range(2)]
        fin = [sb(f"cfin{i}", [P, D]) for i in range(2)]
        own_in = sem("own_in")
        y_in = [sem(f"y_in{i}") for i in range(4)]
        xs_done = sem("xs_done")
        sum_chain = sem("sum_chain")
        c_aggr = sem("c_aggr")
        c_veps = sem("c_veps")
        c_rstd = sem("c_rstd")
        fin_done = sem("fin_done")
        fin_out = [sem(f"fin_out{i}") for i in range(2)]
        block = c.enter_context(nc.Block())
        orow = out.rearrange("b (n p) c -> b n p c", p=P)

        @block.sync
        def _(sp):
            sp.dma_start(fb[:], bcast_rows(d["L0_ffn_bias"])).then_inc(own_in, 16)
            sp.dma_start(x3[:], m.x3_d.rearrange("(n p) c -> p n c", p=P)).then_inc(own_in, 16)
            for n in range(N):
                sp.wait_ge(fin_done, n + 1)
                sp.dma_start(orow[0, n], fin[n % 2][:]).then_inc(fin_out[n % 2], 16)
            for i in range(2):
                sp.wait_ge(fin_out[i], 16 * (N // 2))

        @block.gpsimd
        def _(pool):
            def gather(n):
                for j in range(TOPK):
                    pool.indirect_dma_start(yg[n % 4][j][:], None, m.y_d,
                                            bass.IndirectOffsetOnAxis(m.pos[:, TOPK * n + j:TOPK * n + j + 1], 0))\
                        .then_inc(y_in[n % 4], 16)

            pool.memset(half[:], -0.5).then_inc(c_veps, 1)
            for n in range(4):
                gather(n)
            for n in range(N):
                pool.wait_ge(c_aggr, n + 1)
                pool.tensor_scalar(veps[n % 2][:], mean[n % 2][:, 1:2], EPS, None, ALU.add).then_inc(c_veps, 1)
                pool.wait_ge(c_veps, n + 2)
                pool.tensor_tensor(rstd[n % 2][:], veps[n % 2][:], half[:], ALU.pow).then_inc(c_rstd, 1)
                if n + 4 < N:
                    gather(n + 4)

        @block.vector
        def _(dve):
            dve.wait_ge(own_in, 32)
            for n in range(N):
                i = n % 2
                dve.tensor_tensor(xs[i][:], x3[:, n, :], fb[:], ALU.add).then_inc(xs_done, 1)
                dve.wait_ge(y_in[n % 4], 32 * (n // 4 + 1))
                dve.wait_ge(xs_done, n + 1)
                dve.scalar_tensor_tensor(out=s1[i][:], in0=yg[n % 4][0][:], scalar=m.tokw[:, TOPK * n:TOPK * n + 1],
                                         in1=xs[i][:], op0=ALU.mult, op1=ALU.add).then_inc(sum_chain, 1)
                dve.wait_ge(sum_chain, 3 * n + 1)
                dve.scalar_tensor_tensor(out=s2[i][:], in0=yg[n % 4][1][:],
                                         scalar=m.tokw[:, TOPK * n + 1:TOPK * n + 2],
                                         in1=s1[i][:], op0=ALU.mult, op1=ALU.add).then_inc(sum_chain, 1)
                dve.wait_ge(sum_chain, 3 * n + 2)
                dve.bn_stats(stats[i][:], s2[i][:]).then_inc(sum_chain, 1)
                dve.wait_ge(sum_chain, 3 * n + 3)
                dve.bn_aggr(mean[i][:], stats[i][:]).then_inc(c_aggr, 1)
                dve.wait_ge(c_rstd, n + 1)
                if n >= 2:
                    dve.wait_ge(fin_out[i], 16 * (n // 2))
                dve.tensor_scalar(fin[i][:], s2[i][:], mean[i][:, 0:1], rstd[i][:, 0:1],
                                  ALU.subtract, ALU.mult).then_inc(fin_done, 1)



def build(nc, d, out):
    m = Mem()
    m.ext_t = nc.dram_tensor("ext_scr", [1, 512], F32)
    m.ext_d = m.ext_t.ap()
    m.perm_d = nc.dram_tensor("perm_scr", [NTILE * P, 1], I32).ap()
    m.q_d = nc.dram_tensor("q_scr", [2, NG, D, GT], F32).ap()
    m.k_d = nc.dram_tensor("k_scr", [2, NG, D, GT], F32).ap()
    m.ctx_d = nc.dram_tensor("ctx_scr", [NH, P, KD * P], F32).ap()
    m.x3_d = nc.dram_tensor("x3_scr", [NTOK, D], F32).ap()
    m.y_d = nc.dram_tensor("y_scr", [NTILE * P, D], F32).ap()
    with ExitStack() as c:
        def sb(name, shape, dt=F32):
            return c.enter_context(nc.sbuf_tensor(name, shape, dt))

        m.ident = sb("ident", [P, P])
        m.ident_r = sb("ident_r", [P, P], F32R)
        m.ones = sb("ones", [P, P])
        m.bq, m.bqs, m.bk = sb("bq", [P, KD]), sb("bqs", [P, KD]), sb("bk", [P, KD])
        m.c0 = sb("c0", [P, 1])
        m.dhi, m.dlo = sb("dhi", [P, 1], F32R), sb("dlo", [P, 1])
        m.t1 = sb("t1", [P, BAND])
        m.t2hi, m.t2lo = sb("t2hi", [P, BAND], F32R), sb("t2lo", [P, BAND], F32R)
        m.woT = [sb(f"woT{i}", [P, KD, D], F32R) for i in range(2)]
        m.g, m.g0, m.vx = sb("g", [P, B, KD, LC]), sb("g0", [1, B, LC]), sb("vx", [LC, B, D])
        m.pos, m.perm = sb("pos", [P, NCOL], I32), sb("perm", [P, NTILE], I32)
        m.tokw = sb("tokw", [P, NCOL])
        m.texp, m.tslot, m.efirst = sb("texp", [1, NTILE], I32), sb("tslot", [1, NTILE], I32), sb("efirst", [1, NE], I32)
        with nc.sbuf_tensor("v", [P, NROW // P, D], F32) as m.v:
            with ExitStack() as cw:
                m.bv = cw.enter_context(nc.sbuf_tensor("bv", [P, D], F32))

                def parts(name):
                    return [cw.enter_context(nc.sbuf_tensor(f"{name}{i}", [P, KD, D], F32R)) for i in range(2)]

                m.wqT, m.wkT, m.wvT = parts("wqT"), parts("wkT"), parts("wvT")
                stage_setup(nc, d, m)
                stage_project(nc, d, m)
            stage_attention(nc, d, m)
        stage_rows(nc, d, m, out)
        stage_experts(nc, d, m, out)


INPUTS = ["x", "ctx_1024", "L0_attn_Wq", "L0_attn_bq", "L0_attn_Wk", "L0_attn_bk", "L0_attn_Wv", "L0_attn_bv",
          "L0_attn_Wo", "L0_attn_bo", "L0_attn_et_gate", "L0_attn_is_gate", "L0_attn_time_bias", "L0_xattn_Wq",
          "L0_xattn_bq", "L0_xattn_Wk", "L0_xattn_bk", "L0_xattn_Wv", "L0_xattn_bv", "L0_ffn_expert_weights",
          "L0_ffn_expert_indices", "L0_ffn_w1", "L0_ffn_w2", "L0_ffn_bias"]


def kernel(**inputs):
    import numpy as _np
    import concourse.bacc as _bacc
    from concourse import mybir as _mybir
    from concourse.bass_utils import run_bass_kernel_spmd as _run

    nc = _bacc.Bacc("TRN2", target_bir_lowering=False, num_devices=1)
    arrays, d = {}, {}
    for name in INPUTS:
        a = _np.ascontiguousarray(inputs[name])
        arrays[f"in_{name}"] = a
        d[name] = nc.dram_tensor(f"in_{name}", a.shape, _mybir.dt.from_np(a.dtype), kind="ExternalInput").ap()
    out = nc.dram_tensor("out_rows", (B, T, D), F32, kind="ExternalOutput").ap()
    build(nc, d, out)
    r = _run(nc, [arrays], core_ids=[0])
    return r.results[0]["out_rows"]
```

```python
from contextlib import ExitStack

import concourse.bass as bass
from concourse import mybir

F32 = mybir.dt.float32
F32R = mybir.dt.float32r
I32 = mybir.dt.int32
ALU = mybir.AluOpType
ACT = mybir.ActivationFunctionType
AX = mybir.AxisListType

P = 128
B, T, D = 2, 2048, 512
H = 16
HD = D // H
NROW = B * T
KD = D // P
NB = T // P
NH = B * H
TB_LEN = 250
TB_MID = TB_LEN // 2
EPS = 1e-5
QSCALE = 1.0 / float(HD) ** 0.5
XSCALE = 1.0 / float(D) ** 0.5
LC = 77
NE, FF = 8, 2048
FC = FF // P
NTOK = 2048
TOPK = 2
NCOL = NTOK // P * TOPK
NTILE = (NTOK * TOPK) // P + NE - 1

NSTEP = NB - 2
ROW_STEP = 3 * HD
ROW_SHIFT = ROW_STEP + 2 * NSTEP
ROWS = ROW_SHIFT + 2
BAND = 3 * P


G = 4
GT = G * P
NG = NROW // GT


class Mem:
    pass


def bcast_rows(ap, n=P):
    return ap.partition_broadcast(n)


def stage_setup(nc, d, m):
    with ExitStack() as c:
        def sb(name, shape, dt=F32):
            return c.enter_context(nc.sbuf_tensor(name, shape, dt))

        def sem(name):
            return c.enter_context(nc.semaphore(name))

        weights = [("wq", d["L0_attn_Wq"]), ("wk", d["L0_attn_Wk"]), ("wv", d["L0_attn_Wv"]), ("wo", d["L0_attn_Wo"]),
                   ("xq", d["L0_xattn_Wq"])]
        raw = [m.v[:, i * KD:(i + 1) * KD, :] for i in range(2)]
        xqT, xk_w, xv_w = (m.v[:, i * KD:(i + 1) * KD, :] for i in (2, 3, 4))
        cx = sb("cx", [LC, B, D])
        cxT = sb("cxT", [P, B, KD, LC])
        kxT = sb("kxT", [P, B, KD, LC])
        xbk = sb("xbk", [P, KD])
        xbq = sb("xbq", [P, KD])
        xbv = sb("xbv", [P, D])
        tb0 = sb("tb0", [P, 1])
        tbl = sb("tbl", [P, 1])
        gates = sb("gates", [P, 2])
        eneg = sb("eneg", [P, 1])
        epl = sb("epl", [P, 1])
        sig = sb("sig", [P, 1])
        dstep = sb("dstep", [P, 1])
        dfar = sb("dfar", [P, 1])
        trow = sb("trow", [1, TB_LEN])
        ext = sb("ext", [1, 512])
        hank = sb("hank", [P, BAND])
        anti = sb("anti", [P, P])
        ei = sb("ei", [P, NCOL], I32)
        ef = sb("ef", [P, NCOL])
        oh = sb("oh", [P, NE, NCOL])
        tri = sb("tri", [P, P])
        tot = sb("tot", [P, NE, NCOL])
        sc = [sb(f"sc{i}", [P, NE, NCOL]) for i in range(5)]
        w1 = sb("w_1", [P, NE, NCOL])
        w2 = sb("w_2", [P, NE, NCOL])
        w3 = sb("w_3", [P, NE, NCOL])
        w4 = sb("w_4", [P, NE, NCOL])
        posf = sb("posf", [P, NCOL])
        cntf = sb("cntf", [P, NE])
        cnti = sb("cnti", [P, NE], I32)
        cntj = sb("cntj", [P, NE], I32)
        pad = sb("pad", [P, NE])
        ps1 = sb("ps1", [P, NE])
        ps2 = sb("ps2", [P, NE])
        ps3 = sb("ps3", [P, NE])
        base = sb("base", [P, NE])
        tio = sb("tio", [1, NTILE])
        tacc = [sb(f"tacc{i}", [1, NTILE]) for i in range(2)]
        zero = sb("zero", [P, D])

        pt = [c.enter_context(nc.psum_tensor(f"pt{i}", [P, 512], F32)) for i in range(4)]
        pr = c.enter_context(nc.psum_tensor("pr", [P, 512], F32))
        pq = c.enter_context(nc.psum_tensor("pq", [P, 512], F32))

        raw_in = [sem(f"raw_in{i}") for i in range(2)]
        small_in = sem("small_in")
        xw_in = sem("xw_in")
        turned = sem("turned")
        hi_done = sem("hi_done")
        lo_done = sem("lo_done")
        const_done = sem("const_done")
        v = sem("v_chain")
        eneg_done = sem("eneg_done")
        ext_out = sem("ext_out")
        tab_in = sem("tab_in")
        fill_out = sem("fill_out")
        rank_done = sem("rank_done")
        xt = sem("xt")
        tab_turned = sem("tab_turned")
        xe = sem("xe")
        block = c.enter_context(nc.Block())

        V_EXT, V_OH, V_POS = 9, 15, 33
        wT = {"wq": m.wqT, "wk": m.wkT, "wv": m.wvT, "wo": m.woT}

        @block.sync
        def _(sp):
            for n in range(2):
                sp.dma_start(raw[n], weights[n][1].rearrange("(o p) i -> p o i", p=P)).then_inc(raw_in[n], 16)
            with nc.allow_non_contiguous_dma("small vectors"):
                sp.dma_start(m.bq[:], d["L0_attn_bq"].rearrange("(m p) -> p m", p=P)).then_inc(small_in, 16)
                sp.dma_start(m.bk[:], d["L0_attn_bk"].rearrange("(m p) -> p m", p=P)).then_inc(small_in, 16)
                sp.dma_start(xbk[:], d["L0_xattn_bk"].rearrange("(m p) -> p m", p=P)).then_inc(small_in, 16)
                sp.dma_start(xbq[:], d["L0_xattn_bq"].rearrange("(m p) -> p m", p=P)).then_inc(small_in, 16)
                tb = d["L0_attn_time_bias"][0, 0]
                sp.dma_start(tb0[:], bcast_rows(tb[0:1])).then_inc(small_in, 16)
                sp.dma_start(tbl[:], bcast_rows(tb[TB_LEN - 1:TB_LEN])).then_inc(small_in, 16)
                sp.dma_start(gates[:, 0:1], bcast_rows(d["L0_attn_et_gate"][0, 0])).then_inc(small_in, 16)
                sp.dma_start(gates[:, 1:2], bcast_rows(d["L0_attn_is_gate"][0, 0])).then_inc(small_in, 16)
                sp.dma_start(ei[:].rearrange("p (c j) -> p c j", j=TOPK),
                             d["L0_ffn_expert_indices"].rearrange("(c p) j -> p c j", p=P)).then_inc(small_in, 16)
                sp.dma_start(m.tokw[:].rearrange("p (c j) -> p c j", j=TOPK),
                             d["L0_ffn_expert_weights"].rearrange("(c p) j -> p c j", p=P)).then_inc(small_in, 16)
            sp.dma_start(trow[:], d["L0_attn_time_bias"][0]).then_inc(small_in, 16)
            sp.dma_start(m.bv[:], bcast_rows(d["L0_attn_bv"])).then_inc(small_in, 16)
            sp.dma_start(xbv[:], bcast_rows(d["L0_xattn_bv"])).then_inc(small_in, 16)
            sp.dma_start(cx[:], d["ctx_1024"].rearrange("b t c -> t b c")).then_inc(xw_in, 16)
            sp.dma_start(xk_w, d["L0_xattn_Wk"].rearrange("(k p) o -> p k o", p=P)).then_inc(xw_in, 16)
            sp.dma_start(xv_w, d["L0_xattn_Wv"].rearrange("(k p) o -> p k o", p=P)).then_inc(xw_in, 16)
            for n in range(2, len(weights)):
                sp.wait_ge(turned, KD * (n - 1))
                sp.dma_start(raw[n % 2], weights[n][1].rearrange("(o p) i -> p o i", p=P)).then_inc(raw_in[n % 2], 16)
            sp.wait_ge(const_done, 8)
            sp.dma_start(m.xs_d.rearrange("(t p) c -> p t c", p=P),
                         zero[:].unsqueeze(1).broadcast_to([P, NTILE, D])).then_inc(fill_out, 16)
            sp.wait_ge(v, V_EXT)
            sp.dma_start(m.ext_d, ext[:]).then_inc(ext_out, 16)
            sp.wait_ge(ext_out, 16)
            sp.dma_start(hank[:], bass.AP(m.ext_t, 0, [[1, P], [1, BAND]])).then_inc(tab_in, 16)
            sp.wait_ge(fill_out, 16)
            sp.wait_ge(tab_in, 16)

        @block.gpsimd
        def _(pool):
            pool.memset(m.ident[:], 0.0).then_inc(const_done, 1)
            pool.memset(tri[:], 1.0).then_inc(const_done, 1)
            pool.memset(anti[:], 0.0).then_inc(const_done, 1)
            pool.wait_ge(const_done, 3)
            pool.affine_select(out=anti[:], in_=anti[:], compare_op=ALU.not_equal, fill=1.0, base=1 - P,
                               pattern=[[1, P]], channel_multiplier=1).then_inc(const_done, 1)
            pool.affine_select(out=m.ident[:], in_=m.ident[:], compare_op=ALU.not_equal, fill=1.0, base=0,
                               pattern=[[-1, P]], channel_multiplier=1).then_inc(const_done, 1)
            pool.affine_select(out=tri[:], in_=tri[:], compare_op=ALU.is_gt, fill=0.0, base=0,
                               pattern=[[1, P]], channel_multiplier=-1).then_inc(const_done, 1)
            pool.iota(tio[:], [[P, NTILE]], base=0, channel_multiplier=0,
                      allow_small_or_imprecise_dtypes=True).then_inc(const_done, 1)
            pool.memset(zero[:], 0.0).then_inc(const_done, 1)

        @block.scalar
        def _(act):
            act.wait_ge(small_in, 16 * 13)
            act.activation(eneg[:], gates[:, 0:1], ACT.Exp, scale=-1.0).then_inc(eneg_done, 1)
            n = 0
            for name, _ in weights[:4]:
                for k in range(KD):
                    act.wait_ge(turned, n + 1)
                    act.copy(wT[name][0][:, k, :], pt[n % 4][:]).then_inc(hi_done, 1)
                    n += 1
            for k in range(KD):
                act.wait_ge(turned, n + 1)
                act.copy(xqT[:, k, :], pt[n % 4][:]).then_inc(hi_done, 1)
                n += 1
            for b in range(B):
                act.wait_ge(xt, b + 1)
                act.copy(cxT[:, b], pt[b][:, 0:KD * LC].rearrange("p (k t) -> p k t", t=LC)).then_inc(xe, 1)
            for b in range(B):
                act.wait_ge(xt, 2 + b + 1)
                for k in range(KD):
                    act.activation(kxT[:, b, k, :], pt[2 + b][:, k * LC:(k + 1) * LC], ACT.Identity,
                                   bias=xbk[:, k:k + 1]).then_inc(xe, 1)
            for b in range(B):
                act.wait_ge(xt, 4 + b + 1)
                act.mul(m.g[:, b], pt[b][:, 0:KD * LC].rearrange("p (k t) -> p k t", t=LC), XSCALE).then_inc(xe, 1)
            act.wait_ge(xt, 7)
            act.mul(m.g0[:], pr[0:1, 0:B * LC].rearrange("p (b t) -> p b t", b=B), XSCALE).then_inc(xe, 1)

        @block.vector
        def _(dve):
            dve.memset(m.ones[:], 1.0).then_inc(v, 1)
            dve.memset(ext[:], 0.0).then_inc(v, 1)
            dve.memset(tacc[0][:], 0.0).then_inc(v, 1)
            dve.wait_ge(small_in, 16 * 13)
            dve.wait_ge(eneg_done, 1)
            dve.tensor_scalar(epl[:], eneg[:], 1.0, None, ALU.add).then_inc(v, 1)
            dve.wait_ge(v, 4)
            dve.reciprocal(sig[:], epl[:]).then_inc(v, 1)
            dve.wait_ge(v, 5)
            dve.tensor_scalar(trow[:], trow[:], tb0[0:1, :], sig[0:1, :], ALU.subtract, ALU.mult).then_inc(v, 1)
            dve.wait_ge(v, 6)
            first = 2 * P - 1 - TB_MID
            dve.tensor_copy(ext[:, first:first + TB_LEN], trow[:]).then_inc(v, 1)
            dve.wait_ge(v, 7)
            dve.tensor_scalar(ext[:, first + TB_LEN:512], ext[:, first + TB_LEN:512],
                              trow[:, TB_LEN - 1:TB_LEN], None, ALU.add).then_inc(v, 2)
            dve.tensor_tensor(dstep[:], tbl[:], tb0[:], ALU.subtract).then_inc(v, 1)
            dve.tensor_scalar(m.c0[:], tb0[:], sig[:, 0:1], gates[:, 1:2], ALU.mult, ALU.add)
            dve.wait_ge(v, 10)
            dve.tensor_tensor(dfar[:], dstep[:], sig[:], ALU.mult).then_inc(v, 1)
            dve.wait_ge(v, 11)
            dve.tensor_copy(m.dhi[:], dfar[:]).then_inc(v, 1)
            dve.wait_ge(v, 12)
            dve.tensor_tensor(m.dlo[:], dfar[:], m.dhi[:].bitcast(F32), ALU.subtract).then_inc(v, 1)
            dve.tensor_copy(ef[:], ei[:]).then_inc(v, 1)
            dve.wait_ge(v, 14)
            for e in range(NE):
                ins = dve.tensor_scalar(oh[:, e, :], ef[:], float(e), None, ALU.is_equal)
            ins.then_inc(v, 1)
            n = 0
            for name, _ in weights[:4]:
                for k in range(KD):
                    dve.wait_ge(hi_done, n + 1)
                    dve.tensor_tensor(wT[name][1][:, k, :], pt[n % 4][:], wT[name][0][:, k, :].bitcast(F32),
                                      ALU.subtract).then_inc(lo_done, 1)
                    n += 1
            dve.wait_ge(rank_done, 2)
            dve.tensor_copy(tot[:], pq[:, 0:NE * NCOL].rearrange("p (e c) -> p e c", e=NE)).then_inc(v, 1)
            dve.wait_ge(v, 16)
            src, step = tot, 1
            for i in range(5):
                dve.tensor_copy(sc[i][:, :, 0:step], src[:, :, 0:step])
                dve.tensor_tensor(sc[i][:, :, step:], src[:, :, step:], src[:, :, 0:NCOL - step], ALU.add)\
                    .then_inc(v, 1)
                dve.wait_ge(v, 17 + i)
                src, step = sc[i], 2 * step
            dve.tensor_scalar(cntf[:], src[:, :, NCOL - 1], float(P - 1), None, ALU.add).then_inc(v, 1)
            dve.wait_ge(v, 22)
            dve.tensor_copy(cnti[:], cntf[:]).then_inc(v, 1)
            dve.wait_ge(v, 23)
            dve.tensor_scalar(cntj[:], cnti[:], 7, 7, ALU.arith_shift_right, ALU.arith_shift_left).then_inc(v, 1)
            dve.wait_ge(v, 24)
            dve.tensor_scalar(pad[:], cntj[:], float(P), None, ALU.max).then_inc(v, 1)
            dve.wait_ge(v, 25)
            src, step = pad, 1
            for i, dst in enumerate((ps1, ps2, ps3)):
                dve.tensor_copy(dst[:, 0:step], src[:, 0:step])
                dve.tensor_tensor(dst[:, step:], src[:, step:], src[:, 0:NE - step], ALU.add).then_inc(v, 1)
                dve.wait_ge(v, 26 + i)
                src, step = dst, 2 * step
            dve.tensor_tensor(w1[:], sc[4][:], tot[:], ALU.subtract)
            dve.tensor_tensor(base[:], ps3[:], pad[:], ALU.subtract).then_inc(v, 1)
            dve.wait_ge(v, 29)
            dve.tensor_tensor(w2[:], w1[:], base[:].unsqueeze(2).broadcast_to([P, NE, NCOL]), ALU.add).then_inc(v, 1)
            dve.wait_ge(v, 30)
            dve.tensor_tensor(w3[:], pr[:, 0:NE * NCOL].rearrange("p (e c) -> p e c", e=NE), w2[:], ALU.add)\
                .then_inc(v, 1)
            dve.wait_ge(v, 31)
            dve.tensor_tensor(w4[:], w3[:], oh[:], ALU.mult).then_inc(v, 1)
            dve.wait_ge(v, 32)
            dve.tensor_reduce(posf[:], w4[:].rearrange("p e c -> p c e"), AX.X, ALU.add)
            dve.drain()
            dve.tensor_copy(m.pos[:], posf[:]).then_inc(v, 1)
            dve.wait_ge(const_done, 8)
            for e in range(1, NE):
                dve.scalar_tensor_tensor(out=tacc[e % 2][:], in0=tio[:], scalar=base[0:1, e:e + 1],
                                         in1=tacc[(e + 1) % 2][:], op0=ALU.is_ge, op1=ALU.add)
                dve.drain()
            dve.tensor_copy(m.texp[:], tacc[1][:])
            dve.tensor_scalar(m.efirst[:], base[0:1, :], 1.0 / P, None, ALU.mult).then_inc(v, 1)
            dve.wait_ge(v, 34)
            dve.tensor_scalar(m.tslot[:], m.texp[:], 1, None, ALU.bitwise_and).then_inc(v, 1)
            for b in range(B):
                dve.wait_ge(xt, 7 + b + 1)
                dve.tensor_tensor(m.vx[:, b, :], pt[2 + b][0:LC, :], xbv[0:LC, :], ALU.add).then_inc(v, 1)
            dve.tensor_copy(m.ident_r[:], m.ident[:])
            dve.tensor_scalar(m.bqs[:], m.bq[:], QSCALE, None, ALU.mult)
            dve.wait_ge(tab_turned, 1)
            dve.tensor_copy(m.t1[:], pq[:, 0:BAND]).then_inc(v, 1)
            dve.wait_ge(tab_turned, 2)
            dve.tensor_copy(m.t2hi[:], pt[0][:, 0:BAND]).then_inc(v, 1)
            dve.wait_ge(v, 39)
            dve.tensor_tensor(m.t2lo[:], pt[0][:, 0:BAND], m.t2hi[:].bitcast(F32), ALU.subtract)

        @block.tensor
        def _(pe):
            pe.wait_ge(const_done, 8)
            pe.wait_ge(v, 1)
            n = 0
            for w in range(5):
                pe.wait_ge(raw_in[w % 2], 16 * (w // 2 + 1))
                for k in range(KD):
                    if n >= 4:
                        pe.wait_ge(lo_done if n - 4 < 16 else hi_done, n - 3)
                    for o in range(KD):
                        ins = pe.transpose(pt[n % 4][:, o * P:(o + 1) * P], raw[w % 2][:, o, k * P:(k + 1) * P],
                                           m.ident[:])
                    ins.then_inc(turned, 1)
                    n += 1
            pe.wait_ge(v, V_OH)
            ohf = oh[:].rearrange("p e c -> p (e c)")
            pe.matmul(pr[:, 0:NE * NCOL], tri[:], ohf, start=True, stop=True).then_inc(rank_done, 1)
            pe.matmul(pq[:, 0:NE * NCOL], m.ones[:, 0:P], ohf, start=True, stop=True).then_inc(rank_done, 1)
            pe.wait_ge(xw_in, 48)
            pe.wait_ge(hi_done, 20)
            for b in range(B):
                for k in range(KD):
                    ins = pe.transpose(pt[b][:, k * LC:(k + 1) * LC], cx[:, b, k * P:(k + 1) * P],
                                       m.ident[0:LC, 0:LC])
                ins.then_inc(xt, 1)
            for b in range(B):
                pe.wait_ge(xe, b + 1)
                for o in range(KD):
                    for k in range(KD):
                        ins = pe.matmul(pt[2 + b][:, o * LC:(o + 1) * LC], xk_w[:, k, o * P:(o + 1) * P],
                                        cxT[:, b, k, :], start=(k == 0), stop=(k == KD - 1))
                ins.then_inc(xt, 1)
            for b in range(B):
                pe.wait_ge(xe, 2 + KD * (b + 1))
                for i in range(KD):
                    for o in range(KD):
                        ins = pe.matmul(pt[b][:, i * LC:(i + 1) * LC], xqT[:, o, i * P:(i + 1) * P],
                                        kxT[:, b, o, :], start=(o == 0), stop=(o == KD - 1))
                ins.then_inc(xt, 1)
            pe.wait_ge(v, V_POS)
            for b in range(B):
                for o in range(KD):
                    ins = pe.matmul(pr[0:1, b * LC:(b + 1) * LC], xbq[:, o:o + 1], kxT[:, b, o, :],
                                    start=(o == 0), stop=(o == KD - 1))
            ins.then_inc(xt, 1)
            for b in range(B):
                for k in range(KD):
                    ins = pe.matmul(pt[2 + b][0:LC, :], cxT[:, b, k, :], xv_w[:, k, :],
                                    start=(k == 0), stop=(k == KD - 1))
                ins.then_inc(xt, 1)
            pe.wait_ge(tab_in, 16)
            pe.matmul(pq[:, 0:BAND], anti[:], hank[:], start=True, stop=True).then_inc(tab_turned, 1)
            pe.wait_ge(v, 38)
            pe.wait_ge(xe, 2 + KD * B + 2)
            for a in range(BAND // P):
                ins = pe.transpose(pt[0][:, a * P:(a + 1) * P], m.t1[:, BAND - (a + 1) * P:BAND - a * P], m.ident[:])
            ins.then_inc(tab_turned, 1)


def stage_project(nc, d, m):
    xr = d["x"].rearrange("b (n t p) c -> (b n) p t c", t=G, p=P)
    with ExitStack() as c:
        def sb(name, shape, dt=F32):
            return c.enter_context(nc.sbuf_tensor(name, shape, dt))

        def sem(name):
            return c.enter_context(nc.semaphore(name))

        xg = [sb(f"xg{i}", [P, G, D]) for i in range(2)]
        xh = [sb(f"xh{i}", [P, KD, GT], F32R) for i in range(2)]
        xl = [sb(f"xl{i}", [P, KD, GT], F32R) for i in range(2)]
        qf = [sb(f"qf{i}", [P, GT]) for i in range(2)]
        qh = [sb(f"qh{i}", [P, GT], F32R) for i in range(2)]
        ql = [sb(f"ql{i}", [P, GT], F32R) for i in range(2)]
        pt = [c.enter_context(nc.psum_tensor(f"ptp{i}", [P, GT], F32)) for i in range(KD)]
        pm = [c.enter_context(nc.psum_tensor(f"pmp{i}", [P, GT], F32)) for i in range(4)]

        x_in = [sem(f"x_in{i}") for i in range(2)]
        x_turned = sem("x_turned")
        xh_done = sem("xh_done")
        xl_done = sem("xl_done")
        x_read = sem("x_read")
        mm_done = sem("mm_done")
        qf_done = sem("qf_done")
        qh_done = sem("qh_done")
        ql_done = sem("ql_done")
        v_done = sem("v_done")
        part_out = [sem(f"part_out{i}") for i in range(2)]
        block = c.enter_context(nc.Block())
        NQK = 2 * KD
        NMM = NQK + G
        LAST = NG - 2

        @block.sync
        def _(sp):
            for j in range(2):
                sp.sem_inc(part_out[j], 32)
                sp.dma_start(xg[j][:], xr[j]).then_inc(x_in[j], 16)

            def group(n, par, more):
                if more:
                    sp.wait_ge(x_turned, KD * (n + 1))
                    sp.dma_start(xg[par][:], xr[n + 2]).then_inc(x_in[par], 16)
                for j in range(NQK):
                    sp.wait_ge(ql_done, NQK * n + j + 1 + 2)
                    dst = (m.q_d, m.k_d)[j // KD]
                    rows = slice((j % KD) * P, (j % KD + 1) * P)
                    sp.dma_start(dst[0, n, rows, :], qh[j % 2][:].bitcast(F32)).then_inc(part_out[j % 2], 16)
                    sp.dma_start(dst[1, n, rows, :], ql[j % 2][:].bitcast(F32)).then_inc(part_out[j % 2], 16)

            with sp.Fori(0, LAST // 2) as i:
                for par in range(2):
                    group(2 * i + par, par, True)
            for n in range(LAST, NG):
                group(n, n % 2, False)
            for j in range(2):
                sp.wait_ge(part_out[j], 32 * (NQK // 2 * NG + 1))

        @block.scalar
        def _(act):
            def turn(n, par):
                act.wait_ge(x_read, n + 1)
                for k in range(KD):
                    act.wait_ge(x_turned, KD * n + k + 1)
                    act.copy(xh[par][:, k, :], pt[k][:]).then_inc(xh_done, 1)

            def scale(n):
                for j in range(NQK):
                    act.wait_ge(mm_done, (NMM - 1) * n + j + 1)
                    act.wait_ge(ql_done, NQK * n + j + 1)
                    bias = (m.bqs if j < KD else m.bk)[:, j % KD:j % KD + 1]
                    act.activation(qf[j % 2][:], pm[j % 4][:], ACT.Identity, bias=bias,
                                   scale=QSCALE if j < KD else 1.0).then_inc(qf_done, 1)

            turn(0, 0)
            with act.Fori(0, LAST // 2) as i:
                for par in range(2):
                    turn(2 * i + par + 1, 1 - par)
                    scale(2 * i + par)
            turn(NG - 1, 1)
            scale(NG - 2)
            scale(NG - 1)

        @block.vector
        def _(dve):
            dve.sem_inc(ql_done, 2)
            dve.sem_inc(v_done, G)

            def turn(n, par):
                for k in range(KD):
                    dve.wait_ge(xh_done, KD * n + k + 1)
                    dve.tensor_tensor(xl[par][:, k, :], pt[k][:], xh[par][:, k, :].bitcast(F32),
                                      ALU.subtract).then_inc(xl_done, 1)

            def parts(n):
                for j in range(NQK):
                    dve.wait_ge(qf_done, NQK * n + j + 1)
                    dve.wait_ge(part_out[j % 2], 32 * (NQK // 2 * n + j // 2 + 1))
                    dve.tensor_copy(qh[j % 2][:], qf[j % 2][:]).then_inc(qh_done, 1)
                    dve.wait_ge(qh_done, NQK * n + j + 1)
                    dve.tensor_tensor(ql[j % 2][:], qf[j % 2][:], qh[j % 2][:].bitcast(F32),
                                      ALU.subtract).then_inc(ql_done, 1)
                for j in range(G):
                    if j < G - 1:
                        dve.wait_ge(mm_done, (NMM - 1) * n + NQK + j + 1)
                    else:
                        dve.wait_ge(x_read, n + 1 + 2)
                    dve.tensor_tensor(m.v[:, G * n + j, :], pm[j % 4][:], m.bv[:], ALU.add).then_inc(v_done, 1)

            turn(0, 0)
            with dve.Fori(0, LAST // 2) as i:
                for par in range(2):
                    turn(2 * i + par + 1, 1 - par)
                    parts(2 * i + par)
            turn(NG - 1, 1)
            parts(NG - 2)
            parts(NG - 1)

        @block.tensor
        def _(pe):
            pe.sem_inc(x_read, 2)

            def turn(n, par, uses):
                pe.wait_ge(x_in[par], 16 * uses)
                for k in range(KD):
                    if not isinstance(n, int) or n > 0:
                        pe.wait_ge(xl_done, KD * (n - 1) + k + 1)
                    for t in range(G):
                        ins = pe.transpose(pt[k][:, t * P:(t + 1) * P], xg[par][:, t, k * P:(k + 1) * P], m.ident[:])
                    ins.then_inc(x_turned, 1)

            def products(n, par):
                pe.wait_ge(xl_done, KD * (n + 1))
                for j in range(NMM):
                    if j < 4:
                        pe.wait_ge(v_done, G * n + j + 1)
                    else:
                        pe.wait_ge(qf_done, NQK * n + j - 4 + 1)
                    if j < NQK:
                        w, o = (m.wqT, m.wkT)[j // KD], j % KD
                        terms = [(w[a][:, k, o * P:(o + 1) * P], (xh, xl)[b][par][:, k, :])
                                 for a, b in ((0, 0), (0, 1), (1, 0)) for k in range(KD)]
                    else:
                        t = j - NQK
                        terms = [((xh, xl)[b][par][:, k, t * P:(t + 1) * P], m.wvT[a][:, k, :])
                                 for a, b in ((0, 0), (1, 0), (0, 1)) for k in range(KD)]
                    for i, (lhs, rhs) in enumerate(terms):
                        ins = pe.matmul(pm[j % 4][:], lhs, rhs, start=(i == 0), stop=(i == len(terms) - 1))
                    ins.then_inc(mm_done if j < NMM - 1 else x_read, 1)

            turn(0, 0, 1)
            with pe.Fori(0, LAST // 2) as i:
                for par in range(2):
                    turn(2 * i + par + 1, 1 - par, i + 1 + par)
                    products(2 * i + par, par)
            turn(NG - 1, 1, NG // 2)
            products(NG - 2, 0)
            products(NG - 1, 1)


def band_cols(blk, lo, hi):
    a, b = max(lo, P * (blk - 1)), min(hi, P * (blk + 2))
    return (a, b, a - P * (blk - 1)) if a < b else None


def max_pieces(qb, kc):
    lo, hi = 512 * kc, 512 * (kc + 1)
    band = band_cols(qb, lo, hi)
    if band is None:
        return [(0, 512, None)]
    a, b, f = band
    out = [(0, a - lo, None)] if a > lo else []
    out.append((a - lo, b - lo, f))
    return out + ([(b - lo, 512, None)] if b < hi else [])


NPIECE = 8
MAX_UNITS = NB * 4
PAIRS = NB // 2 - 1
DENS = PAIRS + 2


def load_stacks(eng, m, stack_in, h, batch, u):
    for r, (q, k) in enumerate(((0, 0), (1, 0), (0, 1))):
        for src, part, dst in ((m.q_d, q, m.qst), (m.k_d, k, m.kst)):
            rows = src[part].rearrange("b (h r) t -> b h r t", r=HD).rearrange("(b n) h r t -> b h r n t", b=B)
            eng.dma_start(dst[u][r * HD:(r + 1) * HD, :].bitcast(F32).rearrange("r (n t) -> r n t", t=GT),
                          rows[batch, h]).then_inc(stack_in[u], 16)


def stage_stack_rows(nc, d, m, stack_in):
    with ExitStack() as c:
        def sb(name, shape, dt=F32):
            return c.enter_context(nc.sbuf_tensor(name, shape, dt))

        hot = sb("hot", [NSTEP, T])
        far = sb("far", [NSTEP, T])
        one = sb("one", [2, 512], F32R)
        hot_r = sb("hot_r", [NSTEP, T], F32R)
        far_r = [sb(f"far_r{i}", [NSTEP, T], F32R) for i in range(2)]
        shaped = c.enter_context(nc.semaphore("shaped"))
        one_made = c.enter_context(nc.semaphore("one_made"))
        rows_made = c.enter_context(nc.semaphore("rows_made"))
        rows_in = c.enter_context(nc.semaphore("rows_in"))
        block = c.enter_context(nc.Block())

        @block.gpsimd
        def _(pool):
            pool.memset(hot[:], 1.0).then_inc(shaped, 1)
            pool.memset(far[:], 1.0).then_inc(shaped, 1)
            pool.wait_ge(shaped, 2)
            pool.affine_select(out=hot[:], in_=hot[:], compare_op=ALU.is_ge, fill=0.0, base=0,
                               pattern=[[1, T]], channel_multiplier=-P).then_inc(shaped, 1)
            pool.affine_select(out=far[:], in_=far[:], compare_op=ALU.is_ge, fill=0.0, base=-2 * P,
                               pattern=[[1, T]], channel_multiplier=-P).then_inc(shaped, 1)
            pool.wait_ge(shaped, 4)
            pool.affine_select(out=hot[:], in_=hot[:], compare_op=ALU.is_gt, fill=0.0, base=P,
                               pattern=[[-1, T]], channel_multiplier=P).then_inc(shaped, 1)

        @block.vector
        def _(dve):
            dve.memset(one[:].bitcast(F32), 1.0).then_inc(one_made, 1)
            dve.wait_ge(shaped, 5)
            dve.tensor_copy(hot_r[:], hot[:])
            dve.tensor_scalar(far_r[0][:], far[:], m.dhi[0:NSTEP, :].bitcast(F32), None, ALU.mult)
            dve.tensor_scalar(far_r[1][:], far[:], m.dlo[0:NSTEP, :], None, ALU.mult).then_inc(rows_made, 1)

        @block.sync
        def _(sp):
            for u in range(4):
                load_stacks(sp, m, stack_in, u // B, u % B, u)

        @block.scalar
        def _(act):
            for u in range(4):
                for n in range(T // 512):
                    if u == n == 0:
                        act.wait_ge(one_made, 1)
                    act.dma_start(m.kst[u][ROW_SHIFT:ROWS, n * 512:(n + 1) * 512].bitcast(F32),
                                  one[:].bitcast(F32)).then_inc(rows_in, 16)
            act.wait_ge(rows_made, 1)
            for u in range(4):
                for i in range(2):
                    lo = ROW_STEP + i * NSTEP
                    act.dma_start(m.qst[u][lo:lo + NSTEP, :].bitcast(F32), hot_r[:].bitcast(F32)).then_inc(rows_in, 16)
                    act.dma_start(m.kst[u][lo:lo + NSTEP, :].bitcast(F32), far_r[i][:].bitcast(F32)).then_inc(rows_in, 16)
            act.wait_ge(rows_in, 16 * 32)


def stage_attention(nc, d, m):
    with ExitStack() as c:
        def sb(name, shape, dt=F32):
            return c.enter_context(nc.sbuf_tensor(name, shape, dt))

        def sem(name):
            return c.enter_context(nc.semaphore(name))

        m.qst = [sb(f"qst{u}", [P, T], F32R) for u in range(4)]
        m.kst = [sb(f"kst{u}", [P, T], F32R) for u in range(4)]
        stack_in = [sem(f"stack_in{u}") for u in range(4)]
        stage_stack_rows(nc, d, m, stack_in)

        prob = [sb(f"prob{i}", [P, T]) for i in range(4)]
        vh = [sb(f"vh{i}", [P, NB, HD]) for i in range(2)]
        acc_s = sb("acc_s", [P, 512])
        sum_s = sb("sum_s", [P, 512])
        cxo = [sb(f"cxo{i}", [P, 16, 32]) for i in range(2)]
        pieces = sb("pieces", [P, NB, NPIECE])
        junk = [sb(f"junk{i}", [P, BAND]) for i in range(2)]
        mq = sb("mq", [P, NB])
        mfull = sb("mfull", [P, NB])
        shift = sb("shift", [P, NB])
        sh_hi = sb("sh_hi", [NB, P], F32R)
        sh_lo = sb("sh_lo", [NB, P], F32R)

        st = [c.enter_context(nc.psum_tensor(f"st{i}", [P, 1024], F32)) for i in range(2)]
        mx = [c.enter_context(nc.psum_tensor(f"mx{i}", [P, 512], F32)) for i in range(2)]
        acc = c.enter_context(nc.psum_tensor("acc", [P, 512], F32))
        den = c.enter_context(nc.psum_tensor("den", [P, 512], F32))

        shift_in = sem("shift_in")
        v_copied = sem("v_copied")
        s_done = [sem(f"s_done{i}") for i in range(2)]
        e_done = [sem(f"e_done{i}") for i in range(2)]
        pv_done = sem("pv_done")
        paired = sem("paired")
        den_done = sem("den_done")
        blank = sem("blank")
        acc_taken = sem("acc_taken")
        mx_done = [sem(f"mx_done{i}") for i in range(2)]
        mx_taken = [sem(f"mx_taken{i}") for i in range(2)]
        m_chain = sem("m_chain")
        shift_done = sem("shift_done")
        turned = sem("sh_turned")
        sh_own = sem("sh_own")
        rec_done = sem("rec_done")
        norm_done = sem("norm_done")
        ctx_out = [sem(f"ctx_out{i}") for i in range(2)]
        block = c.enter_context(nc.Block())

        CTX_INC = 16 * 16
        LOOPS = NH // 4 - 1
        USES = (MAX_UNITS // 2 + 1, MAX_UNITS // 2)

        def four_heads(eng, body):
            with eng.Fori(0, LOOPS) as i:
                for u in range(4):
                    body(4 * i + u, i, u, False)
            for u in range(4):
                body(4 * LOOPS + u, LOOPS, u, u == 3)

        @block.sync
        def _(sp):
            for i in range(2):
                sp.sem_inc(ctx_out[i], CTX_INC + 16)
            sp.wait_ge(mx_taken[0], USES[0] + 1)
            sp.dma_start(m.qst[0][ROW_SHIFT:ROW_SHIFT + 1, :].bitcast(F32), sh_hi[:].bitcast(F32)).then_inc(shift_in, 16)
            sp.dma_start(m.qst[0][ROW_SHIFT + 1:ROWS, :].bitcast(F32), sh_lo[:].bitcast(F32)).then_inc(shift_in, 16)

            def head(hh, i, u, last):
                if not last:
                    sp.wait_ge(mx_taken[0], USES[0] * (hh + 2) + 1)
                    nxt = m.qst[(u + 1) % 4]
                    sp.dma_start(nxt[ROW_SHIFT:ROW_SHIFT + 1, :].bitcast(F32), sh_hi[:].bitcast(F32)).then_inc(shift_in, 16)
                    sp.dma_start(nxt[ROW_SHIFT + 1:ROWS, :].bitcast(F32), sh_lo[:].bitcast(F32)).then_inc(shift_in, 16)
                if not isinstance(hh, int):
                    sp.wait_ge(s_done[1], NB * (hh + 1))
                    load_stacks(sp, m, stack_in, i * 2 + (u // B + 2), u % B, u)
                sp.wait_ge(norm_done, hh + 1 + 1)
                dst = m.ctx_d[hh].rearrange("(jm d) (jk g i) -> g d jk jm i", d=HD, jk=KD, g=4)
                src = cxo[u % 2]
                for g in range(4):
                    for jm in range(4):
                        sp.dma_start(dst[g, :, :, jm], src[g * HD:(g + 1) * HD, jm::4, :]).then_inc(ctx_out[u % 2], 16)

            four_heads(sp, head)
            for i in range(2):
                sp.wait_ge(ctx_out[i], CTX_INC * (NH // 2 + 1) + 16)

        @block.gpsimd
        def _(pool):
            def copy_v(h, batch, par):
                src = m.v[:, batch * NB:(batch + 1) * NB, :].rearrange("p b (h e) -> p b h e", e=HD)
                pool.tensor_copy(vh[par][:], src[:, :, h, :]).then_inc(v_copied, 1)

            copy_v(0, 0, 0)

            def normalise(hh, i, u):
                pool.wait_ge(acc_taken, hh + 1)
                pool.wait_ge(rec_done, hh + 1)
                pool.wait_ge(ctx_out[(u + 1) % 2], CTX_INC * (i * 2 + (u - 1) // 2 + 1) + 16)
                out = cxo[(u + 1) % 2][:].rearrange("p j i -> p i j")
                pool.tensor_tensor(out, acc_s[:].rearrange("p (i j) -> p i j", j=16),
                                   sum_s[:].rearrange("p (i j) -> p i j", j=16), ALU.mult).then_inc(norm_done, 1)

            def head(hh, i, u, last):
                for pair in range(PAIRS):
                    even, odd = prob[2 * pair % 4], prob[(2 * pair + 1) % 4]
                    for half in range(2):
                        pool.wait_ge(e_done[half], NB * hh + 2 * pair + 3)
                    pool.wait_ge(pv_done, NB * hh + 2 * pair + 1)
                    pool.tensor_tensor(even[:], even[:], odd[:], ALU.add).then_inc(paired, 1)
                    if pair == 0:
                        normalise(hh, i, u)
                    if pair == 1 and not last:
                        nu = u + 1
                        copy_v(i * 2 + nu // B, nu % B, nu % 2)

            four_heads(pool, head)
            normalise(NH, LOOPS, 4)

        @block.scalar
        def _(act):
            for i in range(2):
                act.sem_inc(e_done[i], 1)
            act.wait_ge(blank, 1)
            act.sem_inc(acc_taken, 1)

            def head(hh, i, u, last):
                for kb in range(NB):
                    if kb < 4:
                        act.wait_ge(den_done, DENS * hh + (PAIRS, PAIRS, PAIRS + 1, DENS)[kb])
                    else:
                        act.wait_ge(den_done, DENS * (hh + 1) + kb // 2 - 1)
                    for half in range(2):
                        act.wait_ge(s_done[half], NB * hh + kb + 1)
                        act.activation(prob[kb % 4][:, half * 1024:(half + 1) * 1024], st[half][:],
                                       ACT.Exp).then_inc(e_done[half], 1)
                act.wait_ge(den_done, DENS * (hh + 2))
                act.wait_ge(norm_done, hh + 1)
                act.copy(acc_s[:], acc[:])
                act.copy(sum_s[:], den[:]).then_inc(acc_taken, 1)

            four_heads(act, head)

        @block.vector
        def _(dve):
            for i in range(2):
                dve.sem_inc(mx_taken[i], 1)
            dve.memset(sum_s[:], 1.0)
            dve.memset(acc_s[:], 0.0)
            dve.memset(pieces[:], -3.0e38).then_inc(blank, 1)
            dve.wait_ge(blank, 1)

            def invert(piece):
                part = sum_s[:, piece * P:(piece + 1) * P]
                ins = dve.reciprocal(part, part)
                if piece == 3:
                    ins.then_inc(rec_done, 1)

            def maxima(hh, beside=()):
                slot = [0] * NB
                n_band = 0
                for unit in range(MAX_UNITS):
                    qb, kc, bank = unit // 4, unit % 4, unit % 2
                    scored = MAX_UNITS // 2 * hh + unit // 2 + 1
                    dve.wait_ge(mx_done[bank], scored)
                    cuts = sorted(max_pieces(qb, kc), key=lambda piece: piece[2] is not None)
                    for a, b, f in cuts:
                        out = pieces[:, qb, slot[qb]:slot[qb] + 1]
                        slot[qb] += 1
                        if f is None:
                            ins = dve.tensor_reduce(out, mx[bank][:, a:b], AX.X, ALU.max)
                        else:
                            ins = dve.tensor_tensor_reduce(junk[bank][:, 0:b - a], mx[bank][:, a:b],
                                                           m.t1[:, f:f + b - a], 1.0, -3.0e38, ALU.add, ALU.max, out)
                    ins.then_inc(mx_taken[bank], 1)
                    if unit in beside:
                        invert(beside.index(unit))
                assert max(slot) <= NPIECE
                for bank in range(2):
                    dve.wait_ge(mx_taken[bank], USES[bank] * hh + MAX_UNITS // 2 + 1)
                dve.tensor_reduce(mq[:], pieces[:], AX.X, ALU.max).then_inc(m_chain, 1)
                dve.wait_ge(m_chain, 2 * hh + 1)
                dve.tensor_scalar(mfull[:], mq[:], m.c0[:, 0:1], None, ALU.add).then_inc(m_chain, 1)
                dve.wait_ge(m_chain, 2 * hh + 2)
                dve.tensor_scalar(shift[:], mfull[:], -1.0, m.c0[:, 0:1], ALU.mult, ALU.add).then_inc(shift_done, 1)
                dve.wait_ge(turned, hh + 1)
                if not isinstance(hh, int) or hh > 0:
                    dve.wait_ge(shift_in, 32 * hh)
                dve.tensor_copy(sh_hi[:], mx[0][0:NB, 0:P]).then_inc(sh_own, 1)
                dve.wait_ge(sh_own, hh + 1)
                dve.tensor_tensor(sh_lo[:], mx[0][0:NB, 0:P], sh_hi[:].bitcast(F32), ALU.subtract).then_inc(mx_taken[0], 1)

            maxima(0)

            def head(hh, i, u, last):
                dve.wait_ge(acc_taken, hh + 1)
                if not last:
                    maxima(hh + 1, (2, 6, 9, 12))
                else:
                    for piece in range(4):
                        invert(piece)

            four_heads(dve, head)
            dve.wait_ge(acc_taken, NH + 1)
            for piece in range(4):
                invert(piece)

        @block.tensor
        def _(pe):
            pe.sem_inc(den_done, DENS)

            def max_unit(hh, u, unit):
                qb, kc, bank = unit // 4, unit % 4, unit % 2
                pe.wait_ge(mx_taken[bank], USES[bank] * hh + unit // 2 + 1)
                pe.matmul(mx[bank][:], m.qst[u][0:ROW_SHIFT, qb * P:(qb + 1) * P],
                          m.kst[u][0:ROW_SHIFT, kc * 512:(kc + 1) * 512], start=True, stop=True)\
                    .then_inc(mx_done[bank], 1)

            def turn_shift(hh):
                pe.wait_ge(shift_done, hh + 1)
                pe.wait_ge(mx_taken[0], USES[0] * hh + MAX_UNITS // 2 + 1)
                pe.transpose(mx[0][0:NB, 0:P], shift[:], m.ident[:]).then_inc(turned, 1)

            def scores(hh, u, kb, half):
                pe.wait_ge(e_done[half], NB * hh + kb + 1)
                for n in range(2):
                    q0 = half * 1024 + n * 512
                    band = band_cols(kb, q0, q0 + 512)
                    ins = pe.matmul(st[half][:, n * 512:(n + 1) * 512], m.kst[u][0:ROWS, kb * P:(kb + 1) * P],
                                    m.qst[u][0:ROWS, q0:q0 + 512], start=True, stop=band is None)
                    if band:
                        a, b, f = band
                        o = a - half * 1024
                        for part in (m.t2hi, m.t2lo):
                            ins = pe.matmul(st[half][:, o:o + b - a], m.ident_r[:], part[:, f:f + b - a],
                                            start=False, stop=part is m.t2lo)
                ins.then_inc(s_done[half], 1)

            def values(hh, par, kb):
                for half in range(2):
                    pe.wait_ge(e_done[half], NB * hh + kb + 2)
                if kb == 0:
                    pe.wait_ge(acc_taken, hh + 1)
                for g in range(4):
                    ins = pe.matmul(acc[g * HD:(g + 1) * HD, :], vh[par][:, kb, :], prob[kb % 4][:, g * 512:(g + 1) * 512],
                                    start=(kb == 0), stop=(kb == NB - 1))
                ins.then_inc(pv_done, 1)

            def row_sums(hh, n):
                if n < PAIRS:
                    pe.wait_ge(paired, PAIRS * hh + n + 1)
                kb = 2 * n if n < PAIRS else PAIRS + n
                for g in range(4):
                    ins = pe.matmul(den[g * HD:(g + 1) * HD, :], m.ones[:, 0:HD], prob[kb % 4][:, g * 512:(g + 1) * 512],
                                    start=(n == 0), stop=(n == DENS - 1))
                ins.then_inc(den_done, 1)

            pe.wait_ge(stack_in[0], 96)
            for unit in range(MAX_UNITS):
                max_unit(0, 0, unit)
            turn_shift(0)

            def head(hh, i, u, last):
                pe.wait_ge(shift_in, 32 * (hh + 1))
                nu = (u + 1) % 4
                if not last:
                    pe.wait_ge(stack_in[nu], 96 * (i + 1 + (u == 3)))
                units = list(range(MAX_UNITS)) if not last else []

                def spread(n):
                    for _ in range(n):
                        if units:
                            max_unit(hh + 1, nu, units.pop(0))

                for kb in range(NB):
                    scores(hh, u, kb, 0)
                    spread(1)
                    scores(hh, u, kb, 1)
                    spread(1)
                    if kb == 0:
                        pe.wait_ge(v_copied, hh + 1)
                        spread(1)
                        continue
                    values(hh, u % 2, kb - 1)
                    if kb == NB - 1 and not last:
                        assert not units
                        turn_shift(hh + 1)
                    spread(2)
                    if kb % 2 == 1 and kb > 1:
                        row_sums(hh, (kb - 3) // 2)
                        spread(1)
                row_sums(hh, PAIRS)
                values(hh, u % 2, NB - 1)
                row_sums(hh, PAIRS + 1)

            four_heads(pe, head)


class Norm:
    def __init__(self, sem, name):
        self.res = sem(name + "_res")
        self.stats = sem(name + "_stats")
        self.aggr = sem(name + "_aggr")
        self.veps = sem(name + "_veps")
        self.rstd = sem(name + "_rstd")
        self.done = sem(name + "_done")


SLOTS = 4
TURNS = NB // SLOTS


def stage_rows(nc, d, m, out):
    with ExitStack() as c:
        def sb(name, shape, dt=F32):
            return c.enter_context(nc.sbuf_tensor(name, shape, dt))

        def sem(name):
            return c.enter_context(nc.semaphore(name))

        def slots(name, shape, dt=F32):
            return [sb(f"{name}{u}", shape, dt) for u in range(SLOTS)]

        bo, fb = sb("bo", [P, D]), sb("fb_r", [P, D])
        half, eps = sb("half", [P, 1]), sb("eps", [P, 1])
        cin, xin = slots("cin", [P, KD, P]), slots("xin", [P, D])
        ch, cl = slots("ch", [P, KD, P], F32R), slots("cl", [P, KD, P], F32R)
        res1, x2, x2T = slots("res1", [P, D]), slots("x2", [P, D]), slots("x2T", [P, KD, P])
        row3 = slots("row3", [P, D])
        stats = [slots(f"stats{k}", [P, 6]) for k in range(3)]
        mean = [slots(f"mean{k}", [P, 2]) for k in range(3)]
        veps = [slots(f"veps{k}", [P, 1]) for k in range(3)]
        rstd = [slots(f"rstd{k}", [P, 1]) for k in range(3)]
        pick = slots("pick", [P, TOPK], I32)
        nmax, esum, rsum = slots("nmax", [P, 1]), slots("esum", [P, 1]), slots("rsum", [P, 1])
        ex, exT = slots("pex", [P, LC]), slots("pexT", [LC, P])
        pa = [c.enter_context(nc.psum_tensor(f"pa{u}", [P, 512], F32)) for u in range(SLOTS)]
        pb = [c.enter_context(nc.psum_tensor(f"pb{u}", [P, 512], F32)) for u in range(SLOTS)]

        bias_in = sem("bias_in")
        tile_in = [sem(f"tile_in{u}") for u in range(SLOTS)]
        const_made = sem("const_made")
        cut_hi = sem("cut_hi")
        cut = sem("cut")
        xb_done = sem("xb_done")
        proj_done = sem("proj_done")
        x2_turned = sem("x2_turned")
        x2T_done = sem("x2T_done")
        cs_done = sem("cs_done")
        nmax_done = sem("nmax_done")
        ex_done = sem("ex_done")
        rsum_done = sem("rsum_done")
        ex_turned = sem("ex_turned")
        exT_done = sem("exT_done")
        cv_done = sem("cv_done")
        stored = [sem(f"stored{u}") for u in range(SLOTS)]
        picked = sem("picked")
        sorted_out = [sem(f"sorted_out{u}") for u in range(SLOTS)]
        sorted_seen = [sem(f"sorted_seen{u}") for u in range(SLOTS)]
        n1, n2, n3 = Norm(sem, "norm1"), Norm(sem, "norm2"), Norm(sem, "norm3")
        block = c.enter_context(nc.Block())
        xrow = d["x"].rearrange("b (n p) c -> (b n) p c", p=P)
        x3row = m.x3_d.rearrange("(n p) c -> n p c", p=P)
        orow = out.rearrange("b (n p) c -> b n p c", p=P)

        def turns(eng, front, both, back):
            front(0)
            with eng.Fori(0, TURNS) as i:
                both(i, 0, True)
            with eng.Fori(0, TURNS - 2) as i:
                both(i + TURNS, 1, True)
            both(B * TURNS - 2, 1, False)
            back(B * TURNS - 1, 1)

        @block.sync
        def _(sp):
            sp.dma_start(bo[:], bcast_rows(d["L0_attn_bo"])).then_inc(bias_in, 16)
            sp.dma_start(fb[:], bcast_rows(d["L0_ffn_bias"])).then_inc(bias_in, 16)
            for u in range(SLOTS):
                sp.sem_inc(stored[u], 16)
                sp.sem_inc(sorted_seen[u], 1)

            def load(t):
                for u in range(SLOTS):
                    sp.wait_ge(cut, SLOTS * t + u + 1)
                    sp.wait_ge(n1.res, SLOTS * t + u + 1)
                    sp.dma_start(cin[u][:].rearrange("p k r -> p (k r)"), m.ctx_d[SLOTS * t + u]).then_inc(tile_in[u], 16)
                    sp.dma_start(xin[u][:], xrow[SLOTS * t + u]).then_inc(tile_in[u], 16)

            def store(t, b):
                for u in range(SLOTS):
                    if b == 0:
                        sp.wait_ge(n2.done, SLOTS * t + u + 1)
                        sp.dma_start(x3row[SLOTS * t + u], row3[u][:]).then_inc(stored[u], 16)
                    else:
                        sp.wait_ge(n3.done, SLOTS * (t - TURNS) + u + 1)
                        sp.dma_start(orow[1, SLOTS * (t - TURNS) + u], row3[u][:]).then_inc(stored[u], 16)

            load(0)
            load(1)
            with sp.Fori(0, TURNS) as i:
                load(i + 2)
                store(i, 0)
                for u in range(SLOTS):
                    sp.wait_ge(sorted_out[u], 32 * (i + 1))
                    sp.sem_inc(sorted_seen[u], 1)
            with sp.Fori(0, TURNS - 2) as i:
                load(i + TURNS + 2)
                store(i + TURNS, 1)
            for t in range(B * TURNS - 2, B * TURNS):
                store(t, 1)
            for u in range(SLOTS):
                sp.wait_ge(stored[u], 16 * (B * TURNS + 1))

        @block.gpsimd
        def _(pool):
            pool.memset(eps[:], EPS)
            pool.memset(half[:], -0.5).then_inc(const_made, 1)
            pool.wait_ge(const_made, 1)
            pool.wait_ge(bias_in, 32)

            def add_bias(t):
                for u in range(SLOTS):
                    pool.wait_ge(tile_in[u], 32 * (t + 1))
                    pool.tensor_tensor(xin[u][:], xin[u][:], bo[:], ALU.add).then_inc(xb_done, 1)

            def rstds(norm, k, t):
                for u in range(SLOTS):
                    pool.wait_ge(norm.aggr, SLOTS * t + u + 1)
                    pool.tensor_tensor(veps[k][u][:], mean[k][u][:, 1:2], eps[:], ALU.add).then_inc(norm.veps, 1)
                for u in range(SLOTS):
                    pool.wait_ge(norm.veps, SLOTS * t + u + 1)
                    pool.tensor_tensor(rstd[k][u][:], veps[k][u][:], half[:], ALU.pow).then_inc(norm.rstd, 1)

            def sort_rows(t):
                for u in range(SLOTS):
                    pool.wait_ge(sorted_seen[u], t + 1)
                    pool.tensor_copy(pick[u][:], m.pos[:, bass.ds((t * SLOTS + u) * TOPK, TOPK)]).then_inc(picked, 1)
                for u in range(SLOTS):
                    pool.wait_ge(const_made, 1)
                    pool.wait_ge(picked, SLOTS * t + u + 1)
                    pool.wait_ge(n2.done, SLOTS * t + u + 1)
                    for j in range(TOPK):
                        pool.indirect_dma_start(m.xs_d, bass.IndirectOffsetOnAxis(pick[u][:, j:j + 1], 0),
                                                row3[u][:], None).then_inc(sorted_out[u], 16)

            def front(t):
                add_bias(t)
                rstds(n1, 0, t)

            def both(t, b, more):
                add_bias(t + 1)
                rstds(n1, 0, t + 1)
                rstds(n2, 1, t)
                if b == 0:
                    sort_rows(t)
                else:
                    rstds(n3, 2, t - TURNS)

            def back(t, b):
                rstds(n2, 1, t)
                rstds(n3, 2, t - TURNS)

            turns(pool, front, both, back)

        @block.scalar
        def _(act):
            def high_parts(t):
                for u in range(SLOTS):
                    act.wait_ge(tile_in[u], 32 * (t + 1))
                    if not isinstance(t, int) or t > 0:
                        act.wait_ge(proj_done, SLOTS * (t - 1) + u + 1)
                    act.copy(ch[u][:], cin[u][:]).then_inc(cut_hi, 1)

            def front(t):
                high_parts(t)
                high_parts(t + 1)

            def copy_x2(t):
                for u in range(SLOTS):
                    act.wait_ge(x2_turned, SLOTS * t + u + 1)
                    act.copy(x2T[u][:], pb[u][:].rearrange("p (k r) -> p k r", k=KD)).then_inc(x2T_done, 1)

            def softmax(t):
                for u in range(SLOTS):
                    act.wait_ge(nmax_done, SLOTS * t + u + 1)
                    act.activation(ex[u][:], pb[u][:, 0:LC], ACT.Exp, bias=nmax[u][:, 0:1],
                                   accum_out=esum[u][:]).then_inc(ex_done, 1)
                for u in range(SLOTS):
                    act.wait_ge(ex_turned, SLOTS * t + u + 1)
                    act.copy(exT[u][:], pb[u][0:LC, P:2 * P]).then_inc(exT_done, 1)

            def both(t, b, more):
                copy_x2(t)
                softmax(t)
                if more:
                    high_parts(t + 2)

            def back(t, b):
                copy_x2(t)
                softmax(t)

            turns(act, front, both, back)

        @block.vector
        def _(dve):
            dve.sem_inc(cut, SLOTS)
            dve.sem_inc(n1.res, SLOTS)
            dve.sem_inc(n2.res, SLOTS)

            def statistics(norm, k, src, t, credit):
                for u in range(SLOTS):
                    dve.wait_ge(norm.res, SLOTS * t + u + 1 + credit)
                    dve.bn_stats(stats[k][u][:], src[u][:]).then_inc(norm.stats, 1)
                for u in range(SLOTS):
                    counted = SLOTS * t + u + 1
                    dve.wait_ge(bias_in, 32)
                    dve.wait_ge(norm.stats, counted)
                    dve.bn_aggr(mean[k][u][:], stats[k][u][:]).then_inc(norm.aggr, 1)

            def apply(norm, k, src, dst, t):
                for u in range(SLOTS):
                    dve.wait_ge(norm.rstd, SLOTS * t + u + 1)
                    if dst is x2:
                        dve.wait_ge(n2.res, SLOTS * t + u + 1)
                    dve.tensor_scalar(dst[u][:], src[u][:], mean[k][u][:, 0:1], rstd[k][u][:, 0:1],
                                      ALU.subtract, ALU.mult).then_inc(norm.done, 1)

            def low_parts(t):
                for u in range(SLOTS):
                    dve.wait_ge(cut_hi, SLOTS * t + u + 1)
                    dve.tensor_tensor(cl[u][:], cin[u][:], ch[u][:].bitcast(F32), ALU.subtract).then_inc(cut, 1)

            def sum1(t):
                for u in range(SLOTS):
                    dve.wait_ge(proj_done, SLOTS * t + u + 1)
                    dve.wait_ge(xb_done, SLOTS * t + u + 1)
                    dve.tensor_tensor(res1[u][:], pa[u][:], xin[u][:], ALU.add).then_inc(n1.res, 1)

            def maxima(t):
                for u in range(SLOTS):
                    dve.wait_ge(cs_done, SLOTS * t + u + 1)
                    dve.tensor_reduce(nmax[u][:], pb[u][:, 0:LC], AX.X, ALU.max, negate=True).then_inc(nmax_done, 1)

            def inverses(t):
                for u in range(SLOTS):
                    dve.wait_ge(ex_done, SLOTS * t + u + 1)
                    dve.reciprocal(rsum[u][:], esum[u][:]).then_inc(rsum_done, 1)

            def sum2(t, b):
                for u in range(SLOTS):
                    dve.wait_ge(cv_done, SLOTS * t + u + 1)
                    dve.wait_ge(rsum_done, SLOTS * t + u + 1)
                    dve.wait_ge(stored[u], 16 * (t + 1))
                    dve.wait_ge(sorted_seen[u], t + 1 if b == 0 else TURNS + 1)
                    dve.scalar_tensor_tensor(out=row3[u][:], in0=pb[u][:], scalar=rsum[u][:, 0:1], in1=x2[u][:],
                                             op0=ALU.mult, op1=ALU.add).then_inc(n2.res, 1)

            def last_norm(t):
                for u in range(SLOTS):
                    dve.wait_ge(n2.done, SLOTS * (t + TURNS) + u + 1)
                    dve.tensor_tensor(row3[u][:], row3[u][:], fb[:], ALU.add).then_inc(n3.res, 1)
                statistics(n3, 2, row3, t, 0)
                apply(n3, 2, row3, row3, t)

            def front(t):
                low_parts(t)
                sum1(t)
                statistics(n1, 0, res1, t, SLOTS)
                apply(n1, 0, res1, x2, t)
                low_parts(t + 1)

            def both(t, b, more):
                maxima(t)
                inverses(t)
                sum1(t + 1)
                statistics(n1, 0, res1, t + 1, SLOTS)
                sum2(t, b)
                apply(n1, 0, res1, x2, t + 1)
                if more:
                    low_parts(t + 2)
                statistics(n2, 1, row3, t, SLOTS)
                apply(n2, 1, row3, row3, t)
                if b == 1:
                    last_norm(t - TURNS)

            def back(t, b):
                maxima(t)
                inverses(t)
                sum2(t, b)
                statistics(n2, 1, row3, t, SLOTS)
                apply(n2, 1, row3, row3, t)
                last_norm(t - TURNS)

            dve.wait_ge(bias_in, 32)
            turns(dve, front, both, back)

        @block.tensor
        def _(pe):
            def project(t, tiles):
                for u in tiles:
                    pe.wait_ge(cut, SLOTS * (t + 1) + u + 1)
                    pe.wait_ge(n1.res, SLOTS * t + u + 1)
                    terms = [((ch, cl)[x][u][:, k, :], m.woT[w][:, k, :])
                             for x, w in ((0, 0), (1, 0), (0, 1)) for k in range(KD)]
                    for n, (lhs, rhs) in enumerate(terms):
                        ins = pe.matmul(pa[u][:], lhs, rhs, start=(n == 0), stop=(n == len(terms) - 1))
                    ins.then_inc(proj_done, 1)

            def turn_x2(t):
                for u in range(SLOTS):
                    pe.wait_ge(n1.done, SLOTS * t + u + 1)
                    pe.wait_ge(n2.res, SLOTS * t + u + 1)
                    for k in range(KD):
                        ins = pe.transpose(pb[u][:, k * P:(k + 1) * P], x2[u][:, k * P:(k + 1) * P], m.ident[:])
                    ins.then_inc(x2_turned, 1)

            def cross_scores(t, b):
                for u in range(SLOTS):
                    pe.wait_ge(x2T_done, SLOTS * t + u + 1)
                    pe.matmul(pb[u][:, 0:LC], m.ones[0:1, :], m.g0[:, b, :], start=True, stop=False)
                    for k in range(KD):
                        ins = pe.matmul(pb[u][:, 0:LC], x2T[u][:, k, :], m.g[:, b, k, :], start=False,
                                        stop=(k == KD - 1))
                    ins.then_inc(cs_done, 1)

            def turn_exp(t):
                for u in range(SLOTS):
                    pe.wait_ge(ex_done, SLOTS * t + u + 1)
                    pe.transpose(pb[u][0:LC, P:2 * P], ex[u][:], m.ident[:]).then_inc(ex_turned, 1)

            def cross_values(t, b):
                for u in range(SLOTS):
                    pe.wait_ge(exT_done, SLOTS * t + u + 1)
                    pe.matmul(pb[u][:], exT[u][:], m.vx[:, b, :], start=True, stop=True).then_inc(cv_done, 1)

            def front(t):
                project(t, range(SLOTS))

            def both(t, b, more):
                turn_x2(t)
                project(t + 1, range(1))
                cross_scores(t, b)
                project(t + 1, range(1, SLOTS - 1))
                turn_exp(t)
                project(t + 1, range(SLOTS - 1, SLOTS))
                cross_values(t, b)

            def back(t, b):
                turn_x2(t)
                cross_scores(t, b)
                turn_exp(t)
                cross_values(t, b)

            turns(pe, front, both, back)


SPLIT = 3


def stage_experts(nc, d, m, out):
    with ExitStack() as c:
        def sb(name, shape, dt=F32):
            return c.enter_context(nc.sbuf_tensor(name, shape, dt))

        def sem(name):
            return c.enter_context(nc.semaphore(name))

        w1 = sb("ew1", [P, 2, KD, FF])
        w2h = sb("ew2h", [P, 2, 4 * SPLIT, D], F32R)
        w2l = sb("ew2l", [P, 2, FC, D], F32R)
        xg = [sb(f"exg{i}", [P, D]) for i in range(2)]
        xgT = [sb(f"exgT{i}", [P, KD, P]) for i in range(2)]
        hid = [sb(f"hid{i}", [P, 512]) for i in range(2)]
        hth = [sb(f"hth{i}", [P, 4, P], F32R) for i in range(2)]
        htl = [sb(f"htl{i}", [P, 4, P], F32R) for i in range(2)]
        htf = sb("htf", [P, 4, P])
        yt = [sb(f"yt{i}", [P, D]) for i in range(2)]
        ph = c.enter_context(nc.psum_tensor("ph", [P, FF], F32))
        pt = [c.enter_context(nc.psum_tensor(f"pte{i}", [P, 512], F32)) for i in range(2)]
        py = c.enter_context(nc.psum_tensor("py", [P, 512], F32))
        px = c.enter_context(nc.psum_tensor("px", [P, 512], F32))

        w1_in = sem("w1_in")
        w2_in = [sem(f"w2_in{j}") for j in range(4)]
        w2_hi = sem("w2_hi")
        w2_split = sem("w2_split")
        rows_in = [sem(f"rows_in{i}") for i in range(2)]
        x_turned = sem("ex_turned_x")
        xT_done = sem("exT_copied")
        h_done = [sem(f"h_done{j}") for j in range(4)]
        g_done = [sem(f"g_done{j}") for j in range(4)]
        ht_done = sem("ht_done")
        ht_hi = sem("ht_hi")
        ht_lo = sem("ht_lo")
        d_done = sem("d_done")
        y_done = sem("y_done")
        y_copied = sem("y_copied")
        y_out = [sem(f"y_out{i}") for i in range(2)]
        block = c.enter_context(nc.Block())
        LOOPS = (NTILE - 3) // 2
        w1v = d["L0_ffn_w1"].rearrange("e (k p) f -> e p k f", p=P)
        w2v = d["L0_ffn_w2"].rearrange("e (k p) n -> e p k n", p=P)
        xrow = m.xs_d.rearrange("(t p) c -> t p c", p=P)
        yrow = m.y_d.rearrange("(t p) c -> t p c", p=P)

        def tiles(eng, body):
            with eng.Fori(0, LOOPS) as i:
                for par in range(2):
                    body(2 * i + par, i, par)
            for t in range(2 * LOOPS, NTILE):
                body(t, t // 2, t % 2)

        def follows(t, n):
            return not isinstance(t, int) or t + n < NTILE

        @block.sync
        def _(sp):
            for e in range(NE):
                if e >= 2:
                    first = sp.value_load(m.efirst[0:1, e - 1:e], min_val=1, max_val=NTILE)
                    sp.wait_ge(y_done, first + 1)
                if e >= 1:
                    sp.wait_ge(w1_in, 16 * e)
                    for j in range(4):
                        sp.wait_ge(w2_in[j], 16 * e)
                else:
                    for i in range(2):
                        sp.wait_ge(rows_in[i], 16)
                sp.dma_start(w1[:, e % 2], w1v[e]).then_inc(w1_in, 16)
                for j in range(4):
                    sp.dma_start(w2l[:, e % 2, 4 * j:4 * j + 4].bitcast(F32), w2v[e][:, 4 * j:4 * j + 4])\
                        .then_inc(w2_in[j], 16)

        @block.gpsimd
        def _(pool):
            for e in range(NE):
                for j in range(SPLIT):
                    pool.wait_ge(w2_in[j], 16 * (e + 1))
                    hi, lo = w2h[:, e % 2, 4 * j:4 * j + 4], w2l[:, e % 2, 4 * j:4 * j + 4]
                    pool.tensor_copy(hi, lo.bitcast(F32)).then_inc(w2_hi, 1)
                    pool.wait_ge(w2_hi, SPLIT * e + j + 1)
                    pool.tensor_tensor(lo, lo.bitcast(F32), hi.bitcast(F32), ALU.subtract).then_inc(w2_split, 1)

        @block.scalar
        def _(act):
            for j in range(4):
                act.sem_inc(g_done[j], 1)
            for i in range(2):
                act.sem_inc(y_out[i], 16)

            def load_rows(t, par):
                act.wait_ge(x_turned, t + 1)
                act.dma_start(xg[par][:], xrow[t]).then_inc(rows_in[par], 16)

            for t in range(2):
                load_rows(t, t)

            def body(t, i, par):
                if follows(t, 2):
                    load_rows(t + 2, par)
                for j in range(4):
                    act.wait_ge(h_done[j], t + 1)
                    act.wait_ge(ht_done, 4 * t + j + 1)
                    act.activation(hid[j % 2][:], ph[:, j * 512:(j + 1) * 512], ACT.Gelu).then_inc(g_done[j], 1)
                act.wait_ge(y_copied, t + 2)
                act.dma_start(yrow[t], yt[par][:]).then_inc(y_out[par], 16)

            tiles(act, body)
            act.wait_ge(y_out[0], 16 * ((NTILE + 1) // 2 + 1))
            act.wait_ge(y_out[1], 16 * (NTILE // 2 + 1))

        @block.vector
        def _(dve):
            dve.sem_inc(ht_lo, 2)
            dve.sem_inc(y_copied, 1)

            def copy_x(t, par):
                dve.wait_ge(x_turned, t + 1 + 2)
                dve.tensor_copy(xgT[par][:], px[:].rearrange("p (k r) -> p k r", k=KD)).then_inc(xT_done, 1)

            copy_x(0, 0)

            def body(t, i, par):
                for j in range(4):
                    bank = pt[j % 2][:].rearrange("p (k r) -> p k r", k=4)
                    dve.wait_ge(ht_done, 4 * t + j + 1 + 2)
                    if j == 1 or j == 3:
                        dve.wait_ge(y_done, t + 1)
                    else:
                        dve.wait_ge(d_done, 3 * t + (3, None, 4)[j])
                    if j >= SPLIT:
                        dve.tensor_copy(htf[:], bank).then_inc(ht_lo, 1)
                        continue
                    dve.tensor_copy(hth[j % 2][:], bank).then_inc(ht_hi, 1)
                    dve.wait_ge(ht_hi, SPLIT * t + j + 1)
                    dve.tensor_tensor(htl[j % 2][:], bank, hth[j % 2][:].bitcast(F32), ALU.subtract).then_inc(ht_lo, 1)
                if follows(t, 1):
                    copy_x(t + 1, 1 - par)
                dve.wait_ge(y_done, t + 2)
                dve.wait_ge(y_out[par], 16 * (i + 1))
                dve.tensor_copy(yt[par][:], py[:]).then_inc(y_copied, 1)

            tiles(dve, body)

        @block.tensor
        def _(pe):
            pe.sem_inc(x_turned, 2)
            pe.sem_inc(ht_done, 2)
            pe.sem_inc(d_done, 3)
            pe.sem_inc(y_done, 1)

            def turn_x(t, i, par):
                pe.wait_ge(rows_in[par], 16 * (i + 1))
                if not isinstance(t, int) or t > 0:
                    pe.wait_ge(xT_done, t)
                for k in range(KD):
                    ins = pe.transpose(px[:, k * P:(k + 1) * P], xg[par][:, k * P:(k + 1) * P], m.ident[:])
                ins.then_inc(x_turned, 1)

            turn_x(0, 0, 0)

            def body(t, i, par):
                expert = pe.value_load(m.texp[0:1, bass.ds(t, 1)], min_val=0, max_val=NE - 1)
                slot = pe.value_load(m.tslot[0:1, bass.ds(t, 1)], min_val=0, max_val=1)

                def up(j):
                    pe.wait_ge(g_done[j], t + 1)
                    for k in range(KD):
                        ins = pe.matmul(ph[:, j * 512:(j + 1) * 512], xgT[par][:, k, :],
                                        w1[:, bass.ds(slot, 1), k, j * 512:(j + 1) * 512]
                                        .rearrange("p s f -> p (s f)"), start=(k == 0), stop=(k == KD - 1))
                    ins.then_inc(h_done[j], 1)

                def turn(j):
                    pe.wait_ge(g_done[j], t + 2)
                    pe.wait_ge(ht_lo, 4 * t + j + 1)
                    for k in range(4):
                        ins = pe.transpose(pt[j % 2][:, k * P:(k + 1) * P], hid[j % 2][:, k * P:(k + 1) * P], m.ident[:])
                    ins.then_inc(ht_done, 1)

                def down(j):
                    pe.wait_ge(ht_lo, 4 * t + j + 1 + 2)
                    if j < SPLIT:
                        pe.wait_ge(w2_split, SPLIT * expert + (j + 1))
                    else:
                        pe.wait_ge(w2_in[j], 16 * expert + 16)
                    if j == 0:
                        pe.wait_ge(y_copied, t + 1)
                    for k in range(4):
                        if j >= SPLIT:
                            ins = pe.matmul(py[:], htf[:, k, :],
                                            w2l[:, bass.ds(slot, 1), 4 * j + k, :].rearrange("p s n -> p (s n)")
                                            .bitcast(F32), start=False, stop=(k == 3))
                            continue
                        for n, (h, w) in enumerate(((hth, w2h), (htl, w2h), (hth, w2l))):
                            ins = pe.matmul(py[:], h[j % 2][:, k, :], w[:, bass.ds(slot, 1), 4 * j + k, :]
                                            .rearrange("p s n -> p (s n)"), start=(j == 0 and k == 0 and n == 0),
                                            stop=False)
                    ins.then_inc(y_done if j == 3 else d_done, 1)

                pe.wait_ge(w1_in, 16 * expert + 16)
                pe.wait_ge(xT_done, t + 1)
                up(0)
                up(1)
                turn(0)
                up(2)
                turn(1)
                down(0)
                up(3)
                turn(2)
                down(1)
                turn(3)
                if follows(t, 1):
                    turn_x(t + 1, i + par, 1 - par)
                down(2)
                down(3)

            tiles(pe, body)

    stage_combine(nc, d, m, out)


def stage_combine(nc, d, m, out):
    with ExitStack() as c:
        def sb(name, shape, dt=F32):
            return c.enter_context(nc.sbuf_tensor(name, shape, dt))

        def sem(name):
            return c.enter_context(nc.semaphore(name))

        N = NTOK // P
        fb = sb("fb_c", [P, D])
        half = sb("half_c", [P, 1])
        veps = [sb(f"cveps{i}", [P, 1]) for i in range(2)]
        x3 = sb("x3c", [P, N, D])
        yg = [[sb(f"yg{i}{j}", [P, D]) for j in range(TOPK)] for i in range(4)]
        s1 = [sb(f"s1_{i}", [P, D]) for i in range(2)]
        s2 = [sb(f"s2_{i}", [P, D]) for i in range(2)]
        xs = [sb(f"xs_{i}", [P, D]) for i in range(2)]
        stats = [sb(f"cst{i}", [P, 6]) for i in range(2)]
        mean = [sb(f"cmean{i}", [P, 2]) for i in range(2)]
        rstd = [sb(f"crstd{i}", [P, 1]) for i in range(2)]
        fin = [sb(f"cfin{i}", [P, D]) for i in range(2)]
        own_in = sem("own_in")
        y_in = [sem(f"y_in{i}") for i in range(4)]
        xs_done = sem("xs_done")
        sum_chain = sem("sum_chain")
        c_aggr = sem("c_aggr")
        c_veps = sem("c_veps")
        c_rstd = sem("c_rstd")
        fin_done = sem("fin_done")
        fin_out = [sem(f"fin_out{i}") for i in range(2)]
        block = c.enter_context(nc.Block())
        orow = out.rearrange("b (n p) c -> b n p c", p=P)

        @block.sync
        def _(sp):
            sp.dma_start(fb[:], bcast_rows(d["L0_ffn_bias"])).then_inc(own_in, 16)
            sp.dma_start(x3[:], m.x3_d.rearrange("(n p) c -> p n c", p=P)).then_inc(own_in, 16)
            for n in range(N):
                sp.wait_ge(fin_done, n + 1)
                sp.dma_start(orow[0, n], fin[n % 2][:]).then_inc(fin_out[n % 2], 16)
            for i in range(2):
                sp.wait_ge(fin_out[i], 16 * (N // 2))

        @block.gpsimd
        def _(pool):
            def gather(n):
                for j in range(TOPK):
                    pool.indirect_dma_start(yg[n % 4][j][:], None, m.y_d,
                                            bass.IndirectOffsetOnAxis(m.pos[:, TOPK * n + j:TOPK * n + j + 1], 0))\
                        .then_inc(y_in[n % 4], 16)

            pool.memset(half[:], -0.5).then_inc(c_veps, 1)
            for n in range(4):
                gather(n)
            for n in range(N):
                pool.wait_ge(c_aggr, n + 1)
                pool.tensor_scalar(veps[n % 2][:], mean[n % 2][:, 1:2], EPS, None, ALU.add).then_inc(c_veps, 1)
                pool.wait_ge(c_veps, n + 2)
                pool.tensor_tensor(rstd[n % 2][:], veps[n % 2][:], half[:], ALU.pow).then_inc(c_rstd, 1)
                if n + 4 < N:
                    gather(n + 4)

        @block.vector
        def _(dve):
            dve.wait_ge(own_in, 32)
            def sums(n):
                i = n % 2
                dve.tensor_tensor(xs[i][:], x3[:, n, :], fb[:], ALU.add).then_inc(xs_done, 1)
                dve.wait_ge(y_in[n % 4], 32 * (n // 4 + 1))
                dve.wait_ge(xs_done, n + 1)
                dve.scalar_tensor_tensor(out=s1[i][:], in0=yg[n % 4][0][:], scalar=m.tokw[:, TOPK * n:TOPK * n + 1],
                                         in1=xs[i][:], op0=ALU.mult, op1=ALU.add).then_inc(sum_chain, 1)
                dve.wait_ge(sum_chain, 3 * n + 1)
                if n >= 2:
                    dve.wait_ge(fin_done, n - 1)
                dve.scalar_tensor_tensor(out=s2[i][:], in0=yg[n % 4][1][:],
                                         scalar=m.tokw[:, TOPK * n + 1:TOPK * n + 2],
                                         in1=s1[i][:], op0=ALU.mult, op1=ALU.add).then_inc(sum_chain, 1)
                dve.wait_ge(sum_chain, 3 * n + 2)
                dve.bn_stats(stats[i][:], s2[i][:]).then_inc(sum_chain, 1)
                dve.wait_ge(sum_chain, 3 * n + 3)
                dve.bn_aggr(mean[i][:], stats[i][:]).then_inc(c_aggr, 1)

            def apply(n):
                i = n % 2
                dve.wait_ge(c_rstd, n + 1)
                if n >= 2:
                    dve.wait_ge(fin_out[i], 16 * (n // 2))
                dve.tensor_scalar(fin[i][:], s2[i][:], mean[i][:, 0:1], rstd[i][:, 0:1],
                                  ALU.subtract, ALU.mult).then_inc(fin_done, 1)

            for n in range(N):
                sums(n)
                if n >= 1:
                    apply(n - 1)
            apply(N - 1)



def build(nc, d, out):
    m = Mem()
    m.ext_t = nc.dram_tensor("ext_scr", [1, 512], F32)
    m.ext_d = m.ext_t.ap()
    m.xs_d = nc.dram_tensor("xs_scr", [NTILE * P, D], F32).ap()
    m.q_d = nc.dram_tensor("q_scr", [2, NG, D, GT], F32).ap()
    m.k_d = nc.dram_tensor("k_scr", [2, NG, D, GT], F32).ap()
    m.ctx_d = nc.dram_tensor("ctx_scr", [NH, P, KD * P], F32).ap()
    m.x3_d = nc.dram_tensor("x3_scr", [NTOK, D], F32).ap()
    m.y_d = nc.dram_tensor("y_scr", [NTILE * P, D], F32).ap()
    with ExitStack() as c:
        def sb(name, shape, dt=F32):
            return c.enter_context(nc.sbuf_tensor(name, shape, dt))

        m.ident, m.ones = sb("ident", [P, P]), sb("ones", [P, P])
        m.pos = sb("pos", [P, NCOL], I32)
        m.tokw = sb("tokw", [P, NCOL])
        m.texp, m.tslot, m.efirst = sb("texp", [1, NTILE], I32), sb("tslot", [1, NTILE], I32), sb("efirst", [1, NE], I32)
        with ExitStack() as ca:
            def sa(name, shape, dt=F32):
                return ca.enter_context(nc.sbuf_tensor(name, shape, dt))

            m.ident_r = sa("ident_r", [P, P], F32R)
            m.bq, m.bqs, m.bk = sa("bq", [P, KD]), sa("bqs", [P, KD]), sa("bk", [P, KD])
            m.c0 = sa("c0", [P, 1])
            m.dhi, m.dlo = sa("dhi", [P, 1], F32R), sa("dlo", [P, 1])
            m.t1 = sa("t1", [P, BAND])
            m.t2hi, m.t2lo = sa("t2hi", [P, BAND], F32R), sa("t2lo", [P, BAND], F32R)
            m.woT = [sa(f"woT{i}", [P, KD, D], F32R) for i in range(2)]
            m.g, m.g0, m.vx = sa("g", [P, B, KD, LC]), sa("g0", [1, B, LC]), sa("vx", [LC, B, D])
            with nc.sbuf_tensor("v", [P, NROW // P, D], F32) as m.v:
                with ExitStack() as cw:
                    m.bv = cw.enter_context(nc.sbuf_tensor("bv", [P, D], F32))

                    def parts(name):
                        return [cw.enter_context(nc.sbuf_tensor(f"{name}{i}", [P, KD, D], F32R)) for i in range(2)]

                    m.wqT, m.wkT, m.wvT = parts("wqT"), parts("wkT"), parts("wvT")
                    stage_setup(nc, d, m)
                    stage_project(nc, d, m)
                stage_attention(nc, d, m)
            stage_rows(nc, d, m, out)
        stage_experts(nc, d, m, out)


INPUTS = ["x", "ctx_1024", "L0_attn_Wq", "L0_attn_bq", "L0_attn_Wk", "L0_attn_bk", "L0_attn_Wv", "L0_attn_bv",
          "L0_attn_Wo", "L0_attn_bo", "L0_attn_et_gate", "L0_attn_is_gate", "L0_attn_time_bias", "L0_xattn_Wq",
          "L0_xattn_bq", "L0_xattn_Wk", "L0_xattn_bk", "L0_xattn_Wv", "L0_xattn_bv", "L0_ffn_expert_weights",
          "L0_ffn_expert_indices", "L0_ffn_w1", "L0_ffn_w2", "L0_ffn_bias"]


def kernel(**inputs):
    import numpy as _np
    import concourse.bacc as _bacc
    from concourse import mybir as _mybir
    from concourse.bass_utils import run_bass_kernel_spmd as _run

    nc = _bacc.Bacc("TRN2", target_bir_lowering=False, num_devices=1)
    arrays, d = {}, {}
    for name in INPUTS:
        a = _np.ascontiguousarray(inputs[name])
        arrays[f"in_{name}"] = a
        d[name] = nc.dram_tensor(f"in_{name}", a.shape, _mybir.dt.from_np(a.dtype), kind="ExternalInput").ap()
    out = nc.dram_tensor("out_rows", (B, T, D), F32, kind="ExternalOutput").ap()
    build(nc, d, out)
    r = _run(nc, [arrays], core_ids=[0])
    return r.results[0]["out_rows"]
```
